# Optimizing a Trainium2 kernel written in Bass

```python
import numpy as np
import jax
import jax.numpy as jnp

def _softmax(x, axis=-1):
    return jax.nn.softmax(x, axis=axis)

def _gelu(x):
    return jax.nn.gelu(x, approximate=True)

def _silu(x):
    return jax.nn.silu(x)

def _sigmoid(x):
    return jax.nn.sigmoid(x)

def _layernorm(x, axis=-1, eps=1e-05):
    m = jnp.mean(x, axis=axis, keepdims=True)
    v = jnp.var(x, axis=axis, keepdims=True)
    return (x - m) / jnp.sqrt(v + eps)

def _scatter_add(tgt, idx, src, axis=0):
    return tgt.at[idx].add(src)

def _segment_sum(src, seg, n):
    return jax.ops.segment_sum(src, seg, n)
kernel_name = 'mk_vit_tower_cls_d1_tok_img768_r4_cfebbf'

def setup_inputs(seed: int=0):
    np.random.seed(seed)
    _w = jnp.asarray

    def _rec_inputs():
        import jax
        import jax.numpy as jnp
        _rk = jax.random.key(seed)
        x = -0.000222058 + 0.999998 * jax.random.normal(jax.random.fold_in(_rk, 1), (64, 3, 96, 96), jnp.float32)
        cls_tok = 0.02 * jax.random.normal(jax.random.fold_in(_rk, 5), (1, 1, 192), jnp.float32)
        return (x, cls_tok)
    x, cls_tok = _rec_inputs()

    def _L0_tok_setup():
        import jax, jax.numpy as jnp
        import numpy as np
        KERNEL = 16
        C = 3
        H = 128
        B = 32
        IN_FEAT = C * KERNEL * KERNEL
        HIDDEN = 192
        key = jax.random.key(seed)
        k1, k2, k3 = jax.random.split(key, 3)
        x = jax.random.normal(k1, (B, C, H, H), dtype=jnp.float32)
        bound = float(np.sqrt(6.0 / IN_FEAT))
        W = jax.random.uniform(k2, (HIDDEN, IN_FEAT), dtype=jnp.float32, minval=-bound, maxval=bound)
        b = jnp.zeros((HIDDEN,), dtype=jnp.float32)
        return {'x': x, 'W': W, 'b': b}
    _L0_tok_all = _L0_tok_setup()
    _L0_tok_in = {k: v for k, v in _L0_tok_all.items() if k in ('W', 'b')}
    del _L0_tok_all

    def _L0_attn_setup():
        import jax, jax.numpy as jnp
        import numpy as np
        N_HEADS, D_MODEL, D_HEAD = (12, 192, 64)
        INIT_RANGE = 0.02
        IGNORE = -100000.0
        key = jax.random.key(seed)
        ks = jax.random.split(key, 5)
        x = jax.random.normal(ks[0], (4, 512, D_MODEL), dtype=jnp.float32)
        W_Q = jax.random.normal(ks[1], (N_HEADS, D_MODEL, D_HEAD), dtype=jnp.float32) * INIT_RANGE
        W_K = jax.random.normal(ks[2], (N_HEADS, D_MODEL, D_HEAD), dtype=jnp.float32) * INIT_RANGE
        W_V = jax.random.normal(ks[3], (N_HEADS, D_MODEL, D_HEAD), dtype=jnp.float32) * INIT_RANGE
        W_O = jax.random.normal(ks[4], (N_HEADS, D_HEAD, D_MODEL), dtype=jnp.float32) * INIT_RANGE
        b_Q = jnp.zeros((N_HEADS, D_HEAD), dtype=jnp.float32)
        b_K = jnp.zeros((N_HEADS, D_HEAD), dtype=jnp.float32)
        b_V = jnp.zeros((N_HEADS, D_HEAD), dtype=jnp.float32)
        b_O = jnp.zeros((D_MODEL,), dtype=jnp.float32)
        return {'normalized_resid_pre': x, 'W_Q': W_Q, 'b_Q': b_Q, 'W_K': W_K, 'b_K': b_K, 'W_V': W_V, 'b_V': b_V, 'W_O': W_O, 'b_O': b_O}
    _L0_attn_all = _L0_attn_setup()
    _L0_attn_in = {k: v for k, v in _L0_attn_all.items() if k in ('W_Q', 'b_Q', 'W_K', 'b_K', 'W_V', 'b_V', 'W_O', 'b_O')}
    del _L0_attn_all

    def _L0_ffn_setup():
        import jax, jax.numpy as jnp
        import numpy as np
        N_EMBD = 192
        N_EXPERTS = 8
        TOP_K = 2
        D_FF = 4 * N_EMBD
        key = jax.random.key(seed)
        ks = jax.random.split(key, 7)
        B, T, C, E, H = (4, 512, N_EMBD, N_EXPERTS, D_FF)
        s_gate = 1.0 / np.sqrt(C)
        s1 = 1.0 / np.sqrt(C)
        s2 = 1.0 / np.sqrt(H)
        return {'x': jax.random.normal(ks[0], (B, T, C), dtype=jnp.float32), 'gate_w': jax.random.uniform(ks[1], (C, E), jnp.float32, -s_gate, s_gate), 'gate_b': jax.random.uniform(ks[2], (E,), jnp.float32, -s_gate, s_gate), 'w1': jax.random.uniform(ks[3], (E, C, H), jnp.float32, -s1, s1), 'b1': jax.random.uniform(ks[4], (E, H), jnp.float32, -s1, s1), 'w2': jax.random.uniform(ks[5], (E, H, C), jnp.float32, -s2, s2), 'b2': jax.random.uniform(ks[6], (E, C), jnp.float32, -s2, s2)}
    _L0_ffn_all = _L0_ffn_setup()
    _L0_ffn_in = {k: v for k, v in _L0_ffn_all.items() if k in ('gate_w', 'gate_b', 'w1', 'b1', 'w2', 'b2')}
    del _L0_ffn_all
    return {'x': x, 'cls_tok': cls_tok, 'L0_tok_W': _L0_tok_in['W'], 'L0_tok_b': _L0_tok_in['b'], 'L0_attn_W_Q': _L0_attn_in['W_Q'], 'L0_attn_b_Q': _L0_attn_in['b_Q'], 'L0_attn_W_K': _L0_attn_in['W_K'], 'L0_attn_b_K': _L0_attn_in['b_K'], 'L0_attn_W_V': _L0_attn_in['W_V'], 'L0_attn_b_V': _L0_attn_in['b_V'], 'L0_attn_W_O': _L0_attn_in['W_O'], 'L0_attn_b_O': _L0_attn_in['b_O'], 'L0_ffn_gate_w': _L0_ffn_in['gate_w'], 'L0_ffn_gate_b': _L0_ffn_in['gate_b'], 'L0_ffn_w1': _L0_ffn_in['w1'], 'L0_ffn_b1': _L0_ffn_in['b1'], 'L0_ffn_w2': _L0_ffn_in['w2'], 'L0_ffn_b2': _L0_ffn_in['b2']}

def reference(x, cls_tok, L0_tok_W, L0_tok_b, L0_attn_W_Q, L0_attn_b_Q, L0_attn_W_K, L0_attn_b_K, L0_attn_W_V, L0_attn_b_V, L0_attn_W_O, L0_attn_b_O, L0_ffn_gate_w, L0_ffn_gate_b, L0_ffn_w1, L0_ffn_b1, L0_ffn_w2, L0_ffn_b2):
    import jax
    import jax.numpy as jnp

    def _L0_tok_ref(x, W, b):
        import jax, jax.numpy as jnp
        import numpy as np
        KERNEL = 16
        C = 3
        H = 128
        B = 32
        IN_FEAT = C * KERNEL * KERNEL
        HIDDEN = 192
        bsz, c, h, w = x.shape
        step = h // KERNEL
        p = x.reshape(bsz, c, step, KERNEL, step, KERNEL)
        p = p.transpose(0, 2, 4, 1, 3, 5)
        p = p.reshape(bsz, step * step, c * KERNEL * KERNEL)
        return jnp.einsum('blf,hf->blh', p, W) + b

    def _L0_attn_ref(normalized_resid_pre, W_Q, b_Q, W_K, b_K, W_V, b_V, W_O, b_O):
        import jax, jax.numpy as jnp
        import numpy as np
        N_HEADS, D_MODEL, D_HEAD = (12, 192, 64)
        INIT_RANGE = 0.02
        IGNORE = -100000.0
        x = normalized_resid_pre
        q = jnp.einsum('bsd,hde->bshe', x, W_Q) + b_Q
        k = jnp.einsum('bsd,hde->bshe', x, W_K) + b_K
        v = jnp.einsum('bsd,hde->bshe', x, W_V) + b_V
        scores = jnp.einsum('bqhe,bkhe->bhqk', q, k) / jnp.sqrt(jnp.float32(D_HEAD))
        S = x.shape[1]
        causal = jnp.triu(jnp.ones((S, S), dtype=bool), k=1)
        scores = jnp.where(causal, jnp.float32(IGNORE), scores)
        pattern = jax.nn.softmax(scores, axis=-1)
        z = jnp.einsum('bhqk,bkhe->bqhe', pattern, v)
        attn_out = jnp.einsum('bqhe,hed->bqd', z, W_O) + b_O
        return attn_out

    def _L0_ffn_ref(x, gate_w, gate_b, w1, b1, w2, b2):
        import jax, jax.numpy as jnp
        import numpy as np
        N_EMBD = 192
        N_EXPERTS = 8
        TOP_K = 2
        D_FF = 4 * N_EMBD
        B, T, C = x.shape
        x_flat = x.reshape(B * T, C)
        gate_logits = x_flat @ gate_w + gate_b
        gate_probs = jax.nn.softmax(gate_logits, axis=-1)
        topk_probs, topk_idx = jax.lax.top_k(gate_probs, TOP_K)
        topk_probs = topk_probs / jnp.sum(topk_probs, axis=-1, keepdims=True)
        h = jax.nn.gelu(jnp.einsum('nc,ech->neh', x_flat, w1) + b1[None], approximate=False)
        expert_out = jnp.einsum('neh,ehc->nec', h, w2) + b2[None]
        sel = jnp.take_along_axis(expert_out, topk_idx[:, :, None], axis=1)
        combined = jnp.sum(topk_probs[:, :, None] * sel, axis=1)
        return combined.reshape(B, T, C)
    h = _L0_tok_ref(x, L0_tok_W, L0_tok_b)
    h = jnp.concatenate([jnp.broadcast_to(cls_tok, (h.shape[0], 1, h.shape[2])), h], axis=1)
    h = h + _L0_attn_ref(_layernorm(h, axis=-1), L0_attn_W_Q, L0_attn_b_Q, L0_attn_W_K, L0_attn_b_K, L0_attn_W_V, L0_attn_b_V, L0_attn_W_O, L0_attn_b_O)
    h = h + _L0_ffn_ref(_layernorm(h, axis=-1), L0_ffn_gate_w, L0_ffn_gate_b, L0_ffn_w1, L0_ffn_b1, L0_ffn_w2, L0_ffn_b2)
    return h

_drawn_inputs = setup_inputs


def setup_inputs(seed=0):
    import zlib

    import numpy as np

    out = dict(_drawn_inputs(seed))
    spreads = {'L0_tok_b': (0.0, 0.1),
     'L0_attn_b_Q': (0.0, 0.8),
     'L0_attn_b_K': (0.0, 0.8),
     'L0_attn_b_V': (0.0, 0.1),
     'L0_attn_b_O': (0.0, 0.1)}
    factors = {'L0_attn_W_Q': 8.0, 'L0_attn_W_K': 8.0, 'L0_ffn_b1': 7.341, 'L0_ffn_b2': 5.221}
    for name, (base, spread) in spreads.items():
        noise = np.random.default_rng([zlib.crc32(name.encode()), seed]).standard_normal(out[name].shape)
        drawn = base * np.exp(spread * noise) if base else spread * noise
        out[name] = jnp.asarray(drawn.astype(out[name].dtype))
    for name, factor in factors.items():
        out[name] = (out[name] * factor).astype(out[name].dtype)
    return out
```

```python
import concourse.bass as bass
from concourse import mybir
from contextlib import ExitStack


def vit_tower_kernel(nc, x, cls_tok, tok_w, tok_b, w_q, b_q, w_k, b_k, w_v, b_v, w_o, b_o,
                     gate_w, gate_b, w1, b1, w2, b2, out):
    fp32, bf16 = mybir.dt.float32, mybir.dt.bfloat16
    i32, u32 = mybir.dt.int32, mybir.dt.uint32
    ALU = mybir.AluOpType
    ACT = mybir.ActivationFunctionType
    AX = mybir.AxisListType

    P = 128
    NI, C, IMG, _ = x.shape
    D, F_IN = tok_w.shape
    KER = 16
    STEP = IMG // KER
    T = STEP * STEP + 1
    H, _, DH = w_q.shape
    HD = H * DH
    E, _, F = w1.shape
    D1 = D - P
    KF = F_IN // P
    ROWS_A = P // NI
    GROUPS = STEP // ROWS_A
    TILES_A = GROUPS * STEP
    G3 = 3
    TT = G3 * T
    NT = -(-NI // G3)
    NIT = NT // 2
    NTOK = NI * T
    NPAD = NT * TT
    LAST = NTOK - (NT - 1) * TT
    HC = H // 2
    HB = 4
    NG = H // HB
    KH = F // P
    W2T = 2 * TT
    ROW = D + 2
    REGION = NTOK + P
    NTILE = (2 * NTOK - E) // P + E
    U = 4
    EPS = 1e-5
    CAUSAL = -1e5 * DH ** 0.5
    FAR = -1e30
    assert NTILE % U == 0 and NT % 2 == 0 and ROWS_A * NI == P

    resid = nc.dram_tensor("resid", [NI, T, D], fp32).ap()
    resid_rows = resid.rearrange("b t d -> (b t) d")
    acc = nc.dram_tensor("acc", [NTOK + P, D], fp32).ap()
    queue = nc.dram_tensor("queue", [(E + 1) * REGION, ROW], fp32).ap()

    ctx = ExitStack()
    with ctx:
        def sb(name, shape, dt=fp32):
            return ctx.enter_context(nc.sbuf_tensor(name, shape, dt))

        def sem(name):
            return ctx.enter_context(nc.semaphore(name))

        bank = [ctx.enter_context(nc.psum_tensor(f"bank{i}", [P, 512], fp32)) for i in range(8)]

        ident = sb("ident", [P, P])
        identb = sb("identb", [TT, TT], bf16)
        maskf = sb("maskf", [TT, HB * TT])
        mask = sb("mask", [TT, HB * TT], bf16)
        trif = sb("trif", [TT, TT])
        tri = sb("tri", [TT, TT], bf16)
        onesb = sb("onesb", [TT, P], bf16)
        mhalf = sb("mhalf", [P, 1])
        iota8 = sb("iota8", [P, E])
        idtab = sb("idtab", [P, NT])
        tokb = sb("tokb", [P, D])
        bo = sb("bo", [P, D])
        wtok = sb("wtok", [P, KF, D])
        wqk0, wqk1 = sb("wqk0", [P, 2, HD]), sb("wqk1", [D1 + 1, 2, HD])
        wv0, wv1 = sb("wv0", [P, HD]), sb("wv1", [D1 + 1, HD])
        wo = sb("wo", [P, HC, D])
        gw0, gw1 = sb("gw0", [P, E]), sb("gw1", [D1 + 1, E])
        w1a, w1b = sb("w1a", [P, E, F]), sb("w1b", [D1 + 1, E, F])
        xw2 = sb("xw2", [P, 2 * C * KER * IMG])
        xin = [xw2[:, g * C * KER * IMG:(g + 1) * C * KER * IMG] for g in range(2)]
        w2s = xw2[:, 0:E * KH * D].rearrange("p (e k d) -> p e k d", e=E, k=KH)
        b2s = sb("b2s", [P, E, D])
        xt0, xt1 = sb("xt0", [P, NPAD]), sb("xt1", [D1 + 1, NPAD])
        slot0 = sb("slot0", [P, E])

        ld_tokw, ld_small, ld_cls = sem("ld_tokw"), sem("ld_small"), sem("ld_cls")
        ld_w, ld_w1, ld_w2 = sem("ld_w"), sem("ld_w1"), sem("ld_w2")
        w_acc0 = sem("w_acc0")
        const_pool, const_dve = sem("const_pool"), sem("const_dve")

        N_W = 10

        with ExitStack() as ca:
            def sba(name, shape, dt=fp32):
                return ca.enter_context(nc.sbuf_tensor(name, shape, dt))

            def sema(name):
                return ca.enter_context(nc.semaphore(name))

            wraw0, wraw1 = sba("wraw0", [P, F_IN]), sba("wraw1", [D1, F_IN])
            pxt = [sba(f"pxt{i}", [P, KF, P]) for i in range(2)]
            xc = [sba(f"xc{i}", [P, F_IN]) for i in range(2)]
            hraw = [sba(f"hraw{i}", [P, D]) for i in range(2)]
            xn = [sba(f"xn{i}", [P, D]) for i in range(2)]
            hbo = [sba(f"hbo{i}", [P, STEP, D]) for i in range(2)]
            st = [sba(f"st{i}", [P, 6]) for i in range(3)]
            mv = [sba(f"mv{i}", [P, 2]) for i in range(3)]
            ve = [sba(f"ve{i}", [P, 1]) for i in range(3)]
            rs = [sba(f"rs{i}", [P, 1]) for i in range(3)]
            clsr = sba("clsr", [NI, D])
            clsn = sba("clsn", [NI, D])
            clsbo = sba("clsbo", [NI, D])
            iotai = sba("iotai", [P, E], i32)
            idtabi = sba("idtabi", [P, NT], i32)
            zrow = sba("zrow", [P, D])

            x_in = [sema(f"x_in{i}") for i in range(2)]
            xc_done = sema("xc_done")
            wt_full, wt_out = sema("wt_full"), sema("wt_out")
            tr_done, emb_done, lt_done = sema("tr_done"), sema("emb_done"), sema("lt_done")
            px_act, px_dve = sema("px_act"), sema("px_dve")
            h_done, mv_done, rs_done, xn_done = sema("h_done"), sema("mv_done"), sema("rs_done"), sema("xn_done")
            xt_out, hbo_done, dve_link, pool_link = sema("xt_out"), sema("hbo_done"), sema("dve_link_a"), sema("pool_link_a")
            resid_w = [sema(f"resid_w{i}") for i in range(2)]
            cls_w, cls_mv, cls_rs, cls_xn, cls_full, cls_bo = (sema("cls_w"), sema("cls_mv"), sema("cls_rs"),
                                                               sema("cls_xn"), sema("cls_full"), sema("cls_bo"))

            block = ca.enter_context(nc.Block())

            @block.sync
            def _(sp):
                def load_images(g):
                    for r in range(ROWS_A):
                        row0 = (g * ROWS_A + r) * KER
                        sp.dma_start(xin[g % 2][r * NI:(r + 1) * NI, :].rearrange("b (c n) -> b c n", c=C),
                                     x[:, :, row0:row0 + KER, :].rearrange("b c i w -> b c (i w)")
                                     ).then_inc(x_in[g % 2], 16)

                sp.dma_start(wraw0[:, :], tok_w[0:P, :]).then_inc(ld_tokw, 16)
                sp.dma_start(wraw1[:, :], tok_w[P:D, :]).then_inc(ld_tokw, 16)
                load_images(0)
                sp.dma_start(clsr[:, :], cls_tok.rearrange("a b d -> (a b) d").partition_broadcast(NI)).then_inc(ld_cls, 16)
                sp.dma_start(tokb[:, :], tok_b.rearrange("(a d) -> a d", a=1).partition_broadcast(P)).then_inc(ld_small, 16)
                sp.dma_start(bo[:, :], b_o.rearrange("(a d) -> a d", a=1).partition_broadcast(P)).then_inc(ld_small, 16)
                load_images(1)
                sp.wait_ge(xc_done, STEP)
                load_images(2)
                for g in range(GROUPS):
                    sp.wait_ge(hbo_done, STEP * (g + 1))
                    for r in range(ROWS_A):
                        t0 = 1 + (g * ROWS_A + r) * STEP
                        sp.dma_start(resid[:, t0:t0 + STEP, :].rearrange("b t d -> b (t d)"),
                                     hbo[g % 2][r * NI:(r + 1) * NI, :, :].rearrange("b t d -> b (t d)")
                                     ).then_inc(resid_w[g % 2], 16)
                sp.wait_ge(cls_bo, 1)
                sp.dma_start(resid[:, 0, :], clsbo[:, :]).then_inc(cls_w, 16)
                sp.wait_ge(xc_done, TILES_A)
                sp.dma_start(w2s, w2.rearrange("e (k p) d -> p e k d", p=P)).then_inc(ld_w2, 16)
                sp.wait_ge(cls_w, 16)
                sp.wait_ge(resid_w[0], 64)
                sp.wait_ge(resid_w[1], 32)

            @block.scalar
            def _(act):
                for n, (w, b) in enumerate([(w_q, b_q), (w_k, b_k)]):
                    act.dma_start(wqk0[:, n, :].rearrange("c (h e) -> c h e", h=H),
                                  w[:, 0:P, :].rearrange("h c e -> c h e")).then_inc(ld_w, 16)
                    act.dma_start(wqk1[0:D1, n, :].rearrange("c (h e) -> c h e", h=H),
                                  w[:, P:D, :].rearrange("h c e -> c h e")).then_inc(ld_w, 16)
                    act.dma_start(wqk1[D1:D1 + 1, n, :], b.rearrange("(a h) e -> a (h e)", a=1)).then_inc(ld_w, 16)
                act.dma_start(wv0[:, :].rearrange("c (h e) -> c h e", h=H),
                              w_v[:, 0:P, :].rearrange("h c e -> c h e")).then_inc(ld_w, 16)
                act.dma_start(wv1[0:D1, :].rearrange("c (h e) -> c h e", h=H),
                              w_v[:, P:D, :].rearrange("h c e -> c h e")).then_inc(ld_w, 16)
                act.dma_start(wv1[D1:D1 + 1, :], b_v.rearrange("(a h) e -> a (h e)", a=1)).then_inc(ld_w, 16)
                act.dma_start(wo[:, :, :], w_o.rearrange("(c a) e d -> (a e) c d", a=2)).then_inc(ld_w, 16)
                act.dma_start(gw0[:, :], gate_w[0:P, :]).then_inc(ld_small, 16)
                act.dma_start(gw1[0:D1, :], gate_w[P:D, :]).then_inc(ld_small, 16)
                act.dma_start(gw1[D1:D1 + 1, :], gate_b.rearrange("(a e) -> a e", a=1)).then_inc(ld_small, 16)
                act.dma_start(b2s[:, :, :].rearrange("p e d -> p (e d)"),
                              b2.rearrange("(a e) d -> a (e d)", a=1).partition_broadcast(P)).then_inc(ld_small, 16)
                act.wait_ge(const_pool, 2)
                act.dma_start(acc[NTOK:NTOK + P, :], zrow[:, :]).then_inc(w_acc0, 16)
                for k in range(KF):
                    act.wait_ge(wt_full, k + 1)
                    nc.scalar.copy(wtok[:, k, :], bank[k][:, 0:D]).then_inc(wt_out, 1)
                act.wait_ge(cls_full, 1)
                act.wait_ge(const_pool, 5)
                nc.scalar.copy(xt0[:, 0:NTOK].rearrange("c (b t) -> c b t", t=T)[:, :, 0], bank[6][:, 0:NI])
                nc.scalar.copy(xt1[0:D1, 0:NTOK].rearrange("c (b t) -> c b t", t=T)[:, :, 0],
                               bank[6][0:D1, P:P + NI]).then_inc(xt_out, 1)
                for s in range(TILES_A + 3):
                    if s < TILES_A:
                        act.wait_ge(tr_done, s + 1)
                        if s >= 2:
                            act.wait_ge(emb_done, s - 1)
                        nc.scalar.copy(pxt[s % 2][:, 0:4, :], bank[2 * (s % 2)][:, :]).then_inc(px_act, 1)
                    n = s - 3
                    if n >= 0:
                        g, pj = divmod(n, STEP)
                        act.wait_ge(lt_done, n + 1)
                        for xt, rows, off in ((xt0, P, 0), (xt1, D1, P)):
                            dst = xt[0:rows, 0:NTOK].rearrange("c (b t) -> c b t", t=T)
                            t0 = 1 + g * ROWS_A * STEP + pj
                            dst = dst[:, :, t0:t0 + STEP + 1:STEP].rearrange("c b r -> c r b")
                            last = nc.scalar.copy(dst, bank[6 + n % 2][0:rows, off:off + P].rearrange("c (r b) -> c r b", r=ROWS_A))
                        last.then_inc(xt_out, 1)
                act.wait_ge(w_acc0, 16)

            @block.gpsimd
            def _(pool):
                pool.memset(ident[:, :], 0.0).then_inc(pool_link, 1)
                pool.wait_ge(pool_link, 1)
                pool.affine_select(out=ident[:, :], in_=ident[:, :], compare_op=ALU.not_equal, fill=1.0,
                                   base=0, pattern=[[-1, P]], channel_multiplier=1).then_inc(const_pool, 1)
                pool.memset(mhalf[:, :], -0.5)
                pool.memset(zrow[:, :], 0.0).then_inc(const_pool, 1)
                pool.memset(xt0[:, NTOK:NPAD], 0.0).then_inc(const_pool, 1)
                pool.memset(xt1[0:D1, NTOK:NPAD], 0.0).then_inc(const_pool, 1)
                pool.wait_ge(const_pool, 4)
                pool.memset(xt1[D1:D1 + 1, :], 1.0).then_inc(const_pool, 1)
                pool.wait_ge(const_pool, 5)
                pool.memset(maskf[:, :], 0.0).then_inc(pool_link, 1)
                pool.memset(trif[:, :], 1.0).then_inc(pool_link, 1)
                pool.wait_ge(pool_link, 3)
                m4 = maskf[:, :].rearrange("q (h k) -> q h k", h=HB)
                m5 = maskf[:, :].rearrange("q (h b k) -> q h b k", h=HB, b=G3)
                pool.affine_select(out=m4, in_=m4, compare_op=ALU.is_ge, fill=CAUSAL, base=0,
                                   pattern=[[0, HB], [-1, TT]], channel_multiplier=1).then_inc(pool_link, 1)
                pool.wait_ge(pool_link, 4)
                pool.affine_select(out=m5, in_=m5, compare_op=ALU.is_ge, fill=FAR, base=T - 1,
                                   pattern=[[0, HB], [T, G3], [0, T]], channel_multiplier=-1).then_inc(pool_link, 1)
                pool.wait_ge(pool_link, 5)
                pool.affine_select(out=m5, in_=m5, compare_op=ALU.is_ge, fill=FAR, base=0,
                                   pattern=[[0, HB], [-T, G3], [0, T]], channel_multiplier=1).then_inc(pool_link, 1)
                pool.affine_select(out=trif[:, :], in_=trif[:, :], compare_op=ALU.is_ge, fill=0.0, base=-1,
                                   pattern=[[1, TT]], channel_multiplier=-1).then_inc(pool_link, 1)
                pool.iota(iotai[:, :], pattern=[[1, E]], base=0, channel_multiplier=0).then_inc(pool_link, 1)
                pool.iota(idtabi[:, :], pattern=[[TT, NT]], base=0, channel_multiplier=1).then_inc(pool_link, 1)
                pool.wait_ge(pool_link, 9)
                pool.memset(onesb[:, :], 1.0).then_inc(const_pool, 1)
                pool.wait_ge(cls_mv, 1)
                pool.tensor_scalar(ve[2][0:NI, :], mv[2][0:NI, 1:2], EPS, None, ALU.add).then_inc(pool_link, 1)
                pool.wait_ge(pool_link, 10)
                pool.tensor_tensor(rs[2][0:NI, :], ve[2][0:NI, :], mhalf[0:NI, :], ALU.pow).then_inc(cls_rs, 1)
                pool.wait_ge(ld_small, 16 * 6)
                pool.tensor_tensor(clsbo[:, :], clsr[:, :], bo[0:NI, :], ALU.add).then_inc(cls_bo, 1)
                for s in range(TILES_A + 2):
                    if s < TILES_A:
                        g, pj = divmod(s, STEP)
                        if pj == 0:
                            pool.wait_ge(x_in[g % 2], 32 * (g // 2 + 1))
                        if s >= 2:
                            pool.wait_ge(tr_done, s - 1)
                        pool.tensor_copy(xc[s % 2][:, :].rearrange("p (m k) -> p m k", k=KER),
                                         xin[g % 2].rearrange("p (m j k) -> p m j k", j=STEP, k=KER)[:, :, pj, :]
                                         ).then_inc(xc_done, 1)
                    n = s - 2
                    if n < 0:
                        continue
                    g, pj = divmod(n, STEP)
                    pool.wait_ge(mv_done, n + 1)
                    pool.tensor_scalar(ve[n % 2][:, :], mv[n % 2][:, 1:2], EPS, None, ALU.add).then_inc(pool_link, 1)
                    pool.wait_ge(pool_link, 11 + n)
                    pool.tensor_tensor(rs[n % 2][:, :], ve[n % 2][:, :], mhalf[:, :], ALU.pow).then_inc(rs_done, 1)
                    if n == 2 * STEP:
                        pool.wait_ge(resid_w[0], 32)
                    pool.tensor_tensor(hbo[g % 2][:, pj, :], hraw[n % 2][:, :], bo[:, :], ALU.add).then_inc(hbo_done, 1)

            @block.vector
            def _(dve):
                links = [0]

                def link(ins):
                    links[0] += 1
                    ins.then_inc(dve_link, 1)
                    dve.wait_ge(dve_link, links[0])

                dve.wait_ge(ld_cls, 16)
                link(nc.vector.bn_stats(st[2][0:NI, :], clsr[:, :]))
                nc.vector.bn_aggr(mv[2][0:NI, :], st[2][0:NI, :]).then_inc(cls_mv, 1)
                dve.wait_ge(const_pool, 6)
                nc.vector.tensor_copy(mask[:, :], maskf[:, :])
                nc.vector.tensor_copy(tri[:, :], trif[:, :])
                nc.vector.tensor_copy(identb[:, :], ident[0:TT, 0:TT])
                nc.vector.tensor_copy(idtab[:, :], idtabi[:, :])
                link(nc.vector.tensor_copy(iota8[:, :], iotai[:, :]))
                nc.vector.tensor_scalar(slot0[:, :], iota8[:, :], float(REGION), None, ALU.mult).then_inc(const_dve, 1)
                dve.wait_ge(cls_rs, 1)
                dve.wait_ge(cls_mv, 1)
                nc.vector.tensor_scalar(clsn[:, :], clsr[:, :], mv[2][0:NI, 0:1], rs[2][0:NI, 0:1],
                                        ALU.subtract, ALU.mult).then_inc(cls_xn, 1)
                dve.wait_ge(ld_small, 16 * 6)
                for s in range(TILES_A + 2):
                    if s < TILES_A:
                        dve.wait_ge(tr_done, s + 1)
                        if s >= 2:
                            dve.wait_ge(emb_done, s - 1)
                        nc.vector.tensor_copy(pxt[s % 2][:, 4:KF, :], bank[2 * (s % 2) + 1][:, 0:(KF - 4) * P]).then_inc(px_dve, 1)
                    n = s - 2
                    if n >= 0:
                        dve.wait_ge(rs_done, n + 1)
                        if n >= 2:
                            dve.wait_ge(lt_done, n - 1)
                        nc.vector.tensor_scalar(xn[n % 2][:, :], hraw[n % 2][:, :], mv[n % 2][:, 0:1], rs[n % 2][:, 0:1],
                                                ALU.subtract, ALU.mult).then_inc(xn_done, 1)
                    n = s - 1
                    if 0 <= n < TILES_A:
                        dve.wait_ge(emb_done, n + 1)
                        if n >= 2:
                            dve.wait_ge(hbo_done, n - 1)
                            dve.wait_ge(xn_done, n - 1)
                        nc.vector.tensor_tensor(hraw[n % 2][:, :], bank[4 + n % 2][:, 0:D], tokb[:, :], ALU.add).then_inc(h_done, 1)
                        dve.wait_ge(h_done, n + 1)
                        link(nc.vector.bn_stats(st[n % 2][:, :], hraw[n % 2][:, :]))
                        nc.vector.bn_aggr(mv[n % 2][:, :], st[n % 2][:, :]).then_inc(mv_done, 1)

            @block.tensor
            def _(pe):
                pe.wait_ge(const_pool, 1)
                pe.wait_ge(ld_tokw, 32)
                for k in range(KF):
                    nc.tensor.transpose(bank[k][:, 0:P], wraw0[:, k * P:(k + 1) * P], ident[:, :])
                    nc.tensor.transpose(bank[k][:, P:D], wraw1[:, k * P:(k + 1) * P], ident[0:D1, 0:D1]).then_inc(wt_full, 1)
                pe.wait_ge(cls_xn, 1)
                nc.tensor.transpose(bank[6][:, 0:NI], clsn[:, 0:P], ident[0:NI, 0:NI])
                nc.tensor.transpose(bank[6][0:D1, P:P + NI], clsn[:, P:D], ident[0:NI, 0:NI]).then_inc(cls_full, 1)
                pe.wait_ge(wt_out, KF)
                pe.wait_ge(xt_out, 1)
                for s in range(TILES_A + 3):
                    if s < TILES_A:
                        pe.wait_ge(xc_done, s + 1)
                        if s >= 2:
                            pe.wait_ge(px_act, s - 1)
                            pe.wait_ge(px_dve, s - 1)
                        for k in range(KF):
                            last = nc.tensor.transpose(bank[2 * (s % 2) + k // 4][:, (k % 4) * P:(k % 4 + 1) * P],
                                                       xc[s % 2][:, k * P:(k + 1) * P], ident[:, :])
                        last.then_inc(tr_done, 1)
                    n = s - 1
                    if 0 <= n < TILES_A:
                        pe.wait_ge(px_act, n + 1)
                        pe.wait_ge(px_dve, n + 1)
                        if n >= 2:
                            pe.wait_ge(h_done, n - 1)
                        for k in range(KF):
                            last = nc.tensor.matmul(bank[4 + n % 2][:, 0:D], pxt[n % 2][:, k, :], wtok[:, k, :],
                                                    start=(k == 0), stop=(k == KF - 1))
                        last.then_inc(emb_done, 1)
                    n = s - 3
                    if n >= 0:
                        pe.wait_ge(xn_done, n + 1)
                        if n >= 2:
                            pe.wait_ge(xt_out, n)
                        nc.tensor.transpose(bank[6 + n % 2][:, 0:P], xn[n % 2][:, 0:P], ident[:, :])
                        nc.tensor.transpose(bank[6 + n % 2][0:D1, P:2 * P], xn[n % 2][:, P:D], ident[:, :]).then_inc(lt_done, 1)

        PROJ_JOBS, ROT_JOBS = 5, 8
        ATT_JOBS = 6
        with ExitStack() as cb:
            def sbb(name, shape, dt=fp32):
                return cb.enter_context(nc.sbuf_tensor(name, shape, dt))

            def semb(name):
                return cb.enter_context(nc.semaphore(name))

            xs0, xs1 = sbb("xs0", [P, W2T]), sbb("xs1", [D1 + 1, W2T])
            qk = sbb("qk", [P, HC, 2, W2T])
            vs = [sbb(f"vs{j}", [TT, H, DH + 1]) for j in range(2)]
            pr = [sbb(f"pr{j}", [TT, H, TT]) for j in range(2)]
            mx = [sbb(f"mx{j}", [TT, H]) for j in range(2)]
            pt = [sbb(f"pt{g}", [TT, HB, TT]) for g in range(NG)]
            z = [sbb(f"z{j}", [TT, H, DH]) for j in range(2)]
            rinv = [sbb(f"rinv{j}", [TT, H]) for j in range(2)]
            zt = [sbb(f"zt{j}", [P, HC, TT]) for j in range(2)]
            hb = [sbb(f"hb{j}", [TT, D]) for j in range(2)]
            h2 = [sbb(f"h2{j}", [TT, D]) for j in range(2)]
            stb = [sbb(f"stb{j}", [TT, 6]) for j in range(2)]
            mvb = [sbb(f"mvb{j}", [TT, 2]) for j in range(2)]
            veb = [sbb(f"veb{j}", [TT, 1]) for j in range(2)]
            rsb = [sbb(f"rsb{j}", [TT, 1]) for j in range(2)]
            xr = [[sbb(f"xr{j}{k}", [TT, ROW]) for k in range(2)] for j in range(2)]
            x2t0 = [sbb(f"x2t0{j}", [P, TT]) for j in range(2)]
            x2t1 = [sbb(f"x2t1{j}", [D1 + 1, TT]) for j in range(2)]
            lg = [sbb(f"lg{j}", [TT, E]) for j in range(2)]
            mx8 = [sbb(f"mx8{j}", [TT, 8]) for j in range(2)]
            ix8 = [sbb(f"ix8{j}", [TT, 8], u32) for j in range(2)]
            ixf = [sbb(f"ixf{j}", [TT, 2]) for j in range(2)]
            msk = [sbb(f"msk{j}", [TT, 2, E]) for j in range(2)]
            mskb = [sbb(f"mskb{j}", [TT, E], bf16) for j in range(2)]
            dl = [sbb(f"dl{j}", [TT, 1]) for j in range(2)]
            el = [sbb(f"el{j}", [TT, 2]) for j in range(2)]
            s8 = [sbb(f"s8{j}", [TT, 3, E]) for j in range(2)]
            slf = [sbb(f"slf{j}", [TT, 2]) for j in range(2)]
            sli = [sbb(f"sli{j}", [TT, 2], u32) for j in range(2)]

            full = [semb(f"full{b}") for b in range(8)]
            free = [semb(f"free{b}") for b in range(8)]
            xs_ready, ones_done, row1_done = semb("xs_ready"), semb("ones_done"), semb("row1_done")
            even_done, scored, sub_done, exp_done = semb("even_done"), semb("scored"), semb("sub_done"), semb("exp_done")
            h2_done, mvb_done, rsb_done, xnb_done = semb("h2_done"), semb("mvb_done"), semb("rsb_done"), semb("xnb_done")
            mask_done, dl_done, el_done = semb("mask_done"), semb("dl_done"), semb("el_done")
            slot_done, row_done = semb("slot_done"), semb("row_done")
            scat = [semb(f"scat{j}") for j in range(2)]
            xr_free = [semb(f"xr_free{j}") for j in range(2)]
            settled = {e.engine: semb(f"settled{n}") for n, e in enumerate((nc.vector, nc.gpsimd))}
            hb_in = [semb(f"hb_in{j}") for j in range(2)]
            acc_w = [semb(f"acc_w{j}") for j in range(2)]
            att_link, tail_link, pool_linkb = semb("att_link"), semb("tail_link"), semb("pool_link_b")

            def settle(engine):
                engine.sem_inc(settled[engine.engine], 1)

            def head_of(g, n):
                return 2 * n + g if g < 2 else 2 * HB + n

            def heads(t, g):
                return t[:, g:2 * HB:2, :] if g < 2 else t[:, 2 * HB:H, :]

            def turn(i, jobs, k):
                return i * jobs + k

            block = cb.enter_context(nc.Block())

            @block.sync
            def _(sp):
                def load_hb(i, j, rows=TT):
                    sp.wait_ge(h2_done, i * 2 + (j + 1))
                    sp.dma_start(hb[j][0:rows, :], resid_rows[bass.ds(i * W2T + j * TT, rows), :]).then_inc(hb_in[j], 16)

                def store_h2(i, j, rows=TT):
                    sp.wait_ge(h2_done, i * 2 + (j + 3))
                    sp.dma_start(acc[bass.ds(i * W2T + j * TT, rows), :], h2[j][0:rows, :]).then_inc(acc_w[j], 16)

                for j in range(2):
                    sp.sem_inc(acc_w[j], 1)
                for j in range(2):
                    load_hb(0, j)
                sp.dma_start(w1a[:, :, :], w1[:, 0:P, :].rearrange("e c f -> c e f")).then_inc(ld_w1, 16)
                sp.dma_start(w1b[0:D1, :, :], w1[:, P:D, :].rearrange("e c f -> c e f")).then_inc(ld_w1, 16)
                sp.dma_start(w1b[D1:D1 + 1, :, :].rearrange("a e f -> a (e f)"),
                             b1.rearrange("(a e) f -> a (e f)", a=1)).then_inc(ld_w1, 16)
                with sp.Fori(0, NIT - 2) as i:
                    for j in range(2):
                        store_h2(i, j)
                        load_hb(i + 1, j)
                store_h2(NIT - 2, 0)
                load_hb(NIT - 1, 0)
                store_h2(NIT - 2, 1)
                load_hb(NIT - 1, 1, LAST)
                store_h2(NIT - 1, 0)
                store_h2(NIT - 1, 1, LAST)
                for j in range(2):
                    sp.wait_ge(acc_w[j], 16 * NIT + 1)

            @block.gpsimd
            def _(pool):
                def copy_tokens(i):
                    nc.gpsimd.tensor_copy(xs0[:, :], xt0[:, bass.ds(i * W2T, W2T)])
                    nc.gpsimd.tensor_copy(xs1[:, :], xt1[:, bass.ds(i * W2T, W2T)]).then_inc(xs_ready, 1)

                def rstd(i, j):
                    pool.wait_ge(mvb_done, i * 2 + (j + 1))
                    settle(pool)
                    nc.gpsimd.tensor_scalar(veb[j][:, :], mvb[j][:, 1:2], EPS, None, ALU.add).then_inc(pool_linkb, 1)
                    pool.wait_ge(pool_linkb, i * 2 + (j + 1))
                    nc.gpsimd.tensor_tensor(rsb[j][:, :], veb[j][:, :], mhalf[0:TT, :], ALU.pow).then_inc(rsb_done, 1)

                def attention(i, more=True):
                    if more:
                        pool.wait_ge(full[1], turn(i, PROJ_JOBS, PROJ_JOBS))
                        settle(pool)
                        copy_tokens(i + 1)
                    for j in range(2):
                        rstd(i, j)

                def tail(i, rows=(TT, TT)):
                    for j in range(2):
                        pool.wait_ge(xnb_done, i * 2 + (j + 1))
                        settle(pool)
                        nc.gpsimd.tensor_copy(xr[j][1][:, 0:D], xr[j][0][:, 0:D])
                        for k in range(2):
                            last = nc.gpsimd.tensor_copy(xr[j][k][:, D + 1:D + 2], idtab[0:TT, bass.ds(i * 2 + j, 1)])
                        last.then_inc(row_done, 1)
                    for j in range(2):
                        pool.wait_ge(row_done, i * 2 + (j + 1))
                        pool.wait_ge(slot_done, i * 2 + (j + 1))
                        settle(pool)
                        for k in range(2):
                            nc.gpsimd.indirect_dma_start(
                                out=queue[:, :], out_offset=bass.IndirectOffsetOnAxis(sli[j][0:rows[j], k:k + 1], 0),
                                in_=xr[j][k][0:rows[j], :], in_offset=None,
                                bounds_check=(E + 1) * REGION - 1, oob_is_err=True).then_inc(scat[j], 16)
                    for j in range(2):
                        pool.wait_ge(scat[j], i * 32 + 32)
                        pool.sem_inc(xr_free[j], 1)

                for j in range(2):
                    pool.memset(vs[j][:, :, :], 1.0).then_inc(ones_done, 1)
                    pool.sem_inc(xr_free[j], 1)
                copy_tokens(0)
                attention(0)
                with pool.Fori(1, NIT - 1) as i:
                    tail(i - 1)
                    attention(i)
                tail(NIT - 2)
                attention(NIT - 1, more=False)
                tail(NIT - 1, (TT, LAST))

            @block.scalar
            def _(act):
                def drain(i, b, jobs, k, dst, src):
                    act.wait_ge(full[b], turn(i, jobs, k))
                    nc.scalar.copy(dst, src).then_inc(free[b], 1)

                def qk_even(i, n):
                    drain(i, 0, PROJ_JOBS, n + 1, qk[:, 2 * n, :, :].rearrange("p a t -> p (a t)"), bank[0][:, 0:2 * W2T])

                def v_half(i, j):
                    drain(i, 0, PROJ_JOBS, 4 + j, vs[j][:, 0:H // 2, 0:DH],
                          bank[0][0:TT, 0:HD // 2].rearrange("p (h e) -> p h e", e=DH))

                def probs(i, j):
                    act.wait_ge(sub_done, i * 2 + (j + 2))
                    nc.scalar.activation(pr[j][:, :, :], pr[j][:, :, :], ACT.Exp, scale=DH ** -0.5).then_inc(exp_done, 1)

                def pt_out(i, b, k, g):
                    drain(i, b, ROT_JOBS, k, pt[g][:, :, :].rearrange("p h k -> p (h k)"), bank[b][0:TT, 0:HB * TT])

                def zt_out(i, b, k, j, c0, n):
                    drain(i, b, ROT_JOBS, k, zt[j][:, c0:c0 + n, :].rearrange("p c t -> p (c t)"), bank[b][:, 0:n * TT])

                def attention(i):
                    v_half(i, 0)
                    v_half(i, 1)
                    probs(i, 0)
                    pt_out(i, 5, 1, 0)
                    pt_out(i, 5, 2, 2)
                    probs(i, 1)
                    pt_out(i, 5, 3, 0)
                    zt_out(i, 7, 3, 0, 0, 4)
                    pt_out(i, 5, 4, 2)
                    zt_out(i, 6, 4, 0, 4, 2)
                    zt_out(i, 5, 6, 1, 0, 4)
                    zt_out(i, 6, 6, 1, 4, 2)

                def x2_out(i, b, j):
                    act.wait_ge(full[b], turn(i, ROT_JOBS, 7))
                    nc.scalar.copy(x2t0[j][:, :], bank[b][:, 0:TT])
                    nc.scalar.copy(x2t1[j][0:D1, :], bank[b][0:D1, TT:2 * TT]).then_inc(free[b], 1)

                def gate_exp(i, j):
                    act.wait_ge(dl_done, i * 2 + (j + 1))
                    nc.scalar.activation(el[j][:, 0:1], dl[j][:, :], ACT.Exp).then_inc(el_done, 1)

                act.sem_inc(free[0], 1)
                act.wait_ge(ones_done, 2)
                for n in range(3):
                    qk_even(0, n)
                attention(0)
                with act.Fori(1, NIT) as i:
                    qk_even(i, 0)
                    x2_out(i - 1, 5, 0)
                    x2_out(i - 1, 6, 1)
                    qk_even(i, 1)
                    qk_even(i, 2)
                    gate_exp(i - 1, 0)
                    gate_exp(i - 1, 1)
                    attention(i)
                x2_out(NIT - 1, 5, 0)
                x2_out(NIT - 1, 6, 1)
                gate_exp(NIT - 1, 0)
                gate_exp(NIT - 1, 1)

            @block.vector
            def _(dve):
                ATT_LINKS, TAIL_LINKS = 8, 16
                count = {"att": 0, "tail": 0}

                def link_att(i, ins):
                    count["att"] += 1
                    ins.then_inc(att_link, 1)
                    dve.wait_ge(att_link, i * ATT_LINKS + count["att"])

                def link_tail(i, ins):
                    count["tail"] += 1
                    ins.then_inc(tail_link, 1)
                    dve.wait_ge(tail_link, i * TAIL_LINKS + count["tail"])

                def drain(i, b, jobs, k, dst, src):
                    dve.wait_ge(full[b], turn(i, jobs, k))
                    nc.vector.tensor_copy(dst, src).then_inc(free[b], 1)

                def qk_odd(i, n):
                    drain(i, 1, PROJ_JOBS, n + 1, qk[:, 2 * n + 1, :, :].rearrange("p a t -> p (a t)"), bank[1][:, 0:2 * W2T])

                def v_half(i, j):
                    drain(i, 1, PROJ_JOBS, 4 + j, vs[j][:, H // 2:H, 0:DH],
                          bank[1][0:TT, 0:HD // 2].rearrange("p (h e) -> p h e", e=DH))

                def sub_max(i, j):
                    dve.wait_ge(scored, i * 2 + (j + 1))
                    for g in range(NG):
                        sv = bank[2 + g][0:TT, 0:HB * TT].rearrange("q (h k) -> q h k", h=HB)
                        last = nc.vector.reduce_max(mx[j][:, g * HB:(g + 1) * HB], sv, AX.X)
                    link_att(i, last)
                    for g in range(NG):
                        sv = bank[2 + g][0:TT, 0:HB * TT].rearrange("q (h k) -> q h k", h=HB)
                        mb = mx[j][:, g * HB:(g + 1) * HB].rearrange("q (h o) -> q h o", o=1).to_broadcast([TT, HB, TT])
                        last = nc.vector.tensor_tensor(pr[j][:, g * HB:(g + 1) * HB, :], sv, mb, ALU.subtract)
                    last.then_inc(sub_done, 1)

                def pt_out(i, k):
                    drain(i, 6, ROT_JOBS, k, pt[1][:, :, :].rearrange("p h k -> p (h k)"), bank[6][0:TT, 0:HB * TT])

                def z_out(i, b, k, j, g):
                    dve.wait_ge(full[b], turn(i, ROT_JOBS, k))
                    pv = bank[b][0:TT, 0:HB * (DH + 1)].rearrange("q (h e) -> q h e", h=HB)
                    ri = rinv[j][:, g * HB:(g + 1) * HB]
                    link_att(i, nc.vector.reciprocal(ri, pv[:, :, DH]))
                    nc.vector.tensor_tensor(heads(z[j], g), pv[:, :, 0:DH],
                                            ri.rearrange("q (h o) -> q h o", o=1).to_broadcast([TT, HB, DH]),
                                            ALU.mult).then_inc(free[b], 1)

                def o_out(i, b, k, j):
                    dve.wait_ge(full[b], turn(i, ROT_JOBS, k))
                    dve.wait_ge(hb_in[j], (i + 1) * 16)
                    dve.wait_ge(acc_w[j], i * 16 + 1)
                    nc.vector.tensor_tensor(h2[j][:, :], bank[b][0:TT, 0:D], hb[j][:, :], ALU.add).then_inc(free[b], 1)
                    dve.wait_ge(free[b], turn(i, ROT_JOBS, k + 1))
                    nc.vector.bn_stats(stb[j][:, :], h2[j][:, :]).then_inc(h2_done, 1)
                    dve.wait_ge(h2_done, i * 2 + (j + 3))
                    settle(dve)
                    nc.vector.bn_aggr(mvb[j][:, :], stb[j][:, :]).then_inc(mvb_done, 1)

                def attention(i):
                    count["att"] = 0
                    v_half(i, 0)
                    sub_max(i, 0)
                    v_half(i, 1)
                    sub_max(i, 1)
                    pt_out(i, 1)
                    z_out(i, 7, 1, 0, 0)
                    z_out(i, 6, 2, 0, 1)
                    z_out(i, 7, 2, 0, 2)
                    pt_out(i, 3)
                    z_out(i, 7, 4, 1, 0)
                    o_out(i, 5, 5, 0)
                    z_out(i, 6, 5, 1, 1)
                    z_out(i, 7, 5, 1, 2)
                    o_out(i, 7, 6, 1)
                    assert count["att"] == ATT_LINKS

                def norm(i, j):
                    dve.wait_ge(rsb_done, i * 2 + (j + 1))
                    dve.wait_ge(mvb_done, i * 2 + (j + 1))
                    dve.wait_ge(xr_free[j], i + 1)
                    nc.vector.tensor_scalar(xr[j][0][:, 0:D], h2[j][:, :], mvb[j][:, 0:1], rsb[j][:, 0:1],
                                            ALU.subtract, ALU.mult).then_inc(xnb_done, 1)

                def route(i, b, k, j):
                    dve.wait_ge(full[b], turn(i, ROT_JOBS, k))
                    nc.vector.tensor_copy(lg[j][:, :], bank[b][0:TT, 0:E]).then_inc(free[b], 1)
                    dve.wait_ge(free[b], turn(i, ROT_JOBS, k + 1))
                    settle(dve)
                    link_tail(i, nc.vector.max(mx8[j][:, :], lg[j][:, :]))
                    nc.vector.tensor_tensor(dl[j][:, :], mx8[j][:, 1:2], mx8[j][:, 0:1], ALU.subtract).then_inc(dl_done, 1)
                    link_tail(i, nc.vector.max_index(ix8[j][:, :], mx8[j][:, :], lg[j][:, :]))
                    link_tail(i, nc.vector.tensor_copy(ixf[j][:, :], ix8[j][:, 0:2]))
                    for n in range(2):
                        last = nc.vector.tensor_scalar(msk[j][:, n, :], iota8[0:TT, :], ixf[j][:, n:n + 1], None, ALU.is_equal)
                    link_tail(i, last)
                    nc.vector.tensor_tensor(mskb[j][:, :], msk[j][:, 0, :], msk[j][:, 1, :], ALU.add).then_inc(mask_done, 1)

                def slots(i, b, k, j):
                    dve.wait_ge(full[b], turn(i, ROT_JOBS, k))
                    link_tail(i, nc.vector.tensor_tensor(s8[j][:, 0, :], bank[b][0:TT, 0:E], slot0[0:TT, :], ALU.add))
                    nc.vector.tensor_tensor(slot0[:, :], bank[b][:, E:2 * E], slot0[:, :], ALU.add).then_inc(free[b], 1)
                    for n in range(2):
                        last = nc.vector.tensor_tensor_reduce(out=s8[j][:, 1 + n, :], in0=msk[j][:, n, :], in1=s8[j][:, 0, :],
                                                              scale=1.0, scalar=0.0, op0=ALU.mult, op1=ALU.add,
                                                              accum_out=slf[j][:, n:n + 1])
                    link_tail(i, last)
                    dve.wait_ge(free[b], turn(i, ROT_JOBS, k + 1))
                    nc.vector.tensor_copy(sli[j][:, :], slf[j][:, :])

                def weights(i, j):
                    dve.wait_ge(el_done, i * 2 + (j + 1))
                    link_tail(i, nc.vector.tensor_scalar(el[j][:, 1:2], el[j][:, 0:1], 1.0, None, ALU.add))
                    link_tail(i, nc.vector.reciprocal(xr[j][0][:, D:D + 1], el[j][:, 1:2]))
                    nc.vector.tensor_tensor(xr[j][1][:, D:D + 1], el[j][:, 0:1], xr[j][0][:, D:D + 1],
                                            ALU.mult).then_inc(slot_done, 1)

                def tail(i, project):
                    count["tail"] = 0
                    norm(i, 0)
                    norm(i, 1)
                    project(0)
                    route(i, 7, 7, 0)
                    route(i, 5, 8, 1)
                    project(1)
                    slots(i, 6, 8, 0)
                    slots(i, 7, 8, 1)
                    project(2)
                    weights(i, 0)
                    weights(i, 1)
                    assert count["tail"] == TAIL_LINKS

                for j in range(2):
                    nc.vector.memset(x2t1[j][D1:D1 + 1, :], 1.0).then_inc(row1_done, 1)
                dve.sem_inc(sub_done, 1)
                dve.sem_inc(h2_done, 2)
                for b in (1, 5, 6, 7):
                    dve.sem_inc(free[b], 1)
                dve.wait_ge(ones_done, 2)
                for n in range(3):
                    qk_odd(0, n)
                attention(0)
                with dve.Fori(1, NIT) as i:
                    tail(i - 1, lambda n: qk_odd(i, n))
                    attention(i)
                tail(NIT - 1, lambda n: None)

            @block.tensor
            def _(pe):
                mm = nc.tensor.matmul

                def start(i, b, jobs, k):
                    pe.wait_ge(free[b], turn(i, jobs, k))

                def qk_proj(i, c):
                    b, k = c % 2, c // 2 + 1
                    start(i, b, PROJ_JOBS, k)
                    for n in range(2):
                        o = bank[b][:, n * W2T:(n + 1) * W2T]
                        mm(o, wqk0[:, n, c * P:(c + 1) * P], xs0[:, :], start=True, stop=False)
                        last = mm(o, wqk1[:, n, c * P:(c + 1) * P], xs1[:, :], start=False, stop=True)
                    last.then_inc(full[b], 1)

                def v_proj(i, j):
                    for b in range(2):
                        start(i, b, PROJ_JOBS, 4 + j)
                        o = bank[b][0:TT, 0:HD // 2]
                        cols = slice(b * HD // 2, (b + 1) * HD // 2)
                        mm(o, xs0[:, j * TT:(j + 1) * TT], wv0[:, cols], start=True, stop=False)
                        mm(o, xs1[:, j * TT:(j + 1) * TT], wv1[:, cols], start=False, stop=True).then_inc(full[b], 1)

                def scores(i, j):
                    pe.wait_ge(sub_done, i * 2 + (j + 1))
                    for g in range(NG):
                        mm(bank[2 + g][0:TT, 0:HB * TT], identb[:, :], mask[:, :], start=True, stop=True)

                    def head(g, n):
                        h = head_of(g, n)
                        rows = slice(DH * (h % 2), DH * (h % 2 + 1))
                        q = qk[rows, h // 2, 0, j * TT:(j + 1) * TT]
                        k = qk[rows, h // 2, 1, j * TT:(j + 1) * TT]
                        return mm(bank[2 + g][0:TT, n * TT:(n + 1) * TT], q, k, start=False, stop=True,
                                  skip_group_check=True)

                    head(2, 0)
                    head(2, 2).then_inc(even_done, 1)
                    for n in range(HB):
                        head(0, n)
                    pe.wait_ge(even_done, i * 2 + (j + 1))
                    head(2, 1)
                    head(2, 3)
                    for n in range(HB):
                        last = head(1, n)
                    last.then_inc(scored, 1)

                def pt_job(i, b, k, j, g):
                    pe.wait_ge(exp_done, i * 2 + (j + 1))
                    start(i, b, ROT_JOBS, k)
                    for n in range(HB):
                        last = nc.tensor.transpose(bank[b][0:TT, n * TT:(n + 1) * TT], pr[j][:, g * HB + n, :], ident[0:TT, 0:TT])
                    last.then_inc(full[b], 1)

                def pv_job(i, b, k, j, g, pt_bank, pt_turn):
                    pe.wait_ge(free[pt_bank], turn(i, ROT_JOBS, pt_turn + 1))
                    start(i, b, ROT_JOBS, k)
                    for n in range(HB):
                        last = mm(bank[b][0:TT, n * (DH + 1):(n + 1) * (DH + 1)], pt[g][:, n, :], vs[j][:, head_of(g, n), :],
                                  start=True, stop=True)
                    last.then_inc(full[b], 1)

                def zt_job(i, b, k, j, c0, n, z_turns):
                    for zb, zk in z_turns:
                        pe.wait_ge(free[zb], turn(i, ROT_JOBS, zk + 1))
                    start(i, b, ROT_JOBS, k)
                    zv = z[j][:, :, :].rearrange("q h e -> q (h e)")
                    for m in range(n):
                        last = nc.tensor.transpose(bank[b][:, m * TT:(m + 1) * TT], zv[:, (c0 + m) * P:(c0 + m + 1) * P],
                                                   ident[0:TT, 0:TT])
                    last.then_inc(full[b], 1)

                def o_job(i, b, k, j, zt_turns):
                    for zb, zk in zt_turns:
                        pe.wait_ge(free[zb], turn(i, ROT_JOBS, zk + 1))
                    start(i, b, ROT_JOBS, k)
                    for c in range(HC):
                        last = mm(bank[b][0:TT, 0:D], zt[j][:, c, :], wo[:, c, :], start=(c == 0), stop=(c == HC - 1))
                    last.then_inc(full[b], 1)

                def attention(i):
                    pe.wait_ge(free[0], turn(i, PROJ_JOBS, 4))
                    v_proj(i, 0)
                    pe.wait_ge(free[1], turn(i, PROJ_JOBS, 4))
                    scores(i, 0)
                    v_proj(i, 1)
                    scores(i, 1)
                    pt_job(i, 5, 1, 0, 0)
                    pt_job(i, 6, 1, 0, 1)
                    pe.wait_ge(free[0], turn(i, PROJ_JOBS, 6))
                    pe.wait_ge(free[1], turn(i, PROJ_JOBS, 6))
                    pv_job(i, 7, 1, 0, 0, 5, 1)
                    pt_job(i, 5, 2, 0, 2)
                    pv_job(i, 6, 2, 0, 1, 6, 1)
                    pv_job(i, 7, 2, 0, 2, 5, 2)
                    pt_job(i, 5, 3, 1, 0)
                    pt_job(i, 6, 3, 1, 1)
                    zt_job(i, 7, 3, 0, 0, 4, [(7, 1), (6, 2)])
                    pt_job(i, 5, 4, 1, 2)
                    zt_job(i, 6, 4, 0, 4, 2, [(7, 2)])
                    pv_job(i, 7, 4, 1, 0, 5, 3)
                    o_job(i, 5, 5, 0, [(7, 3), (6, 4)])
                    pv_job(i, 6, 5, 1, 1, 6, 3)
                    pv_job(i, 7, 5, 1, 2, 5, 4)
                    zt_job(i, 5, 6, 1, 0, 4, [(7, 4), (6, 5)])
                    zt_job(i, 6, 6, 1, 4, 2, [(7, 5)])
                    o_job(i, 7, 6, 1, [(5, 6), (6, 6)])

                def x2_job(i, b, j):
                    pe.wait_ge(xnb_done, i * 2 + (j + 1))
                    start(i, b, ROT_JOBS, 7)
                    nc.tensor.transpose(bank[b][:, 0:TT], xr[j][0][:, 0:P], ident[0:TT, 0:TT])
                    nc.tensor.transpose(bank[b][0:D1, TT:2 * TT], xr[j][0][:, P:D], ident[0:TT, 0:TT]).then_inc(full[b], 1)

                def gate_job(i, b, k, j, x2_bank):
                    pe.wait_ge(free[x2_bank], turn(i, ROT_JOBS, 8))
                    start(i, b, ROT_JOBS, k)
                    mm(bank[b][0:TT, 0:E], x2t0[j][:, :], gw0[:, :], start=True, stop=False)
                    mm(bank[b][0:TT, 0:E], x2t1[j][:, :], gw1[:, :], start=False, stop=True).then_inc(full[b], 1)

                def rank_job(i, b, k, j, rows):
                    pe.wait_ge(mask_done, i * 2 + (j + 1))
                    start(i, b, ROT_JOBS, k)
                    mm(bank[b][0:TT, 0:E], tri[0:rows, :], mskb[j][0:rows, :], start=True, stop=True)
                    mm(bank[b][:, E:2 * E], onesb[0:rows, :], mskb[j][0:rows, :], start=True, stop=True).then_inc(full[b], 1)

                def tail(i, project, rows=(TT, TT)):
                    project(0)
                    project(1)
                    x2_job(i, 5, 0)
                    x2_job(i, 6, 1)
                    project(2)
                    gate_job(i, 7, 7, 0, 5)
                    gate_job(i, 5, 8, 1, 6)
                    project(3)
                    project(4)
                    rank_job(i, 6, 8, 0, rows[0])
                    rank_job(i, 7, 8, 1, rows[1])
                    project(5)

                pe.wait_ge(ld_w, 16 * N_W)
                pe.wait_ge(ones_done, 2)
                pe.wait_ge(row1_done, 2)
                pe.wait_ge(xs_ready, 1)
                for c in range(HC):
                    qk_proj(0, c)
                attention(0)
                with pe.Fori(1, NIT) as i:
                    pe.wait_ge(xs_ready, i + 1)
                    tail(i - 1, lambda c: qk_proj(i, c))
                    attention(i)
                tail(NIT - 1, lambda c: None, (TT, LAST))

        with ExitStack() as cc:
            def sbc(name, shape, dt=fp32):
                return cc.enter_context(nc.sbuf_tensor(name, shape, dt))

            def semc(name):
                return cc.enter_context(nc.semaphore(name))

            xq = [sbc(f"xq{u}", [P, ROW]) for u in range(U)]
            idx = [sbc(f"idx{u}", [P, 1], u32) for u in range(U)]
            xqt0, xqt1 = sbc("xqt0", [P, P]), sbc("xqt1", [D1 + 1, P])
            hid = sbc("hid", [P, F])
            hidt = sbc("hidt", [P, KH, P])
            ysum = [sbc(f"ysum{u}", [P, D]) for u in range(2)]
            yout = [sbc(f"yout{u}", [P, D]) for u in range(U)]
            padrow = sbc("padrow", [P, ROW])
            padid = sbc("padid", [P, 1], i32)
            cntf, cnti = sbc("cntf", [1, E]), sbc("cnti", [1, E], i32)
            tilef = sbc("tilef", [1, E])
            cum = [sbc(f"cum{n}", [1, E]) for n in range(4)]
            tii, tif = sbc("tii", [1, NTILE], i32), sbc("tif", [1, NTILE])
            cmp = sbc("cmp", [1, NTILE, E])
            cmpt = sbc("cmpt", [1, NTILE, E])
            et, before = sbc("et", [1, NTILE]), sbc("before", [1, NTILE])
            used = sbc("used", [1, NTILE])
            rowf = sbc("rowf", [1, NTILE])
            rowtab, exptab = sbc("rowtab", [1, NTILE], i32), sbc("exptab", [1, NTILE], i32)
            padtab = sbc("padtab", [1, E], i32)

            iotas, pads = semc("iotas"), semc("pads")
            settled = semc("settled_c")
            tables, link_c = semc("tables"), semc("link_c")
            pad_w = semc("pad_w")
            xq_in = [semc(f"xq_in{u}") for u in range(U)]
            xt_full, xt_ready = semc("xt_full"), semc("xt_ready")
            h_full, gelu_done = semc("h_full"), semc("gelu_done")
            ht_full, ht_dve, ht_act = semc("ht_full"), semc("ht_dve"), semc("ht_act")
            y_full, y_added, y_scaled = semc("y_full"), semc("y_added"), semc("y_scaled")
            sent = [semc(f"sent{u}") for u in range(U)]
            added = semc("added")
            out_w = semc("out_w")

            NLOOP = NTILE // U
            block = cc.enter_context(nc.Block())

            @block.sync
            def _(sp):
                def load_rows(t, u):
                    row = sp.value_load(rowtab[0:1, bass.ds(t, 1)], min_val=0, max_val=E * REGION)
                    sp.dma_start(xq[u][:, :], queue[bass.ds(row, P), :]).then_inc(xq_in[u], 16)

                sp.wait_ge(pads, 1)
                sp.dma_start(queue[E * REGION:E * REGION + P, :], padrow[:, :]).then_inc(pad_w, 16)
                sp.wait_ge(tables, 1)
                for e in range(E):
                    row = sp.value_load(padtab[0:1, e:e + 1], min_val=e * REGION, max_val=e * REGION + NTOK)
                    sp.dma_start(queue[bass.ds(row, P), :], padrow[:, :]).then_inc(pad_w, 16)
                sp.wait_ge(tables, 2)
                sp.wait_ge(pad_w, 16 * (E + 1))
                for u in range(U):
                    load_rows(u, u)
                with sp.Fori(0, NLOOP - 1) as i:
                    for u in range(U):
                        sp.wait_ge(y_scaled, i * U + (u + 3))
                        load_rows((i + 1) * U + u, u)
                sp.wait_ge(added, NTILE + U)
                sp.dma_start(out.rearrange("b t d -> (b t) d"), acc[0:NTOK, :]).then_inc(out_w, 16)
                sp.wait_ge(out_w, 16)

            @block.gpsimd
            def _(pool):
                pool.iota(tii[:, :], pattern=[[1, NTILE]], base=0, channel_multiplier=0).then_inc(iotas, 1)
                pool.memset(padrow[:, :], 0.0).then_inc(iotas, 1)
                pool.iota(padid[:, :], pattern=[[0, 1]], base=NTOK, channel_multiplier=1).then_inc(iotas, 1)
                pool.wait_ge(iotas, 3)
                pool.tensor_copy(padrow[:, D + 1:D + 2], padid[:, :]).then_inc(pads, 1)
                pool.sem_inc(added, U)
                with pool.Fori(0, NLOOP) as i:
                    for u in range(U):
                        pool.wait_ge(y_scaled, i * U + (u + 3))
                        pool.sem_inc(settled, 1)
                        nc.gpsimd.indirect_dma_start(
                            out=acc[:, :], out_offset=bass.IndirectOffsetOnAxis(idx[u][:, :], 0),
                            in_=yout[u][:, :], in_offset=None, bounds_check=NTOK + P - 1, oob_is_err=True,
                            compute_op=ALU.add).then_inc(sent[u], 16)
                        pool.wait_ge(sent[u], i * 16 + 16)
                        pool.sem_inc(added, 1)

            @block.scalar
            def _(act):
                def step(i, u):
                    t = i * U + u
                    act.wait_ge(h_full, t + 1)
                    for n in range(2):
                        last = nc.scalar.activation(hid[:, n * F // 2:(n + 1) * F // 2],
                                                    bank[1 + 2 * (u % 2) + n][:, 0:F // 2], ACT.Gelu)
                    last.then_inc(gelu_done, 1)

                def rest(i, u):
                    t = i * U + u
                    act.wait_ge(ht_full, t * 2 + 2)
                    nc.scalar.copy(hidt[:, 4:KH, :], bank[6][:, 0:(KH - 4) * P]).then_inc(ht_act, 1)

                def scale(i, u):
                    t = i * U + u
                    act.wait_ge(y_added, t + 2)
                    act.wait_ge(added, t + 1)
                    nc.scalar.activation(yout[u][:, :], ysum[u % 2][:, :], ACT.Copy,
                                         scale=xq[u][:, D:D + 1]).then_inc(y_scaled, 1)

                act.sem_inc(gelu_done, 1)
                act.sem_inc(y_scaled, 2)
                step(0, 0)

                def body(i, more=True):
                    for u in range(U):
                        rest(i, u)
                        if u < U - 1:
                            step(i, u + 1)
                        elif more:
                            step(i + 1, 0)
                        scale(i, u)

                with act.Fori(0, NLOOP - 1) as i:
                    body(i)
                body(NLOOP - 1, more=False)

            @block.vector
            def _(dve):
                links = [0]

                def link(ins):
                    links[0] += 1
                    ins.then_inc(link_c, 1)
                    dve.wait_ge(link_c, links[0])

                nc.vector.tensor_copy(padtab[:, :], slot0[0:1, :]).then_inc(tables, 1)
                nc.vector.memset(xqt1[D1:D1 + 1, :], 1.0)
                link(nc.vector.tensor_scalar(cntf[:, :], iota8[0:1, :], -float(REGION), float(P - 1), ALU.mult, ALU.add))
                link(nc.vector.tensor_tensor(cntf[:, :], cntf[:, :], slot0[0:1, :], ALU.add))
                link(nc.vector.tensor_copy(cnti[:, :], cntf[:, :]))
                link(nc.vector.tensor_scalar(cnti[:, :], cnti[:, :], 7, None, ALU.arith_shift_right))
                link(nc.vector.tensor_copy(tilef[:, :], cnti[:, :]))
                link(nc.vector.tensor_copy(cum[0][:, :], tilef[:, :]))
                for n in range(3):
                    d = 1 << n
                    nc.vector.tensor_copy(cum[n + 1][:, 0:d], cum[n][:, 0:d])
                    link(nc.vector.tensor_tensor(cum[n + 1][:, d:E], cum[n][:, d:E], cum[n][:, 0:E - d], ALU.add))
                dve.wait_ge(iotas, 1)
                link(nc.vector.tensor_copy(tif[:, :], tii[:, :]))
                link(nc.vector.tensor_tensor(cmp[:, :, :], tif[:, :].rearrange("a (t o) -> a t o", o=1).to_broadcast([1, NTILE, E]),
                                             cum[3][:, :].rearrange("a (o e) -> a o e", o=1).to_broadcast([1, NTILE, E]), ALU.is_ge))
                link(nc.vector.tensor_tensor(cmpt[:, :, :], cmp[:, :, :],
                                             tilef[:, :].rearrange("a (o e) -> a o e", o=1).to_broadcast([1, NTILE, E]), ALU.mult))
                nc.vector.reduce_sum(et[:, :], cmp[:, :, :], AX.X)
                link(nc.vector.reduce_sum(before[:, :], cmpt[:, :, :], AX.X))
                nc.vector.tensor_scalar(used[:, :], et[:, :], float(E), float(P), ALU.is_lt, ALU.mult)
                link(nc.vector.tensor_tensor(rowf[:, :], tif[:, :], before[:, :], ALU.subtract))
                link(nc.vector.tensor_tensor(rowf[:, :], rowf[:, :], used[:, :], ALU.mult))
                link(nc.vector.scalar_tensor_tensor(rowf[:, :], et[:, :], float(REGION), rowf[:, :], ALU.mult, ALU.add))
                nc.vector.tensor_copy(rowtab[:, :], rowf[:, :])
                link(nc.vector.tensor_scalar(before[:, :], et[:, :], float(E - 1), None, ALU.min))
                nc.vector.tensor_copy(exptab[:, :], before[:, :]).then_inc(tables, 1)
                dve.wait_ge(tables, 2)

                def rows_in(i, u):
                    t = i * U + u
                    dve.wait_ge(xt_full, t + 1)
                    nc.vector.tensor_copy(xqt0[:, :], bank[0][:, 0:P])
                    nc.vector.tensor_copy(xqt1[0:D1, :], bank[0][0:D1, P:2 * P]).then_inc(xt_ready, 1)
                    dve.wait_ge(xq_in[u], i * 16 + 16)
                    dve.wait_ge(added, t + 1)
                    nc.vector.tensor_copy(idx[u][:, :], xq[u][:, D + 1:D + 2])

                def rest(i, u):
                    t = i * U + u
                    dve.wait_ge(ht_full, t * 2 + 1)
                    nc.vector.tensor_copy(hidt[:, 0:4, :], bank[5][:, 0:4 * P]).then_inc(ht_dve, 1)

                def add_bias(i, u):
                    t = i * U + u
                    e = dve.value_load(exptab[0:1, bass.ds(t, 1)], min_val=0, max_val=E - 1)
                    dve.wait_ge(y_full, t + 1)
                    dve.wait_ge(y_scaled, t + 1)
                    nc.vector.tensor_tensor(ysum[u % 2][:, :], bank[7][:, 0:D],
                                            b2s[:, :, :].rearrange("p e d -> p (e d)")[:, bass.ds(e * D, D)],
                                            ALU.add).then_inc(y_added, 1)

                dve.sem_inc(y_added, 1)
                rows_in(0, 0)

                def body(i, more=True):
                    for u in range(U):
                        if u < U - 1:
                            rows_in(i, u + 1)
                        elif more:
                            rows_in(i + 1, 0)
                        rest(i, u)
                        add_bias(i, u)

                with dve.Fori(0, NLOOP - 1) as i:
                    body(i)
                body(NLOOP - 1, more=False)

            @block.tensor
            def _(pe):
                mm = nc.tensor.matmul
                w1a_f = w1a[:, :, :].rearrange("p e f -> p (e f)")
                w1b_f = w1b[:, :, :].rearrange("p e f -> p (e f)")
                w2_f = w2s.rearrange("p e k d -> p (e k d)")

                def transpose_rows(i, u):
                    pe.wait_ge(xq_in[u], i * 16 + 16)
                    nc.tensor.transpose(bank[0][:, 0:P], xq[u][:, 0:P], ident[:, :])
                    nc.tensor.transpose(bank[0][0:D1, P:2 * P], xq[u][:, P:D], ident[:, :]).then_inc(xt_full, 1)

                def up(i, u, e):
                    t = i * U + u
                    pe.wait_ge(xt_ready, t + 1)
                    for n in range(2):
                        o = bank[1 + 2 * (u % 2) + n][:, 0:F // 2]
                        mm(o, xqt0[:, :], w1a_f[:, bass.ds(e * F + n * F // 2, F // 2)], start=True, stop=False)
                        last = mm(o, xqt1[:, :], w1b_f[:, bass.ds(e * F + n * F // 2, F // 2)], start=False, stop=True)
                    last.then_inc(h_full, 1)

                def transpose_hidden(i, u):
                    t = i * U + u
                    pe.wait_ge(gelu_done, t + 2)
                    for k in range(KH):
                        last = nc.tensor.transpose(bank[5 + k // 4][:, (k % 4) * P:(k % 4 + 1) * P],
                                                   hid[:, k * P:(k + 1) * P], ident[:, :])
                        if k in (3, KH - 1):
                            last.then_inc(ht_full, 1)

                def down(i, u, e):
                    t = i * U + u
                    pe.wait_ge(ht_dve, t + 1)
                    pe.wait_ge(ht_act, t + 1)
                    pe.wait_ge(y_added, t + 1)
                    for k in range(KH):
                        last = mm(bank[7][:, 0:D], hidt[:, k, :], w2_f[:, bass.ds(e * (KH * D) + k * D, D)],
                                  start=(k == 0), stop=(k == KH - 1))
                    last.then_inc(y_full, 1)

                def expert(t):
                    return pe.value_load(exptab[0:1, bass.ds(t, 1)], min_val=0, max_val=E - 1)

                def body(i, more=True):
                    for u in range(U):
                        nxt = (i, u + 1) if u < U - 1 else (i + 1, 0)
                        ahead = more or u < U - 1
                        if ahead:
                            transpose_rows(*nxt)
                        transpose_hidden(i, u)
                        if ahead:
                            up(*nxt, expert(nxt[0] * U + nxt[1]))
                        down(i, u, expert(i * U + u))

                pe.wait_ge(tables, 2)
                pe.wait_ge(ld_w1, 48)
                pe.wait_ge(ld_w2, 16)
                pe.wait_ge(pads, 1)
                transpose_rows(0, 0)
                up(0, 0, expert(0))
                with pe.Fori(0, NLOOP - 1) as i:
                    body(i)
                body(NLOOP - 1, more=False)


_INS = ["x", "cls_tok", "L0_tok_W", "L0_tok_b", "L0_attn_W_Q", "L0_attn_b_Q", "L0_attn_W_K", "L0_attn_b_K",
        "L0_attn_W_V", "L0_attn_b_V", "L0_attn_W_O", "L0_attn_b_O", "L0_ffn_gate_w", "L0_ffn_gate_b",
        "L0_ffn_w1", "L0_ffn_b1", "L0_ffn_w2", "L0_ffn_b2"]


def kernel(**inputs):
    import numpy as np
    import concourse.bacc as bacc
    from concourse.bass_utils import run_bass_kernel_spmd

    nc = bacc.Bacc("TRN2", target_bir_lowering=False, num_devices=1)
    arrays, args = {}, []
    for name in _INS:
        a = np.ascontiguousarray(inputs[name])
        arrays[f"in_{name}"] = a
        args.append(nc.dram_tensor(f"in_{name}", a.shape, mybir.dt.from_np(a.dtype), kind="ExternalInput").ap())
    batch, channels, side, _ = inputs["x"].shape
    tokens = (side // 16) ** 2 + 1
    out = nc.dram_tensor("out_0", [batch, tokens, inputs["L0_tok_W"].shape[0]], mybir.dt.float32, kind="ExternalOutput").ap()
    vit_tower_kernel(nc, *args, out)
    r = run_bass_kernel_spmd(nc, [arrays], core_ids=[0])
    return r.results[0]["out_0"]
```

```python
import concourse.bass as bass
from concourse import mybir
from contextlib import ExitStack


def vit_tower_kernel(nc, x, cls_tok, tok_w, tok_b, w_q, b_q, w_k, b_k, w_v, b_v, w_o, b_o,
                     gate_w, gate_b, w1, b1, w2, b2, out):
    fp32, bf16 = mybir.dt.float32, mybir.dt.bfloat16
    fp32r = mybir.dt.float32r
    i32, u32 = mybir.dt.int32, mybir.dt.uint32
    ALU = mybir.AluOpType
    ACT = mybir.ActivationFunctionType
    AX = mybir.AxisListType

    P = 128
    NI, C, IMG, _ = x.shape
    D, F_IN = tok_w.shape
    KER = 16
    STEP = IMG // KER
    T = STEP * STEP + 1
    H, _, DH = w_q.shape
    HD = H * DH
    E, _, F = w1.shape
    D1 = D - P
    KF = F_IN // P
    ROWS_A = P // NI
    GROUPS = STEP // ROWS_A
    TILES_A = GROUPS * STEP
    G3 = 3
    TT = G3 * T
    NT = -(-NI // G3)
    NIT = NT // 2
    NTOK = NI * T
    NPAD = NT * TT
    LAST = NTOK - (NT - 1) * TT
    HC = H // 2
    HB = 4
    NG = H // HB
    KH = F // P
    W2T = 2 * TT
    ROW = D + 2
    REGION = NTOK + P
    NTILE = (2 * NTOK - E) // P + E
    U = 4
    EPS = 1e-5
    CAUSAL = -1e5 * DH ** 0.5
    FAR = -1e30
    assert NTILE % U == 0 and NT % 2 == 0 and ROWS_A * NI == P

    resid = nc.dram_tensor("resid", [NI, T, D], fp32).ap()
    resid_rows = resid.rearrange("b t d -> (b t) d")
    acc = nc.dram_tensor("acc", [NTOK + P, D], fp32).ap()
    b1_split = nc.dram_tensor("b1_split", [2, E * F], fp32).ap()
    queue = nc.dram_tensor("queue", [(E + 1) * REGION, ROW], fp32).ap()

    ctx = ExitStack()
    with ctx:
        def sb(name, shape, dt=fp32):
            return ctx.enter_context(nc.sbuf_tensor(name, shape, dt))

        def sem(name):
            return ctx.enter_context(nc.semaphore(name))

        bank = [ctx.enter_context(nc.psum_tensor(f"bank{i}", [P, 512], fp32)) for i in range(8)]

        ident = sb("ident", [P, P])
        identb = sb("identb", [TT, TT], bf16)
        maskf = sb("maskf", [TT, HB * TT])
        mask = sb("mask", [TT, HB * TT], bf16)
        trif = sb("trif", [TT, TT])
        tri = sb("tri", [TT, TT], bf16)
        onesb = sb("onesb", [TT, P], bf16)
        mhalf = sb("mhalf", [P, 1])
        iota8 = sb("iota8", [P, E])
        idtab = sb("idtab", [P, NT])
        front = sb("front", [P, E * F])
        xt0, xt1 = front[:, 0:NPAD], front[0:D1 + 1, NPAD:2 * NPAD]
        wtok = front[:, 2 * NPAD:2 * NPAD + KF * D].rearrange("p (k d) -> p k d", k=KF)
        w1ah = front[:, :].bitcast(fp32r)
        mid = sb("mid", [P, E * F])
        wqk0 = mid[:, 0:2 * HD].rearrange("p (n d) -> p n d", n=2)
        wqk1 = mid[0:D1 + 1, 2 * HD:4 * HD].rearrange("p (n d) -> p n d", n=2)
        wv0, wv1 = mid[:, 4 * HD:5 * HD], mid[0:D1 + 1, 5 * HD:6 * HD]
        tokb, bo = mid[:, 6 * HD:6 * HD + D], mid[:, 6 * HD + D:6 * HD + 2 * D]
        w1bh = mid[:, :].bitcast(fp32r)
        assert 2 * NPAD + KF * D <= E * F and 6 * HD + 2 * D <= E * F
        wo = sb("wo", [P, HC, D])
        gw0, gw1 = sb("gw0", [P, E]), sb("gw1", [D1 + 1, E])
        w1a, w1b = sb("w1a", [P, E, F]), sb("w1b", [P, E, F])
        w1al = w1a[:, :, :].rearrange("p e f -> p (e f)").bitcast(fp32r)
        w1bl = w1b[0:D1 + 2, :, :].rearrange("p e f -> p (e f)").bitcast(fp32r)
        xw2 = sb("xw2", [P, 2 * C * KER * IMG])
        xin = [xw2[:, g * C * KER * IMG:(g + 1) * C * KER * IMG] for g in range(2)]
        w2s = xw2[:, 0:E * KH * D].rearrange("p (e k d) -> p e k d", e=E, k=KH)
        b2s = sb("b2s", [P, E, D])
        slot0 = sb("slot0", [P, E])
        rowtab, exptab = sb("rowtab", [1, NTILE], i32), sb("exptab", [1, NTILE], i32)
        padtab = sb("padtab", [1, E], i32)

        ld_tokw, ld_small, ld_cls = sem("ld_tokw"), sem("ld_small"), sem("ld_cls")
        ld_bias, tables = sem("ld_bias"), sem("tables")
        ld_w, ld_w1, ld_w2 = sem("ld_w"), sem("ld_w1"), sem("ld_w2")
        w_acc0 = sem("w_acc0")
        const_pool, const_dve = sem("const_pool"), sem("const_dve")

        N_W = 10

        with ExitStack() as ca:
            def sba(name, shape, dt=fp32):
                return ca.enter_context(nc.sbuf_tensor(name, shape, dt))

            def sema(name):
                return ca.enter_context(nc.semaphore(name))

            wraw0, wraw1 = sba("wraw0", [P, F_IN]), sba("wraw1", [D1, F_IN])
            pxt = [sba(f"pxt{i}", [P, KF, P]) for i in range(2)]
            xc = [sba(f"xc{i}", [P, F_IN]) for i in range(2)]
            hraw = [sba(f"hraw{i}", [P, D]) for i in range(2)]
            xn = [sba(f"xn{i}", [P, D]) for i in range(2)]
            hbo = [sba(f"hbo{i}", [P, STEP, D]) for i in range(2)]
            st = [sba(f"st{i}", [P, 6]) for i in range(3)]
            mv = [sba(f"mv{i}", [P, 2]) for i in range(3)]
            ve = [sba(f"ve{i}", [P, 1]) for i in range(3)]
            rs = [sba(f"rs{i}", [P, 1]) for i in range(3)]
            clsr = sba("clsr", [NI, D])
            clsn = sba("clsn", [NI, D])
            clsbo = sba("clsbo", [NI, D])
            iotai = sba("iotai", [P, E], i32)
            idtabi = sba("idtabi", [P, NT], i32)
            zrow = sba("zrow", [P, D])

            x_in = [sema(f"x_in{i}") for i in range(2)]
            xc_done = sema("xc_done")
            wt_full, wt_out = sema("wt_full"), sema("wt_out")
            tr_done, emb_done, lt_done = sema("tr_done"), sema("emb_done"), sema("lt_done")
            px_act, px_dve = sema("px_act"), sema("px_dve")
            h_done, mv_done, rs_done, xn_done = sema("h_done"), sema("mv_done"), sema("rs_done"), sema("xn_done")
            xt_out, hbo_done, dve_link, pool_link = sema("xt_out"), sema("hbo_done"), sema("dve_link_a"), sema("pool_link_a")
            resid_w = [sema(f"resid_w{i}") for i in range(2)]
            cls_w, cls_mv, cls_rs, cls_xn, cls_full, cls_bo = (sema("cls_w"), sema("cls_mv"), sema("cls_rs"),
                                                               sema("cls_xn"), sema("cls_full"), sema("cls_bo"))

            block = ca.enter_context(nc.Block())

            @block.sync
            def _(sp):
                def load_images(g):
                    for r in range(ROWS_A):
                        row0 = (g * ROWS_A + r) * KER
                        sp.dma_start(xin[g % 2][r * NI:(r + 1) * NI, :].rearrange("b (c n) -> b c n", c=C),
                                     x[:, :, row0:row0 + KER, :].rearrange("b c i w -> b c (i w)")
                                     ).then_inc(x_in[g % 2], 16)

                sp.dma_start(wraw0[:, :], tok_w[0:P, :]).then_inc(ld_tokw, 16)
                sp.dma_start(wraw1[:, :], tok_w[P:D, :]).then_inc(ld_tokw, 16)
                load_images(0)
                sp.dma_start(clsr[:, :], cls_tok.rearrange("a b d -> (a b) d").partition_broadcast(NI)).then_inc(ld_cls, 16)
                sp.dma_start(tokb[:, :], tok_b.rearrange("(a d) -> a d", a=1).partition_broadcast(P)).then_inc(ld_bias, 16)
                sp.dma_start(bo[:, :], b_o.rearrange("(a d) -> a d", a=1).partition_broadcast(P)).then_inc(ld_bias, 16)
                load_images(1)
                sp.wait_ge(xc_done, STEP)
                load_images(2)
                for g in range(GROUPS):
                    sp.wait_ge(hbo_done, STEP * (g + 1))
                    for r in range(ROWS_A):
                        t0 = 1 + (g * ROWS_A + r) * STEP
                        sp.dma_start(resid[:, t0:t0 + STEP, :].rearrange("b t d -> b (t d)"),
                                     hbo[g % 2][r * NI:(r + 1) * NI, :, :].rearrange("b t d -> b (t d)")
                                     ).then_inc(resid_w[g % 2], 16)
                sp.wait_ge(cls_bo, 1)
                sp.dma_start(resid[:, 0, :], clsbo[:, :]).then_inc(cls_w, 16)
                sp.wait_ge(xc_done, TILES_A)
                sp.dma_start(w2s, w2.rearrange("e (k p) d -> p e k d", p=P)).then_inc(ld_w2, 16)
                sp.wait_ge(cls_w, 16)
                sp.wait_ge(resid_w[0], 64)
                sp.wait_ge(resid_w[1], 32)

            @block.scalar
            def _(act):
                for k in range(KF):
                    act.wait_ge(wt_full, k + 1)
                    nc.scalar.copy(wtok[:, k, :], bank[k][:, 0:D]).then_inc(wt_out, 1)
                act.wait_ge(x_in[0], 32)
                for n, (w, b) in enumerate([(w_q, b_q), (w_k, b_k)]):
                    act.dma_start(wqk0[:, n, :].rearrange("c (h e) -> c h e", h=H),
                                  w[:, 0:P, :].rearrange("h c e -> c h e")).then_inc(ld_w, 16)
                    act.dma_start(wqk1[0:D1, n, :].rearrange("c (h e) -> c h e", h=H),
                                  w[:, P:D, :].rearrange("h c e -> c h e")).then_inc(ld_w, 16)
                    act.dma_start(wqk1[D1:D1 + 1, n, :], b.rearrange("(a h) e -> a (h e)", a=1)).then_inc(ld_w, 16)
                act.dma_start(wv0[:, :].rearrange("c (h e) -> c h e", h=H),
                              w_v[:, 0:P, :].rearrange("h c e -> c h e")).then_inc(ld_w, 16)
                act.dma_start(wv1[0:D1, :].rearrange("c (h e) -> c h e", h=H),
                              w_v[:, P:D, :].rearrange("h c e -> c h e")).then_inc(ld_w, 16)
                act.dma_start(wv1[D1:D1 + 1, :], b_v.rearrange("(a h) e -> a (h e)", a=1)).then_inc(ld_w, 16)
                act.dma_start(wo[:, :, :], w_o.rearrange("(c a) e d -> (a e) c d", a=2)).then_inc(ld_w, 16)
                act.dma_start(gw0[:, :], gate_w[0:P, :]).then_inc(ld_small, 16)
                act.dma_start(gw1[0:D1, :], gate_w[P:D, :]).then_inc(ld_small, 16)
                act.dma_start(gw1[D1:D1 + 1, :], gate_b.rearrange("(a e) -> a e", a=1)).then_inc(ld_small, 16)
                act.dma_start(b2s[:, :, :].rearrange("p e d -> p (e d)"),
                              b2.rearrange("(a e) d -> a (e d)", a=1).partition_broadcast(P)).then_inc(ld_small, 16)
                act.wait_ge(const_pool, 2)
                act.dma_start(acc[NTOK:NTOK + P, :], zrow[:, :]).then_inc(w_acc0, 16)
                for s in range(TILES_A + 3):
                    if s < TILES_A:
                        act.wait_ge(tr_done, s + 1)
                        if s >= 2:
                            act.wait_ge(emb_done, s - 1)
                        nc.scalar.copy(pxt[s % 2][:, 0:4, :], bank[2 * (s % 2)][:, :]).then_inc(px_act, 1)
                    if s == 2:
                        act.wait_ge(cls_full, 1)
                        act.wait_ge(const_pool, 5)
                        nc.scalar.copy(xt0[:, 0:NTOK].rearrange("c (b t) -> c b t", t=T)[:, :, 0], bank[7][:, 0:NI])
                        nc.scalar.copy(xt1[0:D1, 0:NTOK].rearrange("c (b t) -> c b t", t=T)[:, :, 0],
                                       bank[7][0:D1, P:P + NI]).then_inc(xt_out, 1)
                    n = s - 3
                    if n >= 0:
                        g, pj = divmod(n, STEP)
                        act.wait_ge(lt_done, n + 1)
                        for xt, rows, off in ((xt0, P, 0), (xt1, D1, P)):
                            dst = xt[0:rows, 0:NTOK].rearrange("c (b t) -> c b t", t=T)
                            t0 = 1 + g * ROWS_A * STEP + pj
                            dst = dst[:, :, t0:t0 + STEP + 1:STEP].rearrange("c b r -> c r b")
                            last = nc.scalar.copy(dst, bank[6 + n % 2][0:rows, off:off + P].rearrange("c (r b) -> c r b", r=ROWS_A))
                        last.then_inc(xt_out, 1)
                act.wait_ge(w_acc0, 16)

            @block.gpsimd
            def _(pool):
                pool.memset(ident[:, :], 0.0).then_inc(pool_link, 1)
                pool.wait_ge(pool_link, 1)
                pool.affine_select(out=ident[:, :], in_=ident[:, :], compare_op=ALU.not_equal, fill=1.0,
                                   base=0, pattern=[[-1, P]], channel_multiplier=1).then_inc(const_pool, 1)
                pool.memset(mhalf[:, :], -0.5)
                pool.memset(zrow[:, :], 0.0).then_inc(const_pool, 1)
                pool.memset(xt0[:, NTOK:NPAD], 0.0).then_inc(const_pool, 1)
                pool.memset(xt1[0:D1, NTOK:NPAD], 0.0).then_inc(const_pool, 1)
                pool.wait_ge(const_pool, 4)
                pool.memset(xt1[D1:D1 + 1, :], 1.0).then_inc(const_pool, 1)
                pool.wait_ge(const_pool, 5)
                pool.memset(maskf[:, :], 0.0).then_inc(pool_link, 1)
                pool.memset(trif[:, :], 1.0).then_inc(pool_link, 1)
                pool.wait_ge(pool_link, 3)
                m4 = maskf[:, :].rearrange("q (h k) -> q h k", h=HB)
                m5 = maskf[:, :].rearrange("q (h b k) -> q h b k", h=HB, b=G3)
                pool.affine_select(out=m4, in_=m4, compare_op=ALU.is_ge, fill=CAUSAL, base=0,
                                   pattern=[[0, HB], [-1, TT]], channel_multiplier=1).then_inc(pool_link, 1)
                pool.wait_ge(pool_link, 4)
                pool.affine_select(out=m5, in_=m5, compare_op=ALU.is_ge, fill=FAR, base=T - 1,
                                   pattern=[[0, HB], [T, G3], [0, T]], channel_multiplier=-1).then_inc(pool_link, 1)
                pool.wait_ge(pool_link, 5)
                pool.affine_select(out=m5, in_=m5, compare_op=ALU.is_ge, fill=FAR, base=0,
                                   pattern=[[0, HB], [-T, G3], [0, T]], channel_multiplier=1).then_inc(pool_link, 1)
                pool.affine_select(out=trif[:, :], in_=trif[:, :], compare_op=ALU.is_ge, fill=0.0, base=-1,
                                   pattern=[[1, TT]], channel_multiplier=-1).then_inc(pool_link, 1)
                pool.iota(iotai[:, :], pattern=[[1, E]], base=0, channel_multiplier=0).then_inc(pool_link, 1)
                pool.iota(idtabi[:, :], pattern=[[TT, NT]], base=0, channel_multiplier=1).then_inc(pool_link, 1)
                pool.wait_ge(pool_link, 9)
                pool.memset(onesb[:, :], 1.0).then_inc(const_pool, 1)
                pool.wait_ge(cls_mv, 1)
                pool.tensor_scalar(ve[2][0:NI, :], mv[2][0:NI, 1:2], EPS, None, ALU.add).then_inc(pool_link, 1)
                pool.wait_ge(pool_link, 10)
                pool.tensor_tensor(rs[2][0:NI, :], ve[2][0:NI, :], mhalf[0:NI, :], ALU.pow).then_inc(cls_rs, 1)
                pool.wait_ge(ld_bias, 32)
                pool.tensor_tensor(clsbo[:, :], clsr[:, :], bo[0:NI, :], ALU.add).then_inc(cls_bo, 1)
                for n in range(TILES_A):
                    g, pj = divmod(n, STEP)
                    pool.wait_ge(mv_done, n + 1)
                    pool.tensor_scalar(ve[n % 2][:, :], mv[n % 2][:, 1:2], EPS, None, ALU.add).then_inc(pool_link, 1)
                    pool.wait_ge(pool_link, 11 + n)
                    pool.tensor_tensor(rs[n % 2][:, :], ve[n % 2][:, :], mhalf[:, :], ALU.pow).then_inc(rs_done, 1)
                    if n == 2 * STEP:
                        pool.wait_ge(resid_w[0], 32)
                    pool.tensor_tensor(hbo[g % 2][:, pj, :], hraw[n % 2][:, :], bo[:, :], ALU.add).then_inc(hbo_done, 1)

            @block.vector
            def _(dve):
                links = [0]

                def link(ins):
                    links[0] += 1
                    ins.then_inc(dve_link, 1)
                    dve.wait_ge(dve_link, links[0])

                def gather(s):
                    g, pj = divmod(s, STEP)
                    if pj == 0:
                        dve.wait_ge(x_in[g % 2], 32 * (g // 2 + 1))
                    if s >= 2:
                        dve.wait_ge(tr_done, s - 1)
                    nc.vector.tensor_copy(xc[s % 2][:, :].rearrange("p (m k) -> p m k", k=KER),
                                          xin[g % 2].rearrange("p (m j k) -> p m j k", j=STEP, k=KER)[:, :, pj, :]
                                          ).then_inc(xc_done, 1)

                gather(0)
                gather(1)
                dve.wait_ge(ld_cls, 16)
                link(nc.vector.bn_stats(st[2][0:NI, :], clsr[:, :]))
                nc.vector.bn_aggr(mv[2][0:NI, :], st[2][0:NI, :]).then_inc(cls_mv, 1)
                for s in range(TILES_A + 2):
                    if s == 1:
                        dve.wait_ge(cls_rs, 1)
                        dve.wait_ge(cls_mv, 1)
                        nc.vector.tensor_scalar(clsn[:, :], clsr[:, :], mv[2][0:NI, 0:1], rs[2][0:NI, 0:1],
                                                ALU.subtract, ALU.mult).then_inc(cls_xn, 1)
                        dve.wait_ge(const_pool, 6)
                        nc.vector.tensor_copy(mask[:, :], maskf[:, :])
                        nc.vector.tensor_copy(tri[:, :], trif[:, :])
                        nc.vector.tensor_copy(identb[:, :], ident[0:TT, 0:TT])
                        nc.vector.tensor_copy(idtab[:, :], idtabi[:, :])
                        link(nc.vector.tensor_copy(iota8[:, :], iotai[:, :]))
                        nc.vector.tensor_scalar(slot0[:, :], iota8[:, :], float(REGION), None, ALU.mult).then_inc(const_dve, 1)
                        dve.wait_ge(ld_bias, 32)
                    if s < TILES_A:
                        dve.wait_ge(tr_done, s + 1)
                        if s >= 2:
                            dve.wait_ge(emb_done, s - 1)
                        nc.vector.tensor_copy(pxt[s % 2][:, 4:KF, :], bank[2 * (s % 2) + 1][:, 0:(KF - 4) * P]).then_inc(px_dve, 1)
                        if s + 2 < TILES_A:
                            gather(s + 2)
                    n = s - 2
                    if n >= 0:
                        dve.wait_ge(rs_done, n + 1)
                        if n >= 2:
                            dve.wait_ge(lt_done, n - 1)
                        nc.vector.tensor_scalar(xn[n % 2][:, :], hraw[n % 2][:, :], mv[n % 2][:, 0:1], rs[n % 2][:, 0:1],
                                                ALU.subtract, ALU.mult).then_inc(xn_done, 1)
                    n = s - 1
                    if 0 <= n < TILES_A:
                        dve.wait_ge(emb_done, n + 1)
                        if n >= 2:
                            dve.wait_ge(hbo_done, n - 1)
                            dve.wait_ge(xn_done, n - 1)
                        nc.vector.tensor_tensor(hraw[n % 2][:, :], bank[4 + n % 2][:, 0:D], tokb[:, :], ALU.add).then_inc(h_done, 1)
                        dve.wait_ge(h_done, n + 1)
                        link(nc.vector.bn_stats(st[n % 2][:, :], hraw[n % 2][:, :]))
                        nc.vector.bn_aggr(mv[n % 2][:, :], st[n % 2][:, :]).then_inc(mv_done, 1)

            @block.tensor
            def _(pe):
                pe.wait_ge(const_pool, 1)
                pe.wait_ge(ld_tokw, 32)
                for k in range(KF):
                    nc.tensor.transpose(bank[k][:, 0:P], wraw0[:, k * P:(k + 1) * P], ident[:, :])
                    nc.tensor.transpose(bank[k][:, P:D], wraw1[:, k * P:(k + 1) * P], ident[0:D1, 0:D1]).then_inc(wt_full, 1)
                pe.wait_ge(wt_out, KF)
                for s in range(TILES_A + 3):
                    if s < TILES_A:
                        pe.wait_ge(xc_done, s + 1)
                        if s >= 2:
                            pe.wait_ge(px_act, s - 1)
                            pe.wait_ge(px_dve, s - 1)
                        for k in range(KF):
                            last = nc.tensor.transpose(bank[2 * (s % 2) + k // 4][:, (k % 4) * P:(k % 4 + 1) * P],
                                                       xc[s % 2][:, k * P:(k + 1) * P], ident[:, :])
                        last.then_inc(tr_done, 1)
                    if s == 2:
                        pe.wait_ge(cls_xn, 1)
                        nc.tensor.transpose(bank[7][:, 0:NI], clsn[:, 0:P], ident[0:NI, 0:NI])
                        nc.tensor.transpose(bank[7][0:D1, P:P + NI], clsn[:, P:D], ident[0:NI, 0:NI]).then_inc(cls_full, 1)
                    n = s - 1
                    if 0 <= n < TILES_A:
                        pe.wait_ge(px_act, n + 1)
                        pe.wait_ge(px_dve, n + 1)
                        if n >= 2:
                            pe.wait_ge(h_done, n - 1)
                        for k in range(KF):
                            last = nc.tensor.matmul(bank[4 + n % 2][:, 0:D], pxt[n % 2][:, k, :], wtok[:, k, :],
                                                    start=(k == 0), stop=(k == KF - 1))
                        last.then_inc(emb_done, 1)
                    n = s - 3
                    if n >= 0:
                        pe.wait_ge(xn_done, n + 1)
                        if n >= 1:
                            pe.wait_ge(xt_out, n)
                        nc.tensor.transpose(bank[6 + n % 2][:, 0:P], xn[n % 2][:, 0:P], ident[:, :])
                        nc.tensor.transpose(bank[6 + n % 2][0:D1, P:2 * P], xn[n % 2][:, P:D], ident[:, :]).then_inc(lt_done, 1)

        PROJ_JOBS, ROT_JOBS, TAIL_JOBS = 5, 9, 6
        with ExitStack() as cb:
            def sbb(name, shape, dt=fp32):
                return cb.enter_context(nc.sbuf_tensor(name, shape, dt))

            def semb(name):
                return cb.enter_context(nc.semaphore(name))

            xs0, xs1 = sbb("xs0", [P, W2T]), sbb("xs1", [D1 + 1, W2T])
            qk = sbb("qk", [P, HC, 2, W2T])
            vs = [sbb(f"vs{j}", [TT, H, DH + 1]) for j in range(2)]
            pr = [sbb(f"pr{j}", [TT, H, TT]) for j in range(2)]
            mx = [sbb(f"mx{j}", [TT, H]) for j in range(2)]
            pt = [sbb(f"pt{g}", [TT, HB, TT]) for g in range(NG)]
            z = [sbb(f"z{j}", [TT, H, DH]) for j in range(2)]
            rinv = [sbb(f"rinv{j}", [TT, H]) for j in range(2)]
            zt = [sbb(f"zt{j}", [P, HC, TT]) for j in range(2)]
            hb = [sbb(f"hb{j}", [TT, D]) for j in range(2)]
            h2 = [sbb(f"h2{j}", [TT, D]) for j in range(2)]
            stb = [sbb(f"stb{j}", [TT, 6]) for j in range(2)]
            mvb = [sbb(f"mvb{j}", [TT, 2]) for j in range(2)]
            veb = [sbb(f"veb{j}", [TT, 1]) for j in range(2)]
            rsb = [sbb(f"rsb{j}", [TT, 1]) for j in range(2)]
            xr = [[sbb(f"xr{j}{k}", [TT, ROW]) for k in range(2)] for j in range(2)]
            x2t0 = [sbb(f"x2t0{j}", [P, TT]) for j in range(2)]
            x2t1 = [sbb(f"x2t1{j}", [D1 + 1, TT]) for j in range(2)]
            lg = [sbb(f"lg{j}", [TT, E]) for j in range(2)]
            mx8 = [sbb(f"mx8{j}", [TT, 8]) for j in range(2)]
            ix8 = [sbb(f"ix8{j}", [TT, 8], u32) for j in range(2)]
            ixf = [sbb(f"ixf{j}", [TT, 2]) for j in range(2)]
            msk = [sbb(f"msk{j}", [TT, 2, E]) for j in range(2)]
            mskb = [sbb(f"mskb{j}", [TT, E], bf16) for j in range(2)]
            dl = [sbb(f"dl{j}", [TT, 1]) for j in range(2)]
            el = [sbb(f"el{j}", [TT, 2]) for j in range(2)]
            s8 = [sbb(f"s8{j}", [TT, 3, E]) for j in range(2)]
            slf = [sbb(f"slf{j}", [TT, 2]) for j in range(2)]
            sli = [sbb(f"sli{j}", [TT, 2], u32) for j in range(2)]
            b1r = sbb("b1r", [P, E * F // P])
            b1hl = sbb("b1hl", [P, 2, E * F // P])
            padrow = sbb("padrow", [P, ROW])
            padid = sbb("padid", [P, 1], i32)
            cntf, cnti = sbb("cntf", [1, E]), sbb("cnti", [1, E], i32)
            tilef = sbb("tilef", [1, E])
            cum = [sbb(f"cum{n}", [1, E]) for n in range(4)]
            tii, tif = sbb("tii", [1, NTILE], i32), sbb("tif", [1, NTILE])
            cmp = sbb("cmp", [1, NTILE, E])
            cmpt = sbb("cmpt", [1, NTILE, E])
            et, before = sbb("et", [1, NTILE]), sbb("before", [1, NTILE])
            used = sbb("used", [1, NTILE])
            rowf = sbb("rowf", [1, NTILE])

            full = [semb(f"full{b}") for b in range(8)]
            free = [semb(f"free{b}") for b in range(8)]
            xs_ready, ones_done, row1_done = semb("xs_ready"), semb("ones_done"), semb("row1_done")
            even_done, scored, sub_done, exp_done = semb("even_done"), semb("scored"), semb("sub_done"), semb("exp_done")
            h2_done, mvb_done, rsb_done, xnb_done = semb("h2_done"), semb("mvb_done"), semb("rsb_done"), semb("xnb_done")
            mask_done, dl_done, el_done = semb("mask_done"), semb("dl_done"), semb("el_done")
            slot_done, row_done = semb("slot_done"), semb("row_done")
            scat = [semb(f"scat{j}") for j in range(2)]
            xr_free = [semb(f"xr_free{j}") for j in range(2)]
            settled = {e.engine: semb(f"settled{n}") for n, e in enumerate((nc.vector, nc.gpsimd))}
            hb_in = [semb(f"hb_in{j}") for j in range(2)]
            acc_w = [semb(f"acc_w{j}") for j in range(2)]
            att_link, tail_link, pool_linkb = semb("att_link"), semb("tail_link"), semb("pool_link_b")
            ld_b1, b1_ready, b1_w, b1_in = semb("ld_b1"), semb("b1_ready"), semb("b1_w"), semb("b1_in")
            iotas, pads, pad_w, link_b = semb("iotas"), semb("pads"), semb("pad_w"), semb("link_b")
            hia_done, hib_done = semb("hia_done"), semb("hib_done")

            def settle(engine):
                engine.sem_inc(settled[engine.engine], 1)

            def head_of(g, n):
                return 2 * n + g if g < 2 else 2 * HB + n

            def heads(t, g):
                return t[:, g:2 * HB:2, :] if g < 2 else t[:, 2 * HB:H, :]

            def turn(i, jobs, k):
                return i * jobs + k

            block = cb.enter_context(nc.Block())

            @block.sync
            def _(sp):
                def load_hb(i, j, rows=TT):
                    sp.wait_ge(h2_done, i * 2 + (j + 1))
                    sp.dma_start(hb[j][0:rows, :], resid_rows[bass.ds(i * W2T + j * TT, rows), :]).then_inc(hb_in[j], 16)

                def store_h2(i, j, rows=TT):
                    sp.wait_ge(h2_done, i * 2 + (j + 3))
                    sp.dma_start(acc[bass.ds(i * W2T + j * TT, rows), :], h2[j][0:rows, :]).then_inc(acc_w[j], 16)

                for j in range(2):
                    sp.sem_inc(acc_w[j], 1)
                for j in range(2):
                    load_hb(0, j)
                sp.dma_start(b1r[:, :], b1.rearrange("e f -> (e f)").rearrange("(p n) -> p n", p=P)).then_inc(ld_b1, 16)
                sp.dma_start(w1a[:, :, :], w1[:, 0:P, :].rearrange("e c f -> c e f")).then_inc(ld_w1, 16)
                sp.dma_start(w1b[0:D1, :, :], w1[:, P:D, :].rearrange("e c f -> c e f")).then_inc(ld_w1, 16)
                sp.dma_start(w1b[D1:P, :, :], w1[:, P:D, :].rearrange("e c f -> c e f")).then_inc(ld_w1, 16)
                sp.wait_ge(b1_ready, 1)
                for n in range(2):
                    sp.dma_start(b1_split[n, :].rearrange("(p n) -> p n", p=P), b1hl[:, n, :]).then_inc(b1_w, 16)
                with sp.Fori(0, NIT - 2) as i:
                    for j in range(2):
                        store_h2(i, j)
                        load_hb(i + 1, j)
                store_h2(NIT - 2, 0)
                load_hb(NIT - 1, 0)
                store_h2(NIT - 2, 1)
                load_hb(NIT - 1, 1, LAST)
                sp.wait_ge(b1_w, 32)
                sp.wait_ge(hib_done, E)
                sp.dma_start(w1b[D1:D1 + 2, :, :].rearrange("a e f -> a (e f)"), b1_split[:, :]).then_inc(b1_in, 16)
                store_h2(NIT - 1, 0)
                store_h2(NIT - 1, 1, LAST)
                sp.wait_ge(pads, 1)
                sp.dma_start(queue[E * REGION:E * REGION + P, :], padrow[:, :]).then_inc(pad_w, 16)
                sp.wait_ge(tables, 1)
                for e in range(E):
                    row = sp.value_load(padtab[0:1, e:e + 1], min_val=e * REGION, max_val=e * REGION + NTOK)
                    sp.dma_start(queue[bass.ds(row, P), :], padrow[:, :]).then_inc(pad_w, 16)
                sp.wait_ge(pad_w, 16 * (E + 1))
                sp.wait_ge(b1_in, 16)
                for j in range(2):
                    sp.wait_ge(acc_w[j], 16 * NIT + 1)

            @block.gpsimd
            def _(pool):
                def copy_tokens(i):
                    nc.gpsimd.tensor_copy(xs0[:, :], xt0[:, bass.ds(i * W2T, W2T)])
                    nc.gpsimd.tensor_copy(xs1[:, :], xt1[:, bass.ds(i * W2T, W2T)]).then_inc(xs_ready, 1)

                def rstd(i, j):
                    pool.wait_ge(mvb_done, i * 2 + (j + 1))
                    settle(pool)
                    nc.gpsimd.tensor_scalar(veb[j][:, :], mvb[j][:, 1:2], EPS, None, ALU.add).then_inc(pool_linkb, 1)
                    pool.wait_ge(pool_linkb, i * 2 + (j + 1))
                    nc.gpsimd.tensor_tensor(rsb[j][:, :], veb[j][:, :], mhalf[0:TT, :], ALU.pow).then_inc(rsb_done, 1)

                def next_tokens(i):
                    pool.wait_ge(full[1], turn(i, PROJ_JOBS, PROJ_JOBS))
                    settle(pool)
                    copy_tokens(i + 1)

                def row_copies(i, j):
                    pool.wait_ge(xnb_done, i * 2 + (j + 1))
                    settle(pool)
                    nc.gpsimd.tensor_copy(xr[j][1][:, 0:D], xr[j][0][:, 0:D])
                    for k in range(2):
                        last = nc.gpsimd.tensor_copy(xr[j][k][:, D + 1:D + 2], idtab[0:TT, bass.ds(i * 2 + j, 1)])
                    last.then_inc(row_done, 1)

                def send_rows(i, j, rows=TT):
                    pool.wait_ge(row_done, i * 2 + (j + 1))
                    pool.wait_ge(slot_done, i * 2 + (j + 1))
                    settle(pool)
                    for k in range(2):
                        nc.gpsimd.indirect_dma_start(
                            out=queue[:, :], out_offset=bass.IndirectOffsetOnAxis(sli[j][0:rows, k:k + 1], 0),
                            in_=xr[j][k][0:rows, :], in_offset=None,
                            bounds_check=(E + 1) * REGION - 1, oob_is_err=True).then_inc(scat[j], 16)

                def rows_left(i):
                    for j in range(2):
                        pool.wait_ge(scat[j], i * 32 + 32)
                        pool.sem_inc(xr_free[j], 1)

                def body(i, tail=True, more=True):
                    if tail:
                        row_copies(i - 1, 0)
                        rstd(i - 1, 1)
                        row_copies(i - 1, 1)
                    if more:
                        next_tokens(i)
                    if tail:
                        for j in range(2):
                            send_rows(i - 1, j)
                    rstd(i, 0)
                    if tail:
                        rows_left(i - 1)

                for j in range(2):
                    pool.memset(vs[j][:, :, :], 1.0).then_inc(ones_done, 1)
                    pool.sem_inc(xr_free[j], 1)
                copy_tokens(0)
                pool.iota(tii[:, :], pattern=[[1, NTILE]], base=0, channel_multiplier=0).then_inc(iotas, 1)
                pool.memset(padrow[:, :], 0.0).then_inc(iotas, 1)
                pool.iota(padid[:, :], pattern=[[0, 1]], base=NTOK, channel_multiplier=1).then_inc(iotas, 1)
                pool.wait_ge(iotas, 3)
                pool.tensor_copy(padrow[:, D + 1:D + 2], padid[:, :]).then_inc(pads, 1)
                body(0, tail=False)
                with pool.Fori(1, NIT - 1) as i:
                    body(i)
                body(NIT - 1, more=False)
                row_copies(NIT - 1, 0)
                rstd(NIT - 1, 1)
                row_copies(NIT - 1, 1)
                send_rows(NIT - 1, 0)
                send_rows(NIT - 1, 1, LAST)
                rows_left(NIT - 1)

            @block.scalar
            def _(act):
                def drain(i, b, jobs, k, dst, src):
                    act.wait_ge(full[b], turn(i, jobs, k))
                    nc.scalar.copy(dst, src).then_inc(free[b], 1)

                def qk_out(i, n):
                    drain(i, n % 2, PROJ_JOBS, n // 2 + 1, qk[:, n, :, :].rearrange("p a t -> p (a t)"),
                          bank[n % 2][:, 0:2 * W2T])

                def v_out(i, j):
                    for b in range(2):
                        drain(i, b, PROJ_JOBS, 4 + j, vs[j][:, b * H // 2:(b + 1) * H // 2, 0:DH],
                              bank[b][0:TT, 0:HD // 2].rearrange("p (h e) -> p h e", e=DH))

                def probs(i, j):
                    act.wait_ge(sub_done, i * 2 + (j + 2))
                    nc.scalar.activation(pr[j][:, :, :], pr[j][:, :, :], ACT.Exp, scale=DH ** -0.5).then_inc(exp_done, 1)

                def pt_out(i, b, k, g):
                    drain(i, b, ROT_JOBS, k, pt[g][:, :, :].rearrange("p h k -> p (h k)"), bank[b][0:TT, 0:HB * TT])

                def zt_out(i, b, k, j, c0, n):
                    drain(i, b, ROT_JOBS, k, zt[j][:, c0:c0 + n, :].rearrange("p c t -> p (c t)"), bank[b][:, 0:n * TT])

                def x2_out(i, k, j):
                    act.wait_ge(full[7], turn(i, TAIL_JOBS, k))
                    nc.scalar.copy(x2t0[j][:, :], bank[7][:, 0:TT])
                    nc.scalar.copy(x2t1[j][0:D1, :], bank[7][0:D1, TT:2 * TT]).then_inc(free[7], 1)

                def gate_exp(i, j):
                    act.wait_ge(dl_done, i * 2 + (j + 1))
                    nc.scalar.activation(el[j][:, 0:1], dl[j][:, :], ACT.Exp).then_inc(el_done, 1)

                def high_b(e):
                    nc.scalar.copy(w1bh[:, e * F:(e + 1) * F], w1b[:, e, :]).then_inc(hib_done, 1)

                def high_a(e):
                    nc.scalar.copy(w1ah[:, e * F:(e + 1) * F], w1a[:, e, :]).then_inc(hia_done, 1)

                def body(i, tail=True, fill=qk_out):
                    if tail:
                        x2_out(i - 1, 1, 0)
                    probs(i, 0)
                    v_out(i, 0)
                    if tail:
                        gate_exp(i - 1, 0)
                    v_out(i, 1)
                    if tail:
                        x2_out(i - 1, 3, 1)
                    pt_out(i, 5, 1, 0)
                    pt_out(i, 6, 1, 1)
                    probs(i, 1)
                    fill(i + 1, 0)
                    pt_out(i, 6, 2, 2)
                    fill(i + 1, 1)
                    fill(i + 1, 2)
                    pt_out(i, 5, 4, 0)
                    pt_out(i, 6, 4, 1)
                    if tail:
                        gate_exp(i - 1, 1)
                    fill(i + 1, 3)
                    zt_out(i, 5, 5, 0, 0, 4)
                    pt_out(i, 5, 6, 2)
                    fill(i + 1, 4)
                    zt_out(i, 6, 6, 0, 4, 2)
                    fill(i + 1, 5)
                    zt_out(i, 6, 8, 1, 0, 4)
                    zt_out(i, 6, 9, 1, 4, 2)

                for b in range(2):
                    act.sem_inc(free[b], 1)
                act.wait_ge(ones_done, 2)
                for n in range(HC):
                    qk_out(0, n)
                body(0, tail=False)
                with act.Fori(1, NIT - 1) as i:
                    body(i)
                act.wait_ge(ld_w1, 48)
                body(NIT - 1, fill=lambda i, n: high_b(n))
                high_b(6)
                high_b(7)
                x2_out(NIT - 1, 1, 0)
                high_a(0)
                x2_out(NIT - 1, 3, 1)
                gate_exp(NIT - 1, 0)
                high_a(1)
                high_a(2)
                gate_exp(NIT - 1, 1)
                for e in range(3, E):
                    high_a(e)

            @block.vector
            def _(dve):
                ATT_LINKS, TAIL_LINKS = 8, 16
                count = {"att": 0, "tail": 0}

                def link_att(i, ins):
                    count["att"] += 1
                    ins.then_inc(att_link, 1)
                    dve.wait_ge(att_link, i * ATT_LINKS + count["att"])

                def link_tail(i, ins):
                    count["tail"] += 1
                    ins.then_inc(tail_link, 1)
                    dve.wait_ge(tail_link, i * TAIL_LINKS + count["tail"])

                def sub_max(i, j):
                    dve.wait_ge(scored, i * 2 + (j + 1))
                    for g in range(NG):
                        sv = bank[2 + g][0:TT, 0:HB * TT].rearrange("q (h k) -> q h k", h=HB)
                        last = nc.vector.reduce_max(mx[j][:, g * HB:(g + 1) * HB], sv, AX.X)
                    link_att(i, last)
                    for g in range(NG):
                        sv = bank[2 + g][0:TT, 0:HB * TT].rearrange("q (h k) -> q h k", h=HB)
                        mb = mx[j][:, g * HB:(g + 1) * HB].rearrange("q (h o) -> q h o", o=1).to_broadcast([TT, HB, TT])
                        last = nc.vector.tensor_tensor(pr[j][:, g * HB:(g + 1) * HB, :], sv, mb, ALU.subtract)
                    last.then_inc(sub_done, 1)

                def z_out(i, b, k, j, g):
                    dve.wait_ge(full[b], turn(i, ROT_JOBS, k))
                    pv = bank[b][0:TT, 0:HB * (DH + 1)].rearrange("q (h e) -> q h e", h=HB)
                    ri = rinv[j][:, g * HB:(g + 1) * HB]
                    link_att(i, nc.vector.reciprocal(ri, pv[:, :, DH]))
                    nc.vector.tensor_tensor(heads(z[j], g), pv[:, :, 0:DH],
                                            ri.rearrange("q (h o) -> q h o", o=1).to_broadcast([TT, HB, DH]),
                                            ALU.mult).then_inc(free[b], 1)

                def o_out(i, b, k, j):
                    dve.wait_ge(full[b], turn(i, ROT_JOBS, k))
                    dve.wait_ge(hb_in[j], (i + 1) * 16)
                    dve.wait_ge(acc_w[j], i * 16 + 1)
                    nc.vector.tensor_tensor(h2[j][:, :], bank[b][0:TT, 0:D], hb[j][:, :], ALU.add).then_inc(free[b], 1)
                    dve.wait_ge(free[b], turn(i, ROT_JOBS, k + 1))
                    nc.vector.bn_stats(stb[j][:, :], h2[j][:, :]).then_inc(h2_done, 1)
                    dve.wait_ge(h2_done, i * 2 + (j + 3))
                    settle(dve)
                    nc.vector.bn_aggr(mvb[j][:, :], stb[j][:, :]).then_inc(mvb_done, 1)

                def norm(i, j):
                    dve.wait_ge(rsb_done, i * 2 + (j + 1))
                    dve.wait_ge(mvb_done, i * 2 + (j + 1))
                    dve.wait_ge(xr_free[j], i + 1)
                    nc.vector.tensor_scalar(xr[j][0][:, 0:D], h2[j][:, :], mvb[j][:, 0:1], rsb[j][:, 0:1],
                                            ALU.subtract, ALU.mult).then_inc(xnb_done, 1)

                def route(i, k, j):
                    dve.wait_ge(full[7], turn(i, TAIL_JOBS, k))
                    nc.vector.tensor_copy(lg[j][:, :], bank[7][0:TT, 0:E]).then_inc(free[7], 1)
                    dve.wait_ge(free[7], turn(i, TAIL_JOBS, k + 1))
                    settle(dve)
                    link_tail(i, nc.vector.max(mx8[j][:, :], lg[j][:, :]))
                    nc.vector.tensor_tensor(dl[j][:, :], mx8[j][:, 1:2], mx8[j][:, 0:1], ALU.subtract).then_inc(dl_done, 1)
                    link_tail(i, nc.vector.max_index(ix8[j][:, :], mx8[j][:, :], lg[j][:, :]))
                    link_tail(i, nc.vector.tensor_copy(ixf[j][:, :], ix8[j][:, 0:2]))
                    for n in range(2):
                        last = nc.vector.tensor_scalar(msk[j][:, n, :], iota8[0:TT, :], ixf[j][:, n:n + 1], None, ALU.is_equal)
                    link_tail(i, last)
                    nc.vector.tensor_tensor(mskb[j][:, :], msk[j][:, 0, :], msk[j][:, 1, :], ALU.add).then_inc(mask_done, 1)

                def slots(i, k, j):
                    dve.wait_ge(full[7], turn(i, TAIL_JOBS, k))
                    link_tail(i, nc.vector.tensor_tensor(s8[j][:, 0, :], bank[7][0:TT, 0:E], slot0[0:TT, :], ALU.add))
                    nc.vector.tensor_tensor(slot0[:, :], bank[7][:, E:2 * E], slot0[:, :], ALU.add).then_inc(free[7], 1)
                    for n in range(2):
                        last = nc.vector.tensor_tensor_reduce(out=s8[j][:, 1 + n, :], in0=msk[j][:, n, :], in1=s8[j][:, 0, :],
                                                              scale=1.0, scalar=0.0, op0=ALU.mult, op1=ALU.add,
                                                              accum_out=slf[j][:, n:n + 1])
                    link_tail(i, last)
                    dve.wait_ge(free[7], turn(i, TAIL_JOBS, k + 1))
                    nc.vector.tensor_copy(sli[j][:, :], slf[j][:, :])

                def weights(i, j):
                    dve.wait_ge(el_done, i * 2 + (j + 1))
                    link_tail(i, nc.vector.tensor_scalar(el[j][:, 1:2], el[j][:, 0:1], 1.0, None, ALU.add))
                    link_tail(i, nc.vector.reciprocal(xr[j][0][:, D:D + 1], el[j][:, 1:2]))
                    nc.vector.tensor_tensor(xr[j][1][:, D:D + 1], el[j][:, 0:1], xr[j][0][:, D:D + 1],
                                            ALU.mult).then_inc(slot_done, 1)

                def low_b(e):
                    dve.wait_ge(hib_done, e + 1)
                    w = w1bl[0:D1, e * F:(e + 1) * F]
                    nc.vector.tensor_tensor(w, w1b[0:D1, e, :], w1bh[0:D1, e * F:(e + 1) * F].bitcast(fp32), ALU.subtract)

                def low_a(e):
                    dve.wait_ge(hia_done, e + 1)
                    w = w1al[:, e * F:(e + 1) * F]
                    nc.vector.tensor_tensor(w, w1a[:, e, :], w1ah[:, e * F:(e + 1) * F].bitcast(fp32), ALU.subtract)

                def body(i, tail=True, low=None):
                    count["att"] = count["tail"] = 0
                    if tail:
                        norm(i - 1, 0)
                    sub_max(i, 0)
                    if tail:
                        o_out(i - 1, 5, 9, 1)
                        route(i - 1, 2, 0)
                        norm(i - 1, 1)
                    sub_max(i, 1)
                    if tail:
                        route(i - 1, 4, 1)
                    z_out(i, 5, 2, 0, 0)
                    z_out(i, 5, 3, 0, 1)
                    if tail:
                        slots(i - 1, 5, 0)
                    z_out(i, 6, 3, 0, 2)
                    if tail:
                        slots(i - 1, 6, 1)
                        weights(i - 1, 0)
                        weights(i - 1, 1)
                        assert count["tail"] == TAIL_LINKS
                    if low:
                        low(0)
                        low(1)
                    z_out(i, 6, 5, 1, 0)
                    if low:
                        low(2)
                    z_out(i, 5, 7, 1, 1)
                    z_out(i, 6, 7, 1, 2)
                    if low:
                        low(3)
                    o_out(i, 5, 8, 0)
                    assert count["att"] == ATT_LINKS

                def link(ins):
                    count["tables"] += 1
                    ins.then_inc(link_b, 1)
                    dve.wait_ge(link_b, count["tables"])

                def tables_out():
                    link(nc.vector.tensor_scalar(cntf[:, :], iota8[0:1, :], -float(REGION), float(P - 1), ALU.mult, ALU.add))
                    link(nc.vector.tensor_tensor(cntf[:, :], cntf[:, :], slot0[0:1, :], ALU.add))
                    link(nc.vector.tensor_copy(cnti[:, :], cntf[:, :]))
                    link(nc.vector.tensor_scalar(cnti[:, :], cnti[:, :], 7, None, ALU.arith_shift_right))
                    link(nc.vector.tensor_copy(tilef[:, :], cnti[:, :]))
                    link(nc.vector.tensor_copy(cum[0][:, :], tilef[:, :]))
                    for n in range(3):
                        d = 1 << n
                        nc.vector.tensor_copy(cum[n + 1][:, 0:d], cum[n][:, 0:d])
                        link(nc.vector.tensor_tensor(cum[n + 1][:, d:E], cum[n][:, d:E], cum[n][:, 0:E - d], ALU.add))
                    link(nc.vector.tensor_tensor(cmp[:, :, :], tif[:, :].rearrange("a (t o) -> a t o", o=1).to_broadcast([1, NTILE, E]),
                                                 cum[3][:, :].rearrange("a (o e) -> a o e", o=1).to_broadcast([1, NTILE, E]), ALU.is_ge))
                    link(nc.vector.tensor_tensor(cmpt[:, :, :], cmp[:, :, :],
                                                 tilef[:, :].rearrange("a (o e) -> a o e", o=1).to_broadcast([1, NTILE, E]), ALU.mult))
                    nc.vector.reduce_sum(et[:, :], cmp[:, :, :], AX.X)
                    link(nc.vector.reduce_sum(before[:, :], cmpt[:, :, :], AX.X))
                    nc.vector.tensor_scalar(used[:, :], et[:, :], float(E), float(P), ALU.is_lt, ALU.mult)
                    link(nc.vector.tensor_tensor(rowf[:, :], tif[:, :], before[:, :], ALU.subtract))
                    link(nc.vector.tensor_tensor(rowf[:, :], rowf[:, :], used[:, :], ALU.mult))
                    link(nc.vector.scalar_tensor_tensor(rowf[:, :], et[:, :], float(REGION), rowf[:, :], ALU.mult, ALU.add))
                    nc.vector.tensor_copy(rowtab[:, :], rowf[:, :])
                    link(nc.vector.tensor_scalar(before[:, :], et[:, :], float(E - 1), None, ALU.min))
                    nc.vector.tensor_copy(exptab[:, :], before[:, :]).then_inc(tables, 1)

                for j in range(2):
                    nc.vector.memset(x2t1[j][D1:D1 + 1, :], 1.0).then_inc(row1_done, 1)
                count["tables"] = 0
                dve.sem_inc(sub_done, 1)
                dve.sem_inc(h2_done, 2)
                for b in (5, 6, 7):
                    dve.sem_inc(free[b], 1)
                dve.wait_ge(ld_b1, 16)
                link(nc.vector.tensor_copy(b1hl[:, 0, :].bitcast(fp32r), b1r[:, :]))
                nc.vector.tensor_tensor(b1hl[:, 1, :].bitcast(fp32r), b1r[:, :], b1hl[:, 0, :], ALU.subtract).then_inc(b1_ready, 1)
                dve.wait_ge(iotas, 1)
                nc.vector.tensor_copy(tif[:, :], tii[:, :])
                body(0, tail=False)
                with dve.Fori(1, NIT - 1) as i:
                    body(i)
                body(NIT - 1, low=low_b)
                last_tail = NIT - 1
                count["tail"] = 0
                norm(last_tail, 0)
                low_b(4)
                o_out(last_tail, 5, 9, 1)
                route(last_tail, 2, 0)
                norm(last_tail, 1)
                low_b(5)
                route(last_tail, 4, 1)
                slots(last_tail, 5, 0)
                slots(last_tail, 6, 1)
                nc.vector.tensor_copy(padtab[:, :], slot0[0:1, :]).then_inc(tables, 1)
                weights(last_tail, 0)
                weights(last_tail, 1)
                tables_out()
                low_b(6)
                low_b(7)
                for e in range(E):
                    low_a(e)

            @block.tensor
            def _(pe):
                mm = nc.tensor.matmul

                def start(i, b, jobs, k):
                    pe.wait_ge(free[b], turn(i, jobs, k))

                def qk_proj(i, c):
                    b, k = c % 2, c // 2 + 1
                    start(i, b, PROJ_JOBS, k)
                    for n in range(2):
                        o = bank[b][:, n * W2T:(n + 1) * W2T]
                        mm(o, wqk0[:, n, c * P:(c + 1) * P], xt0[:, bass.ds(i * W2T, W2T)], start=True, stop=False)
                        last = mm(o, wqk1[:, n, c * P:(c + 1) * P], xt1[:, bass.ds(i * W2T, W2T)], start=False, stop=True)
                    last.then_inc(full[b], 1)

                def v_proj(i, j):
                    for b in range(2):
                        start(i, b, PROJ_JOBS, 4 + j)
                        o = bank[b][0:TT, 0:HD // 2]
                        cols = slice(b * HD // 2, (b + 1) * HD // 2)
                        mm(o, xs0[:, j * TT:(j + 1) * TT], wv0[:, cols], start=True, stop=False)
                        mm(o, xs1[:, j * TT:(j + 1) * TT], wv1[:, cols], start=False, stop=True).then_inc(full[b], 1)

                def scores(i, j):
                    pe.wait_ge(sub_done, i * 2 + (j + 1))
                    for g in range(NG):
                        mm(bank[2 + g][0:TT, 0:HB * TT], identb[:, :], mask[:, :], start=True, stop=True)

                    def head(g, n):
                        h = head_of(g, n)
                        rows = slice(DH * (h % 2), DH * (h % 2 + 1))
                        q = qk[rows, h // 2, 0, j * TT:(j + 1) * TT]
                        k = qk[rows, h // 2, 1, j * TT:(j + 1) * TT]
                        return mm(bank[2 + g][0:TT, n * TT:(n + 1) * TT], q, k, start=False, stop=True,
                                  skip_group_check=True)

                    head(2, 0)
                    head(2, 2).then_inc(even_done, 1)
                    for n in range(HB):
                        head(0, n)
                    pe.wait_ge(even_done, i * 2 + (j + 1))
                    head(2, 1)
                    head(2, 3)
                    for n in range(HB):
                        last = head(1, n)
                    last.then_inc(scored, 1)

                def pt_job(i, b, k, j, g):
                    pe.wait_ge(exp_done, i * 2 + (j + 1))
                    start(i, b, ROT_JOBS, k)
                    for n in range(HB):
                        last = nc.tensor.transpose(bank[b][0:TT, n * TT:(n + 1) * TT], pr[j][:, g * HB + n, :], ident[0:TT, 0:TT])
                    last.then_inc(full[b], 1)

                def pv_job(i, b, k, j, g, pt_bank, pt_turn):
                    pe.wait_ge(free[pt_bank], turn(i, ROT_JOBS, pt_turn + 1))
                    start(i, b, ROT_JOBS, k)
                    for n in range(HB):
                        last = mm(bank[b][0:TT, n * (DH + 1):(n + 1) * (DH + 1)], pt[g][:, n, :], vs[j][:, head_of(g, n), :],
                                  start=True, stop=True)
                    last.then_inc(full[b], 1)

                def zt_job(i, b, k, j, c0, n, z_turns):
                    for zb, zk in z_turns:
                        pe.wait_ge(free[zb], turn(i, ROT_JOBS, zk + 1))
                    start(i, b, ROT_JOBS, k)
                    zv = z[j][:, :, :].rearrange("q h e -> q (h e)")
                    for m in range(n):
                        last = nc.tensor.transpose(bank[b][:, m * TT:(m + 1) * TT], zv[:, (c0 + m) * P:(c0 + m + 1) * P],
                                                   ident[0:TT, 0:TT])
                    last.then_inc(full[b], 1)

                def o_job(i, b, k, j, zt_turns):
                    for zb, zk in zt_turns:
                        pe.wait_ge(free[zb], turn(i, ROT_JOBS, zk + 1))
                    start(i, b, ROT_JOBS, k)
                    for c in range(HC):
                        last = mm(bank[b][0:TT, 0:D], zt[j][:, c, :], wo[:, c, :], start=(c == 0), stop=(c == HC - 1))
                    last.then_inc(full[b], 1)

                def x2_job(i, k, j):
                    pe.wait_ge(xnb_done, i * 2 + (j + 1))
                    start(i, 7, TAIL_JOBS, k)
                    nc.tensor.transpose(bank[7][:, 0:TT], xr[j][0][:, 0:P], ident[0:TT, 0:TT])
                    nc.tensor.transpose(bank[7][0:D1, TT:2 * TT], xr[j][0][:, P:D], ident[0:TT, 0:TT]).then_inc(full[7], 1)

                def gate_job(i, k, j):
                    start(i, 7, TAIL_JOBS, k)
                    mm(bank[7][0:TT, 0:E], x2t0[j][:, :], gw0[:, :], start=True, stop=False)
                    mm(bank[7][0:TT, 0:E], x2t1[j][:, :], gw1[:, :], start=False, stop=True).then_inc(full[7], 1)

                def rank_job(i, k, j, rows=TT):
                    pe.wait_ge(mask_done, i * 2 + (j + 1))
                    start(i, 7, TAIL_JOBS, k)
                    mm(bank[7][0:TT, 0:E], tri[0:rows, :], mskb[j][0:rows, :], start=True, stop=True)
                    mm(bank[7][:, E:2 * E], onesb[0:rows, :], mskb[j][0:rows, :], start=True, stop=True).then_inc(full[7], 1)

                def body(i, tail=True, more=True):
                    pe.wait_ge(free[0], turn(i, PROJ_JOBS, 4))
                    pe.wait_ge(free[1], turn(i, PROJ_JOBS, 4))
                    scores(i, 0)
                    if tail:
                        x2_job(i - 1, 1, 0)
                        o_job(i - 1, 5, 9, 1, [(6, 8), (6, 9)])
                    pe.wait_ge(xs_ready, i + 1)
                    v_proj(i, 0)
                    if tail:
                        gate_job(i - 1, 2, 0)
                    scores(i, 1)
                    v_proj(i, 1)
                    if tail:
                        x2_job(i - 1, 3, 1)
                    pt_job(i, 5, 1, 0, 0)
                    pt_job(i, 6, 1, 0, 1)
                    if more:
                        qk_proj(i + 1, 0)
                    if tail:
                        gate_job(i - 1, 4, 1)
                    pe.wait_ge(free[0], turn(i, PROJ_JOBS, 5))
                    pe.wait_ge(free[1], turn(i, PROJ_JOBS, 5))
                    pv_job(i, 5, 2, 0, 0, 5, 1)
                    pt_job(i, 6, 2, 0, 2)
                    if more:
                        qk_proj(i + 1, 1)
                    pv_job(i, 5, 3, 0, 1, 6, 1)
                    if tail:
                        rank_job(i - 1, 5, 0)
                    pv_job(i, 6, 3, 0, 2, 6, 2)
                    if more:
                        qk_proj(i + 1, 2)
                    pt_job(i, 5, 4, 1, 0)
                    pt_job(i, 6, 4, 1, 1)
                    if more:
                        qk_proj(i + 1, 3)
                    if tail:
                        rank_job(i - 1, 6, 1)
                    zt_job(i, 5, 5, 0, 0, 4, [(5, 2), (5, 3)])
                    pe.wait_ge(free[0], turn(i, PROJ_JOBS, 6))
                    pe.wait_ge(free[1], turn(i, PROJ_JOBS, 6))
                    pv_job(i, 6, 5, 1, 0, 5, 4)
                    pt_job(i, 5, 6, 1, 2)
                    if more:
                        qk_proj(i + 1, 4)
                    zt_job(i, 6, 6, 0, 4, 2, [(6, 3)])
                    pv_job(i, 5, 7, 1, 1, 6, 4)
                    pv_job(i, 6, 7, 1, 2, 5, 6)
                    if more:
                        qk_proj(i + 1, 5)
                    zt_job(i, 6, 8, 1, 0, 4, [(6, 5), (5, 7)])
                    o_job(i, 5, 8, 0, [(5, 5), (6, 6)])
                    zt_job(i, 6, 9, 1, 4, 2, [(6, 7)])

                pe.wait_ge(ld_w, 16 * N_W)
                pe.wait_ge(ld_small, 16 * 4)
                pe.wait_ge(ones_done, 2)
                pe.wait_ge(row1_done, 2)
                for c in range(HC):
                    qk_proj(0, c)
                body(0, tail=False)
                with pe.Fori(1, NIT - 1) as i:
                    body(i)
                body(NIT - 1, more=False)
                last_tail = NIT - 1
                x2_job(last_tail, 1, 0)
                o_job(last_tail, 5, 9, 1, [(6, 8), (6, 9)])
                gate_job(last_tail, 2, 0)
                x2_job(last_tail, 3, 1)
                gate_job(last_tail, 4, 1)
                rank_job(last_tail, 5, 0)
                rank_job(last_tail, 6, 1, LAST)

        with ExitStack() as cc:
            def sbc(name, shape, dt=fp32):
                return cc.enter_context(nc.sbuf_tensor(name, shape, dt))

            def semc(name):
                return cc.enter_context(nc.semaphore(name))

            xq = [sbc(f"xq{u}", [P, ROW]) for u in range(U)]
            idx = [sbc(f"idx{u}", [P, 1], u32) for u in range(U)]
            xh0 = [sbc(f"xh0{u}", [P, P], fp32r) for u in range(2)]
            xl0 = [sbc(f"xl0{u}", [P, P], fp32r) for u in range(2)]
            xhl = [sbc(f"xhl{u}", [P, P], fp32r) for u in range(2)]
            xh1 = [sbc(f"xh1{u}", [D1 + 2, P], fp32r) for u in range(2)]
            hid = sbc("hid", [P, F])
            hidt = sbc("hidt", [P, KH, P])
            ysum = [sbc(f"ysum{u}", [P, D]) for u in range(2)]
            yout = [sbc(f"yout{u}", [P, D]) for u in range(U)]

            settled = semc("settled_c")
            link_c = semc("link_c")
            xq_in = [semc(f"xq_in{u}") for u in range(U)]
            xt_full, xt_ready = semc("xt_full"), semc("xt_ready")
            h_full, gelu_done = semc("h_full"), semc("gelu_done")
            ht_full, ht_dve, ht_act = semc("ht_full"), semc("ht_dve"), semc("ht_act")
            y_full, y_added, y_scaled = semc("y_full"), semc("y_added"), semc("y_scaled")
            sent = [semc(f"sent{u}") for u in range(U)]
            added = semc("added")
            out_w = semc("out_w")

            NLOOP = NTILE // U
            block = cc.enter_context(nc.Block())

            @block.sync
            def _(sp):
                def load_rows(t, u):
                    row = sp.value_load(rowtab[0:1, bass.ds(t, 1)], min_val=0, max_val=E * REGION)
                    sp.dma_start(xq[u][:, :], queue[bass.ds(row, P), :]).then_inc(xq_in[u], 16)

                for u in range(U):
                    load_rows(u, u)
                with sp.Fori(0, NLOOP - 1) as i:
                    for u in range(U):
                        sp.wait_ge(y_scaled, i * U + (u + 3))
                        load_rows((i + 1) * U + u, u)
                sp.wait_ge(added, NTILE + U)
                sp.dma_start(out.rearrange("b t d -> (b t) d"), acc[0:NTOK, :]).then_inc(out_w, 16)
                sp.wait_ge(out_w, 16)

            @block.gpsimd
            def _(pool):
                pool.sem_inc(added, U)
                with pool.Fori(0, NLOOP) as i:
                    for u in range(U):
                        pool.wait_ge(y_scaled, i * U + (u + 3))
                        pool.sem_inc(settled, 1)
                        nc.gpsimd.indirect_dma_start(
                            out=acc[:, :], out_offset=bass.IndirectOffsetOnAxis(idx[u][:, :], 0),
                            in_=yout[u][:, :], in_offset=None, bounds_check=NTOK + P - 1, oob_is_err=True,
                            compute_op=ALU.add).then_inc(sent[u], 16)
                        pool.wait_ge(sent[u], i * 16 + 16)
                        pool.sem_inc(added, 1)

            @block.scalar
            def _(act):
                def step(i, u):
                    t = i * U + u
                    act.wait_ge(h_full, t + 1)
                    for n in range(2):
                        last = nc.scalar.activation(hid[:, n * F // 2:(n + 1) * F // 2],
                                                    bank[1 + 2 * (u % 2) + n][:, 0:F // 2], ACT.Gelu)
                    last.then_inc(gelu_done, 1)

                def rest(i, u):
                    t = i * U + u
                    act.wait_ge(ht_full, t * 2 + 2)
                    nc.scalar.copy(hidt[:, 4:KH, :], bank[6][:, 0:(KH - 4) * P]).then_inc(ht_act, 1)

                def scale(i, u):
                    t = i * U + u
                    act.wait_ge(y_added, t + 2)
                    act.wait_ge(added, t + 1)
                    nc.scalar.activation(yout[u][:, :], ysum[u % 2][:, :], ACT.Copy,
                                         scale=xq[u][:, D:D + 1]).then_inc(y_scaled, 1)

                act.sem_inc(gelu_done, 1)
                act.sem_inc(y_scaled, 2)
                step(0, 0)

                def body(i, more=True):
                    for u in range(U):
                        rest(i, u)
                        if u < U - 1:
                            step(i, u + 1)
                        elif more:
                            step(i + 1, 0)
                        scale(i, u)

                with act.Fori(0, NLOOP - 1) as i:
                    body(i)
                body(NLOOP - 1, more=False)

            @block.vector
            def _(dve):
                LINKS = 2

                def rows_in(i, u):
                    t = i * U + u
                    v = u % 2
                    dve.wait_ge(xt_full, t + 1)
                    nc.vector.tensor_copy(xh0[v][:, :], bank[0][:, 0:P])
                    nc.vector.tensor_copy(xh1[v][0:D1, :], bank[0][0:D1, P:2 * P]).then_inc(link_c, 1)
                    nc.vector.tensor_copy(xhl[v][0:D1, :], bank[0][0:D1, P:2 * P]).then_inc(link_c, 1)
                    dve.wait_ge(link_c, t * LINKS + 2)
                    nc.vector.tensor_tensor(xl0[v][:, :], bank[0][:, 0:P], xh0[v][:, :].bitcast(fp32), ALU.subtract)
                    nc.vector.tensor_tensor(xhl[v][D1:P, :], bank[0][0:D1, P:2 * P], xh1[v][0:D1, :].bitcast(fp32),
                                            ALU.subtract).then_inc(xt_ready, 1)
                    dve.wait_ge(xq_in[u], i * 16 + 16)
                    dve.wait_ge(added, t + 1)
                    nc.vector.tensor_copy(idx[u][:, :], xq[u][:, D + 1:D + 2])

                def rest(i, u):
                    t = i * U + u
                    dve.wait_ge(ht_full, t * 2 + 1)
                    nc.vector.tensor_copy(hidt[:, 0:4, :], bank[5][:, 0:4 * P]).then_inc(ht_dve, 1)

                def add_bias(i, u):
                    t = i * U + u
                    e = dve.value_load(exptab[0:1, bass.ds(t, 1)], min_val=0, max_val=E - 1)
                    dve.wait_ge(y_full, t + 1)
                    dve.wait_ge(y_scaled, t + 1)
                    nc.vector.tensor_tensor(ysum[u % 2][:, :], bank[7][:, 0:D],
                                            b2s[:, :, :].rearrange("p e d -> p (e d)")[:, bass.ds(e * D, D)],
                                            ALU.add).then_inc(y_added, 1)

                for v in range(2):
                    nc.vector.memset(xh1[v][D1:D1 + 2, :].bitcast(fp32), 1.0)
                dve.sem_inc(y_added, 1)
                dve.sem_inc(xt_ready, 1)
                rows_in(0, 0)
                rows_in(0, 1)

                def body(i, more=True):
                    for u in range(U):
                        rest(i, u)
                        if u < U - 2:
                            rows_in(i, u + 2)
                        elif more:
                            rows_in(i + 1, u + 2 - U)
                        add_bias(i, u)

                with dve.Fori(0, NLOOP - 1) as i:
                    body(i)
                body(NLOOP - 1, more=False)

            @block.tensor
            def _(pe):
                mm = nc.tensor.matmul
                w2_f = w2s.rearrange("p e k d -> p (e k d)")

                def transpose_rows(i, u):
                    t = i * U + u
                    pe.wait_ge(xq_in[u], i * 16 + 16)
                    pe.wait_ge(xt_ready, t + 1)
                    nc.tensor.transpose(bank[0][:, 0:P], xq[u][:, 0:P], ident[:, :])
                    nc.tensor.transpose(bank[0][0:D1, P:2 * P], xq[u][:, P:D], ident[:, :]).then_inc(xt_full, 1)

                def up(i, u, e):
                    t = i * U + u
                    v = u % 2
                    pe.wait_ge(xt_ready, t + 2)
                    for n in range(2):
                        o = bank[1 + 2 * (u % 2) + n][:, 0:F // 2]
                        cols = bass.ds(e * F + n * F // 2, F // 2)
                        mm(o, xh0[v][:, :], w1ah[:, cols], start=True, stop=False)
                        mm(o, xh0[v][:, :], w1al[:, cols], start=False, stop=False)
                        mm(o, xl0[v][:, :], w1ah[:, cols], start=False, stop=False)
                        mm(o, xhl[v][:, :], w1bh[:, cols], start=False, stop=False)
                        last = mm(o, xh1[v][:, :], w1bl[:, cols], start=False, stop=True)
                    last.then_inc(h_full, 1)

                def transpose_hidden(i, u):
                    t = i * U + u
                    pe.wait_ge(gelu_done, t + 2)
                    for k in range(KH):
                        last = nc.tensor.transpose(bank[5 + k // 4][:, (k % 4) * P:(k % 4 + 1) * P],
                                                   hid[:, k * P:(k + 1) * P], ident[:, :])
                        if k in (3, KH - 1):
                            last.then_inc(ht_full, 1)

                def down(i, u, e):
                    t = i * U + u
                    pe.wait_ge(ht_dve, t + 1)
                    pe.wait_ge(ht_act, t + 1)
                    pe.wait_ge(y_added, t + 1)
                    for k in range(KH):
                        last = mm(bank[7][:, 0:D], hidt[:, k, :], w2_f[:, bass.ds(e * (KH * D) + k * D, D)],
                                  start=(k == 0), stop=(k == KH - 1))
                    last.then_inc(y_full, 1)

                def expert(t):
                    return pe.value_load(exptab[0:1, bass.ds(t, 1)], min_val=0, max_val=E - 1)

                def body(i, more=True):
                    for u in range(U):
                        transpose_hidden(i, u)
                        if u < U - 2:
                            transpose_rows(i, u + 2)
                        elif more:
                            transpose_rows(i + 1, u + 2 - U)
                        if u < U - 1:
                            up(i, u + 1, expert(i * U + u + 1))
                        elif more:
                            up(i + 1, 0, expert((i + 1) * U))
                        down(i, u, expert(i * U + u))

                pe.wait_ge(ld_w2, 16)
                transpose_rows(0, 0)
                transpose_rows(0, 1)
                up(0, 0, expert(0))
                with pe.Fori(0, NLOOP - 1) as i:
                    body(i)
                body(NLOOP - 1, more=False)


_INS = ["x", "cls_tok", "L0_tok_W", "L0_tok_b", "L0_attn_W_Q", "L0_attn_b_Q", "L0_attn_W_K", "L0_attn_b_K",
        "L0_attn_W_V", "L0_attn_b_V", "L0_attn_W_O", "L0_attn_b_O", "L0_ffn_gate_w", "L0_ffn_gate_b",
        "L0_ffn_w1", "L0_ffn_b1", "L0_ffn_w2", "L0_ffn_b2"]


def kernel(**inputs):
    import numpy as np
    import concourse.bacc as bacc
    from concourse.bass_utils import run_bass_kernel_spmd

    nc = bacc.Bacc("TRN2", target_bir_lowering=False, num_devices=1)
    arrays, args = {}, []
    for name in _INS:
        a = np.ascontiguousarray(inputs[name])
        arrays[f"in_{name}"] = a
        args.append(nc.dram_tensor(f"in_{name}", a.shape, mybir.dt.from_np(a.dtype), kind="ExternalInput").ap())
    batch, channels, side, _ = inputs["x"].shape
    tokens = (side // 16) ** 2 + 1
    out = nc.dram_tensor("out_0", [batch, tokens, inputs["L0_tok_W"].shape[0]], mybir.dt.float32, kind="ExternalOutput").ap()
    vit_tower_kernel(nc, *args, out)
    r = run_bass_kernel_spmd(nc, [arrays], core_ids=[0])
    return r.results[0]["out_0"]
```

```python
import concourse.bass as bass
from concourse import mybir
from contextlib import ExitStack


def vit_tower_kernel(nc, x, cls_tok, tok_w, tok_b, w_q, b_q, w_k, b_k, w_v, b_v, w_o, b_o,
                     gate_w, gate_b, w1, b1, w2, b2, out):
    fp32, bf16 = mybir.dt.float32, mybir.dt.bfloat16
    fp32r = mybir.dt.float32r
    i32, u32 = mybir.dt.int32, mybir.dt.uint32
    ALU = mybir.AluOpType
    ACT = mybir.ActivationFunctionType
    AX = mybir.AxisListType

    P = 128
    NI, C, IMG, _ = x.shape
    D, F_IN = tok_w.shape
    KER = 16
    STEP = IMG // KER
    T = STEP * STEP + 1
    H, _, DH = w_q.shape
    HD = H * DH
    E, _, F = w1.shape
    D1 = D - P
    KF = F_IN // P
    ROWS_A = P // NI
    GROUPS = STEP // ROWS_A
    TILES_A = GROUPS * STEP
    G3 = 3
    TT = G3 * T
    NT = -(-NI // G3)
    NIT = NT // 2
    NTOK = NI * T
    NPAD = NT * TT
    LAST = NTOK - (NT - 1) * TT
    HC = H // 2
    HB = 4
    NG = H // HB
    KH = F // P
    W2T = 2 * TT
    ROW = D + 2
    REGION = NTOK + P
    NTILE = (2 * NTOK - E) // P + E
    U = 4
    EPS = 1e-5
    CAUSAL = -1e5 * DH ** 0.5
    FAR = -1e30
    assert NTILE % U == 0 and NT % 2 == 0 and ROWS_A * NI == P

    resid = nc.dram_tensor("resid", [NI, T, D], fp32).ap()
    resid_rows = resid.rearrange("b t d -> (b t) d")
    acc = out
    bqkv_split = nc.dram_tensor("bqkv_split", [2, 3 * HD], fp32).ap()
    b1_split = nc.dram_tensor("b1_split", [2, E * F], fp32).ap()
    queue = nc.dram_tensor("queue", [(E + 1) * REGION, ROW], fp32).ap()

    ctx = ExitStack()
    with ctx:
        def sb(name, shape, dt=fp32):
            return ctx.enter_context(nc.sbuf_tensor(name, shape, dt))

        def sem(name):
            return ctx.enter_context(nc.semaphore(name))

        bank = [ctx.enter_context(nc.psum_tensor(f"bank{i}", [P, 512], fp32)) for i in range(8)]

        ident = sb("ident", [P, P])
        identb = sb("identb", [TT, TT], bf16)
        mask = sb("mask", [TT, HB * TT], bf16)
        tri = sb("tri", [TT, TT], bf16)
        onesb = sb("onesb", [TT, P], bf16)
        mhalf = sb("mhalf", [P, 1])
        iota8 = sb("iota8", [P, E])
        idtab = sb("idtab", [P, NT])
        tokens = sb("tokens", [P, 2 * E * F])
        XHI, XLO, XHL, XH1 = range(4)
        xparts = tokens[:, 0:4 * NPAD].rearrange("p (n t) -> p n t", n=4)
        xp = tokens[:, :].bitcast(fp32r)[:, 0:4 * NPAD].rearrange("p (n t) -> p n t", n=4)
        w1ah = tokens[:, :].bitcast(fp32r)[:, 0:E * F]
        w1bh = tokens[:, :].bitcast(fp32r)[:, E * F:2 * E * F]
        assert 4 * NPAD <= 2 * E * F
        wo = sb("wo", [P, HC, D])
        gw0, gw1 = sb("gw0", [P, E]), sb("gw1", [D1 + 1, E])
        w1s = sb("w1s", [P, 2 * E * F])
        xin = [w1s[:, g * C * KER * IMG:(g + 1) * C * KER * IMG] for g in range(2)]
        XE = 2 * C * KER * IMG
        wtok = w1s[:, XE:XE + KF * D].rearrange("p (k d) -> p k d", k=KF)
        tokb, bo = (w1s[:, XE + KF * D + n * D:XE + KF * D + (n + 1) * D] for n in range(2))
        w1a = w1s[:, 0:E * F].rearrange("p (e f) -> p e f", e=E)
        w1b = w1s[:, E * F:2 * E * F].rearrange("p (e f) -> p e f", e=E)
        w1al = w1s[:, :].bitcast(fp32r)[:, 0:E * F]
        w1bl = w1s[:, :].bitcast(fp32r)[0:D1 + 2, E * F:2 * E * F]
        assert XE + KF * D + 2 * D <= 2 * E * F
        WHI, WLO, WHH, WL1 = range(4)
        with nc.sbuf_tensor("wp", [P, 4, 3 * HD], fp32r) as wp:
            pass
        w2s = sb("w2s", [P, E, KH, D])
        assert 4 * 3 * HD <= E * KH * D
        b2s = sb("b2s", [P, E, D])
        slot0 = sb("slot0", [P, E])
        xq = [sb(f"xq{u}", [P, ROW]) for u in range(U)]
        rowtab, exptab = sb("rowtab", [1, NTILE], i32), sb("exptab", [1, NTILE], i32)
        padtab = sb("padtab", [1, E], i32)

        ld_tokw, ld_small, ld_cls = sem("ld_tokw"), sem("ld_small"), sem("ld_cls")
        ld_bias, tables = sem("ld_bias"), sem("tables")
        ld_w, ld_w1, ld_w2 = sem("ld_w"), sem("ld_w1"), sem("ld_w2")
        w_acc0 = sem("w_acc0")
        const_pool, const_dve = sem("const_pool"), sem("const_dve")

        N_W = 10
        xq_in = [sem(f"xq_in{u}") for u in range(U)]

        with ExitStack() as ca:
            def sba(name, shape, dt=fp32):
                return ca.enter_context(nc.sbuf_tensor(name, shape, dt))

            def sema(name):
                return ca.enter_context(nc.semaphore(name))

            wraw0, wraw1 = sba("wraw0", [P, F_IN]), sba("wraw1", [D1, F_IN])
            pxt = [sba(f"pxt{i}", [P, KF, P]) for i in range(2)]
            xc = [sba(f"xc{i}", [P, F_IN]) for i in range(2)]
            wraw = sba("wraw", [P, 2, 3 * HD])
            maskf = sba("maskf", [TT, HB * TT])
            trif = sba("trif", [TT, TT])
            BW = 3 * HD // 96
            braw = sba("braw", [96, BW])
            bhl = sba("bhl", [96, 2, BW])
            hraw = [sba(f"hraw{i}", [P, D]) for i in range(2)]
            xn = [sba(f"xn{i}", [P, D]) for i in range(2)]
            hbo = [sba(f"hbo{i}", [P, STEP, D]) for i in range(2)]
            st = [sba(f"st{i}", [P, 6]) for i in range(3)]
            mv = [sba(f"mv{i}", [P, 2]) for i in range(3)]
            ve = [sba(f"ve{i}", [P, 1]) for i in range(3)]
            rs = [sba(f"rs{i}", [P, 1]) for i in range(3)]
            clsr = sba("clsr", [NI, D])
            clsn = sba("clsn", [NI, D])
            clsbo = sba("clsbo", [NI, D])
            iotai = sba("iotai", [P, E], i32)
            idtabi = sba("idtabi", [P, NT], i32)
            zrow = sba("zrow", [P, D])

            ld_bqkv, bhl_done, bhl_w, bhl_in = sema("ld_bqkv"), sema("bhl_done"), sema("bhl_w"), sema("bhl_in")
            whi_done, xt_low = sema("whi_done"), sema("xt_low")
            x_in = [sema(f"x_in{i}") for i in range(2)]
            xc_done = sema("xc_done")
            wt_full, wt_out = sema("wt_full"), sema("wt_out")
            tr_done, emb_done, lt_done = sema("tr_done"), sema("emb_done"), sema("lt_done")
            px_act, px_dve = sema("px_act"), sema("px_dve")
            h_done, mv_done, rs_done, xn_done = sema("h_done"), sema("mv_done"), sema("rs_done"), sema("xn_done")
            xt_out, hbo_done, dve_link, pool_link = sema("xt_out"), sema("hbo_done"), sema("dve_link_a"), sema("pool_link_a")
            resid_w = [sema(f"resid_w{i}") for i in range(2)]
            cls_w, cls_mv, cls_rs, cls_xn, cls_full, cls_bo = (sema("cls_w"), sema("cls_mv"), sema("cls_rs"),
                                                               sema("cls_xn"), sema("cls_full"), sema("cls_bo"))

            def columns(n, part, row0, row1):
                g, pj = divmod(n, STEP)
                t0 = 1 + g * ROWS_A * STEP + pj
                dst = xp[row0:row1, part, 0:NTOK].rearrange("c (b t) -> c b t", t=T)
                return dst[:, :, t0:t0 + STEP + 1:STEP].rearrange("c b r -> c r b")

            block = ca.enter_context(nc.Block())

            @block.sync
            def _(sp):
                def load_images(g):
                    for r in range(ROWS_A):
                        row0 = (g * ROWS_A + r) * KER
                        sp.dma_start(xin[g % 2][r * NI:(r + 1) * NI, :].rearrange("b (c n) -> b c n", c=C),
                                     x[:, :, row0:row0 + KER, :].rearrange("b c i w -> b c (i w)")
                                     ).then_inc(x_in[g % 2], 16)

                sp.dma_start(wraw0[:, :], tok_w[0:P, :]).then_inc(ld_tokw, 16)
                sp.dma_start(wraw1[:, :], tok_w[P:D, :]).then_inc(ld_tokw, 16)
                load_images(0)
                sp.dma_start(clsr[:, :], cls_tok.rearrange("a b d -> (a b) d").partition_broadcast(NI)).then_inc(ld_cls, 16)
                sp.dma_start(tokb[:, :], tok_b.rearrange("(a d) -> a d", a=1).partition_broadcast(P)).then_inc(ld_bias, 16)
                sp.dma_start(bo[:, :], b_o.rearrange("(a d) -> a d", a=1).partition_broadcast(P)).then_inc(ld_bias, 16)
                load_images(1)
                for n, b in enumerate((b_q, b_k, b_v)):
                    sp.dma_start(braw[32 * n:32 * (n + 1), :],
                                  b.rearrange("h e -> (h e)").rearrange("(p k) -> p k", p=32)).then_inc(ld_bqkv, 16)
                for n, w in enumerate((w_q, w_k, w_v)):
                    cols = slice(n * HD, (n + 1) * HD)
                    sp.dma_start(wraw[:, 0, cols].rearrange("c (h e) -> c h e", h=H),
                                  w[:, 0:P, :].rearrange("h c e -> c h e")).then_inc(ld_w, 16)
                    for r in range(2):
                        sp.dma_start(wraw[r * D1:(r + 1) * D1, 1, cols].rearrange("c (h e) -> c h e", h=H),
                                      w[:, P:D, :].rearrange("h c e -> c h e")).then_inc(ld_w, 16)
                sp.dma_start(wo[:, :, :], w_o.rearrange("(c a) e d -> (a e) c d", a=2)).then_inc(ld_w, 16)
                sp.dma_start(gw0[:, :], gate_w[0:P, :]).then_inc(ld_small, 16)
                sp.dma_start(gw1[0:D1, :], gate_w[P:D, :]).then_inc(ld_small, 16)
                sp.dma_start(gw1[D1:D1 + 1, :], gate_b.rearrange("(a e) -> a e", a=1)).then_inc(ld_small, 16)
                sp.dma_start(b2s[:, :, :].rearrange("p e d -> p (e d)"),
                              b2.rearrange("(a e) d -> a (e d)", a=1).partition_broadcast(P)).then_inc(ld_small, 16)
                sp.wait_ge(const_pool, 2)
                sp.dma_start(acc[NTOK:NTOK + P, :], zrow[:, :]).then_inc(w_acc0, 16)
                sp.wait_ge(xc_done, STEP)
                load_images(2)
                for g in range(GROUPS):
                    sp.wait_ge(hbo_done, STEP * (g + 1))
                    for r in range(ROWS_A):
                        t0 = 1 + (g * ROWS_A + r) * STEP
                        sp.dma_start(resid[:, t0:t0 + STEP, :].rearrange("b t d -> b (t d)"),
                                     hbo[g % 2][r * NI:(r + 1) * NI, :, :].rearrange("b t d -> b (t d)")
                                     ).then_inc(resid_w[g % 2], 16)
                    if g == 1:
                        sp.wait_ge(whi_done, 6)
                        sp.wait_ge(bhl_done, 1)
                        for n in range(2):
                            sp.dma_start(bqkv_split[n, :].rearrange("(p k) -> p k", p=96), bhl[:, n, :]).then_inc(bhl_w, 16)
                        sp.wait_ge(bhl_w, 32)
                        sp.dma_start(wraw[D1:D1 + 2, 1, :], bqkv_split[:, :]).then_inc(bhl_in, 16)
                sp.wait_ge(cls_bo, 1)
                sp.dma_start(resid[:, 0, :], clsbo[:, :]).then_inc(cls_w, 16)
                sp.wait_ge(bhl_in, 16)
                sp.wait_ge(cls_w, 16)
                sp.wait_ge(resid_w[0], 64)
                sp.wait_ge(resid_w[1], 32)

            @block.scalar
            def _(act):
                for k in range(KF):
                    act.wait_ge(wt_full, k + 1)
                    nc.scalar.copy(wtok[:, k, :], bank[k][:, 0:D]).then_inc(wt_out, 1)
                for s in range(TILES_A + 3):
                    if s < TILES_A:
                        act.wait_ge(tr_done, s + 1)
                        if s >= 2:
                            act.wait_ge(emb_done, s - 1)
                        nc.scalar.copy(pxt[s % 2][:, 0:4, :], bank[2 * (s % 2)][:, :]).then_inc(px_act, 1)
                    if s == 2:
                        act.wait_ge(cls_full, 1)
                        act.wait_ge(const_pool, 5)
                        for part, rows, off in ((XHI, P, 0), (XH1, D1, P), (XHL, D1, P)):
                            last = nc.scalar.copy(xp[0:rows, part, 0:NTOK].rearrange("c (b t) -> c b t", t=T)[:, :, 0],
                                                  bank[7][0:rows, off:off + NI])
                        last.then_inc(xt_out, 1)
                    m = s - 8
                    if 0 <= m < 6:
                        act.wait_ge(ld_w, 16 * N_W)
                        cols = slice(m % 3 * HD, (m % 3 + 1) * HD)
                        nc.scalar.copy(wp[:, (WHI, WHH)[m // 3], cols], wraw[:, m // 3, cols]).then_inc(whi_done, 1)
                    n = s - 3
                    if n >= 0:
                        g, pj = divmod(n, STEP)
                        act.wait_ge(lt_done, n + 1)
                        for part, rows, off in ((XHI, P, 0), (XH1, D1, P), (XHL, D1, P)):
                            last = nc.scalar.copy(columns(n, part, 0, rows),
                                                  bank[6 + n % 2][0:rows, off:off + P].rearrange("c (r b) -> c r b", r=ROWS_A))
                        last.then_inc(xt_out, 1)
                act.wait_ge(bhl_in, 16)
                nc.scalar.copy(wp[D1:D1 + 2, WL1, :], wraw[D1:D1 + 2, 1, :])
                act.wait_ge(w_acc0, 16)

            @block.gpsimd
            def _(pool):
                pool.memset(ident[:, :], 0.0).then_inc(pool_link, 1)
                pool.wait_ge(pool_link, 1)
                pool.affine_select(out=ident[:, :], in_=ident[:, :], compare_op=ALU.not_equal, fill=1.0,
                                   base=0, pattern=[[-1, P]], channel_multiplier=1).then_inc(const_pool, 1)
                pool.memset(mhalf[:, :], -0.5)
                pool.memset(zrow[:, :], 0.0).then_inc(const_pool, 1)
                pool.memset(xparts[:, 0:XH1, NTOK:NPAD], 0.0).then_inc(const_pool, 1)
                pool.memset(xparts[0:D1, XH1, NTOK:NPAD], 0.0).then_inc(const_pool, 1)
                pool.wait_ge(const_pool, 4)
                pool.memset(xparts[D1:P, XH1, :], 1.0).then_inc(const_pool, 1)
                pool.wait_ge(const_pool, 5)
                pool.memset(maskf[:, :], 0.0).then_inc(pool_link, 1)
                pool.memset(trif[:, :], 1.0).then_inc(pool_link, 1)
                pool.wait_ge(pool_link, 3)
                m4 = maskf[:, :].rearrange("q (h k) -> q h k", h=HB)
                m5 = maskf[:, :].rearrange("q (h b k) -> q h b k", h=HB, b=G3)
                pool.affine_select(out=m4, in_=m4, compare_op=ALU.is_ge, fill=CAUSAL, base=0,
                                   pattern=[[0, HB], [-1, TT]], channel_multiplier=1).then_inc(pool_link, 1)
                pool.wait_ge(pool_link, 4)
                pool.affine_select(out=m5, in_=m5, compare_op=ALU.is_ge, fill=FAR, base=T - 1,
                                   pattern=[[0, HB], [T, G3], [0, T]], channel_multiplier=-1).then_inc(pool_link, 1)
                pool.wait_ge(pool_link, 5)
                pool.affine_select(out=m5, in_=m5, compare_op=ALU.is_ge, fill=FAR, base=0,
                                   pattern=[[0, HB], [-T, G3], [0, T]], channel_multiplier=1).then_inc(pool_link, 1)
                pool.affine_select(out=trif[:, :], in_=trif[:, :], compare_op=ALU.is_ge, fill=0.0, base=-1,
                                   pattern=[[1, TT]], channel_multiplier=-1).then_inc(pool_link, 1)
                pool.iota(iotai[:, :], pattern=[[1, E]], base=0, channel_multiplier=0).then_inc(pool_link, 1)
                pool.iota(idtabi[:, :], pattern=[[TT, NT]], base=0, channel_multiplier=1).then_inc(pool_link, 1)
                pool.wait_ge(pool_link, 9)
                pool.memset(onesb[:, :], 1.0).then_inc(const_pool, 1)
                pool.wait_ge(cls_mv, 1)
                pool.tensor_scalar(ve[2][0:NI, :], mv[2][0:NI, 1:2], EPS, None, ALU.add).then_inc(pool_link, 1)
                pool.wait_ge(pool_link, 10)
                pool.tensor_tensor(rs[2][0:NI, :], ve[2][0:NI, :], mhalf[0:NI, :], ALU.pow).then_inc(cls_rs, 1)
                pool.wait_ge(ld_bias, 32)
                pool.tensor_tensor(clsbo[:, :], clsr[:, :], bo[0:NI, :], ALU.add).then_inc(cls_bo, 1)
                for n in range(TILES_A):
                    g, pj = divmod(n, STEP)
                    pool.wait_ge(mv_done, n + 1)
                    pool.tensor_scalar(ve[n % 2][:, :], mv[n % 2][:, 1:2], EPS, None, ALU.add).then_inc(pool_link, 1)
                    pool.wait_ge(pool_link, 11 + n)
                    pool.tensor_tensor(rs[n % 2][:, :], ve[n % 2][:, :], mhalf[:, :], ALU.pow).then_inc(rs_done, 1)
                    if n == 2 * STEP:
                        pool.wait_ge(resid_w[0], 32)
                    pool.tensor_tensor(hbo[g % 2][:, pj, :], hraw[n % 2][:, :], bo[:, :], ALU.add).then_inc(hbo_done, 1)

            @block.vector
            def _(dve):
                links = [0]

                def link(ins):
                    links[0] += 1
                    ins.then_inc(dve_link, 1)
                    dve.wait_ge(dve_link, links[0])

                def gather(s):
                    g, pj = divmod(s, STEP)
                    if pj == 0:
                        dve.wait_ge(x_in[g % 2], 32 * (g // 2 + 1))
                    if s >= 2:
                        dve.wait_ge(tr_done, s - 1)
                    nc.vector.tensor_copy(xc[s % 2][:, :].rearrange("p (m k) -> p m k", k=KER),
                                          xin[g % 2].rearrange("p (m j k) -> p m j k", j=STEP, k=KER)[:, :, pj, :]
                                          ).then_inc(xc_done, 1)

                gather(0)
                gather(1)
                dve.wait_ge(ld_cls, 16)
                link(nc.vector.bn_stats(st[2][0:NI, :], clsr[:, :]))
                nc.vector.bn_aggr(mv[2][0:NI, :], st[2][0:NI, :]).then_inc(cls_mv, 1)
                def low_tokens(n):
                    dve.wait_ge(xt_out, n + 2)
                    src = bank[6 + n % 2]
                    nc.vector.tensor_tensor(columns(n, XLO, 0, P), src[:, 0:P].rearrange("c (r b) -> c r b", r=ROWS_A),
                                            columns(n, XHI, 0, P).bitcast(fp32), ALU.subtract)
                    nc.vector.tensor_tensor(columns(n, XHL, D1, P), src[0:D1, P:2 * P].rearrange("c (r b) -> c r b", r=ROWS_A),
                                            columns(n, XH1, 0, D1).bitcast(fp32), ALU.subtract).then_inc(xt_low, 1)

                for s in range(TILES_A + 4):
                    if s == 3:
                        dve.wait_ge(xt_out, 1)
                        cls = xp[:, :, 0:NTOK].rearrange("c n (b t) -> c n b t", t=T)[:, :, :, 0]
                        nc.vector.tensor_tensor(cls[:, XLO, :], bank[7][:, 0:NI], cls[:, XHI, :].bitcast(fp32), ALU.subtract)
                        nc.vector.tensor_tensor(cls[D1:P, XHL, :], bank[7][0:D1, P:P + NI],
                                                cls[0:D1, XH1, :].bitcast(fp32), ALU.subtract).then_inc(xt_low, 1)
                    if s == 8:
                        dve.wait_ge(ld_bqkv, 48)
                        link(nc.vector.tensor_copy(bhl[:, 0, :].bitcast(fp32r), braw[:, :]))
                        nc.vector.tensor_tensor(bhl[:, 1, :].bitcast(fp32r), braw[:, :], bhl[:, 0, :], ALU.subtract).then_inc(bhl_done, 1)
                    m = s - 9
                    if 0 <= m < 6:
                        dve.wait_ge(whi_done, m + 1)
                        cols = slice(m % 3 * HD, (m % 3 + 1) * HD)
                        rows = (P, D1)[m // 3]
                        nc.vector.tensor_tensor(wp[0:rows, (WLO, WL1)[m // 3], cols], wraw[0:rows, m // 3, cols],
                                                wp[0:rows, (WHI, WHH)[m // 3], cols].bitcast(fp32), ALU.subtract)
                    if s == 1:
                        dve.wait_ge(cls_rs, 1)
                        dve.wait_ge(cls_mv, 1)
                        nc.vector.tensor_scalar(clsn[:, :], clsr[:, :], mv[2][0:NI, 0:1], rs[2][0:NI, 0:1],
                                                ALU.subtract, ALU.mult).then_inc(cls_xn, 1)
                        dve.wait_ge(const_pool, 6)
                        nc.vector.tensor_copy(mask[:, :], maskf[:, :])
                        nc.vector.tensor_copy(tri[:, :], trif[:, :])
                        nc.vector.tensor_copy(identb[:, :], ident[0:TT, 0:TT])
                        nc.vector.tensor_copy(idtab[:, :], idtabi[:, :])
                        link(nc.vector.tensor_copy(iota8[:, :], iotai[:, :]))
                        nc.vector.tensor_scalar(slot0[:, :], iota8[:, :], float(REGION), None, ALU.mult).then_inc(const_dve, 1)
                        dve.wait_ge(ld_bias, 32)
                    if s < TILES_A:
                        dve.wait_ge(tr_done, s + 1)
                        if s >= 2:
                            dve.wait_ge(emb_done, s - 1)
                        nc.vector.tensor_copy(pxt[s % 2][:, 4:KF, :], bank[2 * (s % 2) + 1][:, 0:(KF - 4) * P]).then_inc(px_dve, 1)
                        if s + 2 < TILES_A:
                            gather(s + 2)
                    if s >= 4:
                        low_tokens(s - 4)
                    n = s - 2
                    if 0 <= n < TILES_A:
                        dve.wait_ge(rs_done, n + 1)
                        if n >= 2:
                            dve.wait_ge(lt_done, n - 1)
                        nc.vector.tensor_scalar(xn[n % 2][:, :], hraw[n % 2][:, :], mv[n % 2][:, 0:1], rs[n % 2][:, 0:1],
                                                ALU.subtract, ALU.mult).then_inc(xn_done, 1)
                    n = s - 1
                    if 0 <= n < TILES_A:
                        dve.wait_ge(emb_done, n + 1)
                        if n >= 2:
                            dve.wait_ge(hbo_done, n - 1)
                            dve.wait_ge(xn_done, n - 1)
                        nc.vector.tensor_tensor(hraw[n % 2][:, :], bank[4 + n % 2][:, 0:D], tokb[:, :], ALU.add).then_inc(h_done, 1)
                        dve.wait_ge(h_done, n + 1)
                        link(nc.vector.bn_stats(st[n % 2][:, :], hraw[n % 2][:, :]))
                        nc.vector.bn_aggr(mv[n % 2][:, :], st[n % 2][:, :]).then_inc(mv_done, 1)

            @block.tensor
            def _(pe):
                pe.wait_ge(const_pool, 1)
                pe.wait_ge(ld_tokw, 32)
                for k in range(KF):
                    nc.tensor.transpose(bank[k][:, 0:P], wraw0[:, k * P:(k + 1) * P], ident[:, :])
                    nc.tensor.transpose(bank[k][:, P:D], wraw1[:, k * P:(k + 1) * P], ident[0:D1, 0:D1]).then_inc(wt_full, 1)
                pe.wait_ge(wt_out, KF)
                for s in range(TILES_A + 3):
                    if s < TILES_A:
                        pe.wait_ge(xc_done, s + 1)
                        if s >= 2:
                            pe.wait_ge(px_act, s - 1)
                            pe.wait_ge(px_dve, s - 1)
                        for k in range(KF):
                            last = nc.tensor.transpose(bank[2 * (s % 2) + k // 4][:, (k % 4) * P:(k % 4 + 1) * P],
                                                       xc[s % 2][:, k * P:(k + 1) * P], ident[:, :])
                        last.then_inc(tr_done, 1)
                    if s == 2:
                        pe.wait_ge(cls_xn, 1)
                        nc.tensor.transpose(bank[7][:, 0:NI], clsn[:, 0:P], ident[0:NI, 0:NI])
                        nc.tensor.transpose(bank[7][0:D1, P:P + NI], clsn[:, P:D], ident[0:NI, 0:NI]).then_inc(cls_full, 1)
                    n = s - 1
                    if 0 <= n < TILES_A:
                        pe.wait_ge(px_act, n + 1)
                        pe.wait_ge(px_dve, n + 1)
                        if n >= 2:
                            pe.wait_ge(h_done, n - 1)
                        for k in range(KF):
                            last = nc.tensor.matmul(bank[4 + n % 2][:, 0:D], pxt[n % 2][:, k, :], wtok[:, k, :],
                                                    start=(k == 0), stop=(k == KF - 1))
                        last.then_inc(emb_done, 1)
                    n = s - 3
                    if n >= 0:
                        pe.wait_ge(xn_done, n + 1)
                        if n >= 1:
                            pe.wait_ge(xt_low, n)
                        nc.tensor.transpose(bank[6 + n % 2][:, 0:P], xn[n % 2][:, 0:P], ident[:, :])
                        nc.tensor.transpose(bank[6 + n % 2][0:D1, P:2 * P], xn[n % 2][:, P:D], ident[:, :]).then_inc(lt_done, 1)

        PROJ_JOBS, ROT_JOBS, TAIL_JOBS = 5, 6, 6
        with ExitStack() as cb:
            def sbb(name, shape, dt=fp32):
                return cb.enter_context(nc.sbuf_tensor(name, shape, dt))

            def semb(name):
                return cb.enter_context(nc.semaphore(name))

            xs = sbb("xs", [P, 4, W2T], fp32r)
            qk = sbb("qk", [P, HC, 2, W2T])
            vs = [sbb(f"vs{j}", [TT, H, DH]) for j in range(2)]
            pr = [sbb(f"pr{j}", [TT, H, TT]) for j in range(2)]
            mx = [sbb(f"mx{j}", [TT, H]) for j in range(2)]
            pt = [sbb(f"pt{g}", [TT, HB, TT]) for g in range(NG)]
            rinv = [sbb(f"rinv{j}", [TT, H]) for j in range(2)]
            zt = [sbb(f"zt{j}", [P, HC, TT]) for j in range(2)]
            hb = [sbb(f"hb{j}", [TT, D]) for j in range(2)]
            h2 = [sbb(f"h2{j}", [TT, D]) for j in range(2)]
            stb = [sbb(f"stb{j}", [TT, 6]) for j in range(2)]
            mvb = [sbb(f"mvb{j}", [TT, 2]) for j in range(2)]
            veb = [sbb(f"veb{j}", [TT, 1]) for j in range(2)]
            rsb = [sbb(f"rsb{j}", [TT, 1]) for j in range(2)]
            xr = [[sbb(f"xr{j}{k}", [TT, ROW]) for k in range(2)] for j in range(2)]
            x2t0 = [sbb(f"x2t0{j}", [P, TT]) for j in range(2)]
            x2t1 = [sbb(f"x2t1{j}", [D1 + 1, TT]) for j in range(2)]
            lg = [sbb(f"lg{j}", [TT, E]) for j in range(2)]
            mx8 = [sbb(f"mx8{j}", [TT, 8]) for j in range(2)]
            ix8 = [sbb(f"ix8{j}", [TT, 8], u32) for j in range(2)]
            ixf = [sbb(f"ixf{j}", [TT, 2]) for j in range(2)]
            msk = [sbb(f"msk{j}", [TT, 2, E]) for j in range(2)]
            mskb = [sbb(f"mskb{j}", [TT, E], bf16) for j in range(2)]
            dl = [sbb(f"dl{j}", [TT, 1]) for j in range(2)]
            el = [sbb(f"el{j}", [TT, 2]) for j in range(2)]
            s8 = [sbb(f"s8{j}", [TT, 3, E]) for j in range(2)]
            slf = [sbb(f"slf{j}", [TT, 2]) for j in range(2)]
            sli = [sbb(f"sli{j}", [TT, 2], u32) for j in range(2)]
            b1r = sbb("b1r", [P, E * F // P])
            b1hl = sbb("b1hl", [P, 2, E * F // P])
            padrow = sbb("padrow", [P, ROW])
            padid = sbb("padid", [P, 1], i32)
            cntf, cnti = sbb("cntf", [1, E]), sbb("cnti", [1, E], i32)
            tilef = sbb("tilef", [1, E])
            cum = [tilef] + [sbb(f"cum{n}", [1, E]) for n in range(1, 4)]
            first = sbb("first", [1, E])
            tii, tif = sbb("tii", [1, NTILE], i32), sbb("tif", [1, NTILE])
            cmp, cmpt = (pr[j][0:1, :, :].rearrange("a h k -> a (h k)")[:, 0:NTILE * E].rearrange("a (t e) -> a t e", e=E)
                         for j in range(2))
            et, before = sbb("et", [1, NTILE]), sbb("before", [1, NTILE])
            used = sbb("used", [1, NTILE])
            rowf = sbb("rowf", [1, NTILE])

            full = [semb(f"full{b}") for b in range(8)]
            free = [semb(f"free{b}") for b in range(8)]
            xs_ready, row1_done, p_done = semb("xs_ready"), semb("row1_done"), semb("p_done")
            even_done, scored, sub_done, exp_done = semb("even_done"), semb("scored"), semb("sub_done"), semb("exp_done")
            h2_done, mvb_done, rsb_done, xnb_done = semb("h2_done"), semb("mvb_done"), semb("rsb_done"), semb("xnb_done")
            mask_done, dl_done, el_done = semb("mask_done"), semb("dl_done"), semb("el_done")
            slot_done, row_done = semb("slot_done"), semb("row_done")
            scat = [semb(f"scat{j}") for j in range(2)]
            xr_free = [semb(f"xr_free{j}") for j in range(2)]
            settled = {e.engine: semb(f"settled{n}") for n, e in enumerate((nc.vector, nc.gpsimd))}
            hb_in = [semb(f"hb_in{j}") for j in range(2)]
            acc_w = [semb(f"acc_w{j}") for j in range(2)]
            att_link, tail_link, pool_linkb = semb("att_link"), semb("tail_link"), semb("pool_link_b")
            ld_b1, b1_ready, b1_w, b1_in = semb("ld_b1"), semb("b1_ready"), semb("b1_w"), semb("b1_in")
            iotas, pads, pad_w, link_b = semb("iotas"), semb("pads"), semb("pad_w"), semb("link_b")
            pad_w2 = semb("pad_w2")
            hia_done, hib_done = semb("hia_done"), semb("hib_done")

            def settle(engine):
                engine.sem_inc(settled[engine.engine], 1)

            POOL_LOW = 3

            def head_of(g, n):
                return 2 * n + g if g < 2 else 2 * HB + n

            def turn(i, jobs, k):
                return i * jobs + k

            block = cb.enter_context(nc.Block())

            @block.sync
            def _(sp):
                def load_hb(i, j, rows=TT):
                    sp.wait_ge(h2_done, i * 2 + (j + 1))
                    sp.dma_start(hb[j][0:rows, :], resid_rows[bass.ds(i * W2T + j * TT, rows), :]).then_inc(hb_in[j], 16)

                def store_h2(i, j, rows=TT):
                    sp.wait_ge(h2_done, i * 2 + (j + 3))
                    sp.dma_start(acc[bass.ds(i * W2T + j * TT, rows), :], h2[j][0:rows, :]).then_inc(acc_w[j], 16)

                for j in range(2):
                    sp.sem_inc(acc_w[j], 1)
                for j in range(2):
                    load_hb(0, j)
                sp.dma_start(b1r[:, :], b1.rearrange("e f -> (e f)").rearrange("(p n) -> p n", p=P)).then_inc(ld_b1, 16)
                sp.dma_start(w1a[:, :, :], w1[:, 0:P, :].rearrange("e c f -> c e f")).then_inc(ld_w1, 16)
                sp.dma_start(w1b[0:D1, :, :], w1[:, P:D, :].rearrange("e c f -> c e f")).then_inc(ld_w1, 16)
                sp.dma_start(w1b[D1:P, :, :], w1[:, P:D, :].rearrange("e c f -> c e f")).then_inc(ld_w1, 16)
                sp.wait_ge(b1_ready, 1)
                for n in range(2):
                    sp.dma_start(b1_split[n, :].rearrange("(p n) -> p n", p=P), b1hl[:, n, :]).then_inc(b1_w, 16)
                with sp.Fori(0, NIT - 2) as i:
                    for j in range(2):
                        store_h2(i, j)
                        load_hb(i + 1, j)
                store_h2(NIT - 2, 0)
                load_hb(NIT - 1, 0)
                store_h2(NIT - 2, 1)
                load_hb(NIT - 1, 1, LAST)
                sp.wait_ge(b1_w, 32)
                sp.wait_ge(hib_done, E)
                sp.dma_start(w1b[D1:D1 + 2, :, :].rearrange("a e f -> a (e f)"), b1_split[:, :]).then_inc(b1_in, 16)
                store_h2(NIT - 1, 0)
                store_h2(NIT - 1, 1, LAST)
                sp.wait_ge(pads, 1)
                sp.dma_start(queue[E * REGION:E * REGION + P, :], padrow[:, :]).then_inc(pad_w, 16)
                sp.wait_ge(tables, 1)
                for e in range(E // 2):
                    row = sp.value_load(padtab[0:1, e:e + 1], min_val=e * REGION, max_val=e * REGION + NTOK)
                    sp.dma_start(queue[bass.ds(row, P), :], padrow[:, :]).then_inc(pad_w, 16)
                sp.wait_ge(pad_w, 16 * (E // 2 + 1))
                sp.wait_ge(pad_w2, 16 * (E // 2))
                sp.wait_ge(tables, 2)
                for j in range(2):
                    sp.wait_ge(scat[j], 32 * NIT)
                row = sp.value_load(rowtab[0:1, 0:1], min_val=0, max_val=E * REGION)
                sp.dma_start(xq[0][:, :], queue[bass.ds(row, P), :]).then_inc(xq_in[0], 16)
                sp.wait_ge(b1_in, 16)
                for j in range(2):
                    sp.wait_ge(acc_w[j], 16 * NIT + 1)

            @block.gpsimd
            def _(pool):
                def copy_tokens(i):
                    nc.gpsimd.tensor_copy(xs[:, :, :], xp[:, :, bass.ds(i * W2T, W2T)]).then_inc(xs_ready, 1)

                def rstd(i, j):
                    pool.wait_ge(mvb_done, i * 2 + (j + 1))
                    settle(pool)
                    nc.gpsimd.tensor_scalar(veb[j][:, :], mvb[j][:, 1:2], EPS, None, ALU.add).then_inc(pool_linkb, 1)
                    pool.wait_ge(pool_linkb, i * 2 + (j + 1))
                    nc.gpsimd.tensor_tensor(rsb[j][:, :], veb[j][:, :], mhalf[0:TT, :], ALU.pow).then_inc(rsb_done, 1)

                def next_tokens(i):
                    pool.wait_ge(full[1], turn(i, PROJ_JOBS, PROJ_JOBS))
                    settle(pool)
                    copy_tokens(i + 1)

                def row_copies(i, j):
                    pool.wait_ge(xnb_done, i * 2 + (j + 1))
                    settle(pool)
                    nc.gpsimd.tensor_copy(xr[j][1][:, 0:D], xr[j][0][:, 0:D])
                    for k in range(2):
                        last = nc.gpsimd.tensor_copy(xr[j][k][:, D + 1:D + 2], idtab[0:TT, bass.ds(i * 2 + j, 1)])
                    last.then_inc(row_done, 1)

                def send_rows(i, j, rows=TT):
                    pool.wait_ge(row_done, i * 2 + (j + 1))
                    pool.wait_ge(slot_done, i * 2 + (j + 1))
                    settle(pool)
                    for k in range(2):
                        nc.gpsimd.indirect_dma_start(
                            out=queue[:, :], out_offset=bass.IndirectOffsetOnAxis(sli[j][0:rows, k:k + 1], 0),
                            in_=xr[j][k][0:rows, :], in_offset=None,
                            bounds_check=(E + 1) * REGION - 1, oob_is_err=True).then_inc(scat[j], 16)

                def low_a(e):
                    pool.wait_ge(hia_done, e + 1)
                    w = w1al[:, e * F:(e + 1) * F]
                    nc.gpsimd.tensor_tensor(w, w1a[:, e, :], w1ah[:, e * F:(e + 1) * F].bitcast(fp32), ALU.subtract)

                def rows_left(i, j):
                    pool.wait_ge(scat[j], i * 32 + 32)
                    pool.sem_inc(xr_free[j], 1)

                def body(i, tail=True, more=True):
                    if tail:
                        row_copies(i - 1, 0)
                        rstd(i - 1, 1)
                    if more:
                        next_tokens(i)
                    if tail:
                        row_copies(i - 1, 1)
                        send_rows(i - 1, 0)
                    rstd(i, 0)
                    if tail:
                        rows_left(i - 1, 0)
                        send_rows(i - 1, 1)
                        rows_left(i - 1, 1)

                copy_tokens(0)
                for j in range(2):
                    pool.sem_inc(xr_free[j], 1)
                pool.iota(tii[:, :], pattern=[[1, NTILE]], base=0, channel_multiplier=0).then_inc(iotas, 1)
                pool.memset(padrow[:, :], 0.0).then_inc(iotas, 1)
                pool.iota(padid[:, :], pattern=[[0, 1]], base=NTOK, channel_multiplier=1).then_inc(iotas, 1)
                pool.wait_ge(iotas, 3)
                pool.tensor_copy(padrow[:, D + 1:D + 2], padid[:, :]).then_inc(pads, 1)
                body(0, tail=False)
                with pool.Fori(1, NIT - 1) as i:
                    body(i)
                body(NIT - 1, more=False)
                row_copies(NIT - 1, 0)
                low_a(0)
                rstd(NIT - 1, 1)
                row_copies(NIT - 1, 1)
                for e in range(1, POOL_LOW):
                    low_a(e)
                send_rows(NIT - 1, 0)
                send_rows(NIT - 1, 1, LAST)
                for j in range(2):
                    rows_left(NIT - 1, j)

            @block.scalar
            def _(act):
                def drain(i, b, jobs, k, dst, src):
                    act.wait_ge(full[b], turn(i, jobs, k))
                    nc.scalar.copy(dst, src).then_inc(free[b], 1)

                def qk_out(i, n):
                    drain(i, n % 2, PROJ_JOBS, n // 2 + 1, qk[:, n, :, :].rearrange("p a t -> p (a t)"),
                          bank[n % 2][:, 0:2 * W2T])

                def v_out(i, j):
                    for b in range(2):
                        drain(i, b, PROJ_JOBS, 4 + j, vs[j][:, b * H // 2:(b + 1) * H // 2, 0:DH],
                              bank[b][0:TT, 0:HD // 2].rearrange("p (h e) -> p h e", e=DH))

                def probs(i, j):
                    act.wait_ge(sub_done, i * 2 + (j + 2))
                    nc.scalar.activation(pr[j][:, :, :], pr[j][:, :, :], ACT.Exp, scale=DH ** -0.5).then_inc(exp_done, 1)

                def pt_out(i, b, k, g):
                    drain(i, b, ROT_JOBS, k, pt[g][:, :, :].rearrange("p h k -> p (h k)"), bank[b][0:TT, 0:HB * TT])

                def zt_out(i, b, k, j, c0, n):
                    drain(i, b, ROT_JOBS, k, zt[j][:, c0:c0 + n, :].rearrange("p c t -> p (c t)"), bank[b][:, 0:n * TT])

                def x2_out(i, k, j):
                    act.wait_ge(full[7], turn(i, TAIL_JOBS, k))
                    nc.scalar.copy(x2t0[j][:, :], bank[7][:, 0:TT])
                    nc.scalar.copy(x2t1[j][0:D1, :], bank[7][0:D1, TT:2 * TT]).then_inc(free[7], 1)

                def gate_exp(i, j):
                    act.wait_ge(dl_done, i * 2 + (j + 1))
                    nc.scalar.activation(el[j][:, 0:1], dl[j][:, :], ACT.Exp).then_inc(el_done, 1)

                def high_b(e):
                    nc.scalar.copy(w1bh[:, e * F:(e + 1) * F], w1b[:, e, :]).then_inc(hib_done, 1)

                def high_a(e):
                    nc.scalar.copy(w1ah[:, e * F:(e + 1) * F], w1a[:, e, :]).then_inc(hia_done, 1)

                def body(i, tail=True, fill=qk_out, then=lambda n: None):
                    if tail:
                        x2_out(i - 1, 1, 0)
                    probs(i, 0)
                    v_out(i, 0)
                    v_out(i, 1)
                    then(0)
                    pt_out(i, 5, 1, 0)
                    pt_out(i, 6, 1, 1)
                    fill(i + 1, 0)
                    pt_out(i, 5, 2, 2)
                    probs(i, 1)
                    zt_out(i, 6, 2, 0, 0, 4)
                    zt_out(i, 5, 3, 0, 4, 2)
                    if tail:
                        gate_exp(i - 1, 0)
                    fill(i + 1, 1)
                    fill(i + 1, 2)
                    if tail:
                        x2_out(i - 1, 3, 1)
                    fill(i + 1, 3)
                    fill(i + 1, 4)
                    pt_out(i, 6, 3, 0)
                    pt_out(i, 5, 4, 1)
                    if tail:
                        gate_exp(i - 1, 1)
                    fill(i + 1, 5)
                    pt_out(i, 6, 4, 2)
                    then(1)
                    zt_out(i, 6, 5, 1, 0, 4)
                    zt_out(i, 5, 6, 1, 4, 2)
                    then(2)

                for b in range(2):
                    act.sem_inc(free[b], 1)
                for n in range(HC):
                    qk_out(0, n)
                body(0, tail=False)
                with act.Fori(1, NIT - 1) as i:
                    body(i)
                act.wait_ge(ld_w1, 48)

                def then(n):
                    if n == 0:
                        act.dma_start(w2s[:, :, :, :], w2.rearrange("e (k p) d -> p e k d", p=P)).then_inc(ld_w2, 16)
                    elif n == 1:
                        high_b(6)
                        high_b(7)
                        high_a(0)
                    else:
                        for e in range(1, 5):
                            high_a(e)

                body(NIT - 1, fill=lambda i, n: high_b(n), then=then)
                x2_out(NIT - 1, 1, 0)
                high_a(5)
                high_a(6)
                x2_out(NIT - 1, 3, 1)
                gate_exp(NIT - 1, 0)
                high_a(7)
                gate_exp(NIT - 1, 1)
                act.wait_ge(pads, 1)
                act.wait_ge(tables, 1)
                for e in range(E // 2, E):
                    row = act.value_load(padtab[0:1, e:e + 1], min_val=e * REGION, max_val=e * REGION + NTOK)
                    act.dma_start(queue[bass.ds(row, P), :], padrow[:, :]).then_inc(pad_w2, 16)
                act.wait_ge(pad_w2, 16 * (E // 2))

            @block.vector
            def _(dve):
                ATT_LINKS, TAIL_LINKS = 6, 16
                count = {"att": 0, "tail": 0}

                def link_att(i, ins):
                    count["att"] += 1
                    ins.then_inc(att_link, 1)
                    dve.wait_ge(att_link, i * ATT_LINKS + count["att"])

                def link_tail(i, ins):
                    count["tail"] += 1
                    ins.then_inc(tail_link, 1)
                    dve.wait_ge(tail_link, i * TAIL_LINKS + count["tail"])

                def sub_max(i, j):
                    dve.wait_ge(scored, i * 2 + (j + 1))
                    for g in range(NG):
                        sv = bank[2 + g][0:TT, 0:HB * TT].rearrange("q (h k) -> q h k", h=HB)
                        last = nc.vector.reduce_max(mx[j][:, g * HB:(g + 1) * HB], sv, AX.X)
                    link_att(i, last)
                    for g in range(NG):
                        sv = bank[2 + g][0:TT, 0:HB * TT].rearrange("q (h k) -> q h k", h=HB)
                        mb = mx[j][:, g * HB:(g + 1) * HB].rearrange("q (h o) -> q h o", o=1).to_broadcast([TT, HB, TT])
                        last = nc.vector.tensor_tensor(pr[j][:, g * HB:(g + 1) * HB, :], sv, mb, ALU.subtract)
                    last.then_inc(sub_done, 1)

                def norm_probs(i, j):
                    dve.wait_ge(exp_done, i * 2 + (j + 1))
                    link_att(i, nc.vector.reduce_sum(rinv[j][:, :], pr[j][:, :, :], AX.X))
                    link_att(i, nc.vector.reciprocal(rinv[j][:, :], rinv[j][:, :]))
                    nc.vector.tensor_tensor(pr[j][:, :, :], pr[j][:, :, :],
                                            rinv[j][:, :].rearrange("q (h o) -> q h o", o=1).to_broadcast([TT, H, TT]),
                                            ALU.mult).then_inc(p_done, 1)

                def o_out(i, b, k, j):
                    dve.wait_ge(full[b], turn(i, ROT_JOBS, k))
                    dve.wait_ge(hb_in[j], (i + 1) * 16)
                    dve.wait_ge(acc_w[j], i * 16 + 1)
                    nc.vector.tensor_tensor(h2[j][:, :], bank[b][0:TT, 0:D], hb[j][:, :], ALU.add).then_inc(free[b], 1)
                    dve.wait_ge(free[b], turn(i, ROT_JOBS, k + 1))
                    nc.vector.bn_stats(stb[j][:, :], h2[j][:, :]).then_inc(h2_done, 1)
                    dve.wait_ge(h2_done, i * 2 + (j + 3))
                    settle(dve)
                    nc.vector.bn_aggr(mvb[j][:, :], stb[j][:, :]).then_inc(mvb_done, 1)

                def norm(i, j):
                    dve.wait_ge(rsb_done, i * 2 + (j + 1))
                    dve.wait_ge(mvb_done, i * 2 + (j + 1))
                    dve.wait_ge(xr_free[j], i + 1)
                    nc.vector.tensor_scalar(xr[j][0][:, 0:D], h2[j][:, :], mvb[j][:, 0:1], rsb[j][:, 0:1],
                                            ALU.subtract, ALU.mult).then_inc(xnb_done, 1)

                def route(i, k, j):
                    dve.wait_ge(full[7], turn(i, TAIL_JOBS, k))
                    nc.vector.tensor_copy(lg[j][:, :], bank[7][0:TT, 0:E]).then_inc(free[7], 1)
                    dve.wait_ge(free[7], turn(i, TAIL_JOBS, k + 1))
                    settle(dve)
                    link_tail(i, nc.vector.max(mx8[j][:, :], lg[j][:, :]))
                    nc.vector.tensor_tensor(dl[j][:, :], mx8[j][:, 1:2], mx8[j][:, 0:1], ALU.subtract).then_inc(dl_done, 1)
                    link_tail(i, nc.vector.max_index(ix8[j][:, :], mx8[j][:, :], lg[j][:, :]))
                    link_tail(i, nc.vector.tensor_copy(ixf[j][:, :], ix8[j][:, 0:2]))
                    for n in range(2):
                        last = nc.vector.tensor_scalar(msk[j][:, n, :], iota8[0:TT, :], ixf[j][:, n:n + 1], None, ALU.is_equal)
                    link_tail(i, last)
                    nc.vector.tensor_tensor(mskb[j][:, :], msk[j][:, 0, :], msk[j][:, 1, :], ALU.add).then_inc(mask_done, 1)

                def slots(i, k, j):
                    dve.wait_ge(full[7], turn(i, TAIL_JOBS, k))
                    link_tail(i, nc.vector.tensor_tensor(s8[j][:, 0, :], bank[7][0:TT, 0:E], slot0[0:TT, :], ALU.add))
                    nc.vector.tensor_tensor(slot0[:, :], bank[7][:, E:2 * E], slot0[:, :], ALU.add).then_inc(free[7], 1)
                    for n in range(2):
                        last = nc.vector.tensor_tensor_reduce(out=s8[j][:, 1 + n, :], in0=msk[j][:, n, :], in1=s8[j][:, 0, :],
                                                              scale=1.0, scalar=0.0, op0=ALU.mult, op1=ALU.add,
                                                              accum_out=slf[j][:, n:n + 1])
                    link_tail(i, last)
                    dve.wait_ge(free[7], turn(i, TAIL_JOBS, k + 1))
                    nc.vector.tensor_copy(sli[j][:, :], slf[j][:, :])

                def weights(i, j):
                    dve.wait_ge(el_done, i * 2 + (j + 1))
                    link_tail(i, nc.vector.tensor_scalar(el[j][:, 1:2], el[j][:, 0:1], 1.0, None, ALU.add))
                    link_tail(i, nc.vector.reciprocal(xr[j][0][:, D:D + 1], el[j][:, 1:2]))
                    nc.vector.tensor_tensor(xr[j][1][:, D:D + 1], el[j][:, 0:1], xr[j][0][:, D:D + 1],
                                            ALU.mult).then_inc(slot_done, 1)

                def low_b(e):
                    dve.wait_ge(hib_done, e + 1)
                    w = w1bl[0:D1, e * F:(e + 1) * F]
                    nc.vector.tensor_tensor(w, w1b[0:D1, e, :], w1bh[0:D1, e * F:(e + 1) * F].bitcast(fp32), ALU.subtract)

                def low_a(e):
                    dve.wait_ge(hia_done, e + 1)
                    w = w1al[:, e * F:(e + 1) * F]
                    nc.vector.tensor_tensor(w, w1a[:, e, :], w1ah[:, e * F:(e + 1) * F].bitcast(fp32), ALU.subtract)

                def low_parts(n0, n1):
                    for n in range(n0, n1):
                        if n < E:
                            low_b(n)
                        else:
                            low_a(n - E + POOL_LOW)

                def body(i, tail=True, low=None):
                    count["att"] = count["tail"] = 0
                    if tail:
                        norm(i - 1, 0)
                    sub_max(i, 0)
                    if tail:
                        o_out(i - 1, 6, 6, 1)
                    norm_probs(i, 0)
                    sub_max(i, 1)
                    if tail:
                        route(i - 1, 2, 0)
                        norm(i - 1, 1)
                    norm_probs(i, 1)
                    if tail:
                        route(i - 1, 4, 1)
                        slots(i - 1, 5, 0)
                        weights(i - 1, 0)
                    if low:
                        low(0, 2)
                    o_out(i, 5, 5, 0)
                    if tail:
                        slots(i - 1, 6, 1)
                        weights(i - 1, 1)
                        assert count["tail"] == TAIL_LINKS
                    if low:
                        low(2, 5)
                    assert count["att"] == ATT_LINKS

                def link(ins):
                    count["tables"] += 1
                    ins.then_inc(link_b, 1)
                    dve.wait_ge(link_b, count["tables"])

                def tables_out():
                    link(nc.vector.tensor_tensor(cntf[:, :], first[:, :], slot0[0:1, :], ALU.add))
                    link(nc.vector.tensor_copy(cnti[:, :], cntf[:, :]))
                    link(nc.vector.tensor_scalar(cnti[:, :], cnti[:, :], 7, None, ALU.arith_shift_right))
                    link(nc.vector.tensor_copy(tilef[:, :], cnti[:, :]))
                    for n in range(3):
                        d = 1 << n
                        nc.vector.tensor_copy(cum[n + 1][:, 0:d], cum[n][:, 0:d])
                        link(nc.vector.tensor_tensor(cum[n + 1][:, d:E], cum[n][:, d:E], cum[n][:, 0:E - d], ALU.add))
                    link(nc.vector.tensor_tensor(cmp[:, :, :], tif[:, :].rearrange("a (t o) -> a t o", o=1).to_broadcast([1, NTILE, E]),
                                                 cum[3][:, :].rearrange("a (o e) -> a o e", o=1).to_broadcast([1, NTILE, E]), ALU.is_ge))
                    link(nc.vector.tensor_tensor(cmpt[:, :, :], cmp[:, :, :],
                                                 tilef[:, :].rearrange("a (o e) -> a o e", o=1).to_broadcast([1, NTILE, E]), ALU.mult))
                    nc.vector.reduce_sum(et[:, :], cmp[:, :, :], AX.X)
                    link(nc.vector.reduce_sum(before[:, :], cmpt[:, :, :], AX.X))
                    nc.vector.tensor_scalar(used[:, :], et[:, :], float(E), float(P), ALU.is_lt, ALU.mult)
                    link(nc.vector.tensor_tensor(rowf[:, :], tif[:, :], before[:, :], ALU.subtract))
                    link(nc.vector.tensor_tensor(rowf[:, :], rowf[:, :], used[:, :], ALU.mult))
                    link(nc.vector.scalar_tensor_tensor(rowf[:, :], et[:, :], float(REGION), rowf[:, :], ALU.mult, ALU.add))
                    nc.vector.tensor_copy(rowtab[:, :], rowf[:, :])
                    link(nc.vector.tensor_scalar(before[:, :], et[:, :], float(E - 1), None, ALU.min))
                    nc.vector.tensor_copy(exptab[:, :], before[:, :]).then_inc(tables, 1)

                for j in range(2):
                    nc.vector.memset(x2t1[j][D1:D1 + 1, :], 1.0).then_inc(row1_done, 1)
                count["tables"] = 0
                dve.sem_inc(sub_done, 1)
                dve.sem_inc(h2_done, 2)
                for b in (5, 6, 7):
                    dve.sem_inc(free[b], 1)
                dve.wait_ge(ld_b1, 16)
                link(nc.vector.tensor_copy(b1hl[:, 0, :].bitcast(fp32r), b1r[:, :]))
                nc.vector.tensor_tensor(b1hl[:, 1, :].bitcast(fp32r), b1r[:, :], b1hl[:, 0, :], ALU.subtract).then_inc(b1_ready, 1)
                dve.wait_ge(iotas, 1)
                nc.vector.tensor_copy(tif[:, :], tii[:, :])
                nc.vector.tensor_scalar(first[:, :], iota8[0:1, :], -float(REGION), float(P - 1), ALU.mult, ALU.add)
                body(0, tail=False)
                with dve.Fori(1, NIT - 1) as i:
                    body(i)
                body(NIT - 1, low=low_parts)
                last_tail = NIT - 1
                count["tail"] = 0
                norm(last_tail, 0)
                low_parts(5, 9)
                o_out(last_tail, 6, 6, 1)
                route(last_tail, 2, 0)
                low_parts(9, 10)
                norm(last_tail, 1)
                low_parts(10, 11)
                route(last_tail, 4, 1)
                slots(last_tail, 5, 0)
                weights(last_tail, 0)
                slots(last_tail, 6, 1)
                nc.vector.tensor_copy(padtab[:, :], slot0[0:1, :]).then_inc(tables, 1)
                weights(last_tail, 1)
                tables_out()
                low_parts(11, 13)

            @block.tensor
            def _(pe):
                mm = nc.tensor.matmul

                def start(i, b, jobs, k):
                    pe.wait_ge(free[b], turn(i, jobs, k))

                def mm_parts(o, w, x, x_stationary):
                    steps = ((WHI, XHI, P), (WLO, XHI, P), (WHI, XLO, P), (WHH, XHL, P), (WL1, XH1, D1 + 2))
                    for n, (wn, xn_, rows) in enumerate(steps):
                        pair = (w(wn, rows), x(xn_, rows))
                        last = mm(o, *(pair[::-1] if x_stationary else pair), start=(n == 0), stop=(n == len(steps) - 1))
                    return last

                def qk_proj(i, c):
                    b, k = c % 2, c // 2 + 1
                    start(i, b, PROJ_JOBS, k)
                    for n in range(2):
                        o = bank[b][:, n * W2T:(n + 1) * W2T]
                        cols = slice(n * HD + c * P, n * HD + (c + 1) * P)
                        last = mm_parts(o, lambda part, rows: wp[0:rows, part, cols],
                                        lambda part, rows: xp[0:rows, part, bass.ds(i * W2T, W2T)], False)
                    last.then_inc(full[b], 1)

                def v_proj(i, j):
                    for b in range(2):
                        start(i, b, PROJ_JOBS, 4 + j)
                        o = bank[b][0:TT, 0:HD // 2]
                        cols = slice(2 * HD + b * HD // 2, 2 * HD + (b + 1) * HD // 2)
                        mm_parts(o, lambda part, rows: wp[0:rows, part, cols],
                                 lambda part, rows: xs[0:rows, part, j * TT:(j + 1) * TT], True).then_inc(full[b], 1)

                def scores(i, j):
                    pe.wait_ge(sub_done, i * 2 + (j + 1))
                    for g in range(NG):
                        mm(bank[2 + g][0:TT, 0:HB * TT], identb[:, :], mask[:, :], start=True, stop=True)

                    def head(g, n):
                        h = head_of(g, n)
                        rows = slice(DH * (h % 2), DH * (h % 2 + 1))
                        q = qk[rows, h // 2, 0, j * TT:(j + 1) * TT]
                        k = qk[rows, h // 2, 1, j * TT:(j + 1) * TT]
                        return mm(bank[2 + g][0:TT, n * TT:(n + 1) * TT], q, k, start=False, stop=True,
                                  skip_group_check=True)

                    head(2, 0)
                    head(2, 2).then_inc(even_done, 1)
                    for n in range(HB):
                        head(0, n)
                    pe.wait_ge(even_done, i * 2 + (j + 1))
                    head(2, 1)
                    head(2, 3)
                    for n in range(HB):
                        last = head(1, n)
                    last.then_inc(scored, 1)

                def pt_job(i, b, k, j, g):
                    pe.wait_ge(p_done, i * 2 + (j + 1))
                    start(i, b, ROT_JOBS, k)
                    for n in range(HB):
                        last = nc.tensor.transpose(bank[b][0:TT, n * TT:(n + 1) * TT], pr[j][:, g * HB + n, :], ident[0:TT, 0:TT])
                    last.then_inc(full[b], 1)

                def pv_job(i, b, k, j, chunks, pt_turns):
                    for zb, zk in pt_turns:
                        pe.wait_ge(free[zb], turn(i, ROT_JOBS, zk + 1))
                    start(i, b, ROT_JOBS, k)
                    for m, c in enumerate(chunks):
                        for half in range(2):
                            h = 2 * c + half
                            g, n = (half, c) if h < 2 * HB else (2, h - 2 * HB)
                            last = mm(bank[b][DH * half:DH * (half + 1), m * TT:(m + 1) * TT], vs[j][:, h, :], pt[g][:, n, :],
                                      start=True, stop=True)
                    last.then_inc(full[b], 1)

                def o_job(i, b, k, j, zt_turns):
                    for zb, zk in zt_turns:
                        pe.wait_ge(free[zb], turn(i, ROT_JOBS, zk + 1))
                    start(i, b, ROT_JOBS, k)
                    for c in range(HC):
                        last = mm(bank[b][0:TT, 0:D], zt[j][:, c, :], wo[:, c, :], start=(c == 0), stop=(c == HC - 1))
                    last.then_inc(full[b], 1)

                def x2_job(i, k, j):
                    pe.wait_ge(xnb_done, i * 2 + (j + 1))
                    start(i, 7, TAIL_JOBS, k)
                    nc.tensor.transpose(bank[7][:, 0:TT], xr[j][0][:, 0:P], ident[0:TT, 0:TT])
                    nc.tensor.transpose(bank[7][0:D1, TT:2 * TT], xr[j][0][:, P:D], ident[0:TT, 0:TT]).then_inc(full[7], 1)

                def gate_job(i, k, j):
                    start(i, 7, TAIL_JOBS, k)
                    mm(bank[7][0:TT, 0:E], x2t0[j][:, :], gw0[:, :], start=True, stop=False)
                    mm(bank[7][0:TT, 0:E], x2t1[j][:, :], gw1[:, :], start=False, stop=True).then_inc(full[7], 1)

                def rank_job(i, k, j, rows=TT):
                    pe.wait_ge(mask_done, i * 2 + (j + 1))
                    start(i, 7, TAIL_JOBS, k)
                    mm(bank[7][0:TT, 0:E], tri[0:rows, :], mskb[j][0:rows, :], start=True, stop=True)
                    mm(bank[7][:, E:2 * E], onesb[0:rows, :], mskb[j][0:rows, :], start=True, stop=True).then_inc(full[7], 1)

                def body(i, tail=True, more=True):
                    pe.wait_ge(free[0], turn(i, PROJ_JOBS, 4))
                    pe.wait_ge(free[1], turn(i, PROJ_JOBS, 4))
                    scores(i, 0)
                    if tail:
                        x2_job(i - 1, 1, 0)
                        o_job(i - 1, 6, 6, 1, [(6, 5), (5, 6)])
                    pe.wait_ge(xs_ready, i + 1)
                    v_proj(i, 0)
                    if tail:
                        gate_job(i - 1, 2, 0)
                    scores(i, 1)
                    v_proj(i, 1)
                    pt_job(i, 5, 1, 0, 0)
                    pt_job(i, 6, 1, 0, 1)
                    if more:
                        qk_proj(i + 1, 0)
                    pt_job(i, 5, 2, 0, 2)
                    pe.wait_ge(free[0], turn(i, PROJ_JOBS, 5))
                    pe.wait_ge(free[1], turn(i, PROJ_JOBS, 5))
                    pv_job(i, 6, 2, 0, range(4), [(5, 1), (6, 1)])
                    pv_job(i, 5, 3, 0, range(4, HC), [(5, 2)])
                    if more:
                        qk_proj(i + 1, 1)
                        qk_proj(i + 1, 2)
                    if tail:
                        x2_job(i - 1, 3, 1)
                    if more:
                        qk_proj(i + 1, 3)
                    if tail:
                        gate_job(i - 1, 4, 1)
                    if more:
                        qk_proj(i + 1, 4)
                    pt_job(i, 6, 3, 1, 0)
                    pt_job(i, 5, 4, 1, 1)
                    if tail:
                        rank_job(i - 1, 5, 0)
                    if more:
                        qk_proj(i + 1, 5)
                    pt_job(i, 6, 4, 1, 2)
                    o_job(i, 5, 5, 0, [(6, 2), (5, 3)])
                    if tail:
                        rank_job(i - 1, 6, 1)
                    pe.wait_ge(free[0], turn(i, PROJ_JOBS, 6))
                    pe.wait_ge(free[1], turn(i, PROJ_JOBS, 6))
                    pv_job(i, 6, 5, 1, range(4), [(6, 3), (5, 4)])
                    pv_job(i, 5, 6, 1, range(4, HC), [(6, 4)])

                pe.wait_ge(ld_small, 16 * 4)
                for c in range(HC):
                    qk_proj(0, c)
                pe.wait_ge(row1_done, 2)
                body(0, tail=False)
                with pe.Fori(1, NIT - 1) as i:
                    body(i)
                body(NIT - 1, more=False)
                last_tail = NIT - 1
                o_job(last_tail, 6, 6, 1, [(6, 5), (5, 6)])
                x2_job(last_tail, 1, 0)
                gate_job(last_tail, 2, 0)
                x2_job(last_tail, 3, 1)
                gate_job(last_tail, 4, 1)
                rank_job(last_tail, 5, 0)
                rank_job(last_tail, 6, 1, LAST)

        with ExitStack() as cc:
            def sbc(name, shape, dt=fp32):
                return cc.enter_context(nc.sbuf_tensor(name, shape, dt))

            def semc(name):
                return cc.enter_context(nc.semaphore(name))

            idx = [sbc(f"idx{u}", [P, 1], u32) for u in range(U)]
            xh0 = [sbc(f"xh0{u}", [P, P], fp32r) for u in range(2)]
            xl0 = [sbc(f"xl0{u}", [P, P], fp32r) for u in range(2)]
            xhl = [sbc(f"xhl{u}", [P, P], fp32r) for u in range(2)]
            xh1 = [sbc(f"xh1{u}", [D1 + 2, P], fp32r) for u in range(2)]
            hid = sbc("hid", [P, F])
            hidt = sbc("hidt", [P, KH, P])
            ysum = [sbc(f"ysum{u}", [P, D]) for u in range(2)]
            yout = [sbc(f"yout{u}", [P, D]) for u in range(U)]

            settled = semc("settled_c")
            link_c = semc("link_c")
            xt_full, xt_ready = semc("xt_full"), semc("xt_ready")
            h_full, gelu_done = semc("h_full"), semc("gelu_done")
            ht_full, ht_dve, ht_act = semc("ht_full"), semc("ht_dve"), semc("ht_act")
            y_full, y_added, y_scaled = semc("y_full"), semc("y_added"), semc("y_scaled")
            sent = [semc(f"sent{u}") for u in range(U)]
            added = semc("added")

            NLOOP = NTILE // U
            block = cc.enter_context(nc.Block())

            @block.sync
            def _(sp):
                def load_rows(t, u):
                    row = sp.value_load(rowtab[0:1, bass.ds(t, 1)], min_val=0, max_val=E * REGION)
                    sp.dma_start(xq[u][:, :], queue[bass.ds(row, P), :]).then_inc(xq_in[u], 16)

                for u in range(1, U):
                    load_rows(u, u)
                with sp.Fori(0, NLOOP - 1) as i:
                    for u in range(U):
                        sp.wait_ge(y_scaled, i * U + (u + 3))
                        load_rows((i + 1) * U + u, u)
                sp.wait_ge(added, NTILE + U)

            @block.gpsimd
            def _(pool):
                pool.sem_inc(added, U)
                with pool.Fori(0, NLOOP) as i:
                    for u in range(U):
                        pool.wait_ge(y_scaled, i * U + (u + 3))
                        pool.sem_inc(settled, 1)
                        nc.gpsimd.indirect_dma_start(
                            out=acc[:, :], out_offset=bass.IndirectOffsetOnAxis(idx[u][:, :], 0),
                            in_=yout[u][:, :], in_offset=None, bounds_check=NTOK + P - 1, oob_is_err=True,
                            compute_op=ALU.add).then_inc(sent[u], 16)
                        pool.wait_ge(sent[u], i * 16 + 16)
                        pool.sem_inc(added, 1)

            @block.scalar
            def _(act):
                def step(i, u):
                    t = i * U + u
                    act.wait_ge(h_full, t + 1)
                    for n in range(2):
                        last = nc.scalar.activation(hid[:, n * F // 2:(n + 1) * F // 2],
                                                    bank[1 + 2 * (u % 2) + n][:, 0:F // 2], ACT.Gelu)
                    last.then_inc(gelu_done, 1)

                def rest(i, u):
                    t = i * U + u
                    act.wait_ge(ht_full, t * 2 + 2)
                    nc.scalar.copy(hidt[:, 4:KH, :], bank[6][:, 0:(KH - 4) * P]).then_inc(ht_act, 1)

                def scale(i, u):
                    t = i * U + u
                    act.wait_ge(y_added, t + 2)
                    act.wait_ge(added, t + 1)
                    nc.scalar.activation(yout[u][:, :], ysum[u % 2][:, :], ACT.Copy,
                                         scale=xq[u][:, D:D + 1]).then_inc(y_scaled, 1)

                act.sem_inc(gelu_done, 1)
                act.sem_inc(y_scaled, 2)
                step(0, 0)

                def body(i, more=True):
                    for u in range(U):
                        rest(i, u)
                        if u < U - 1:
                            step(i, u + 1)
                        elif more:
                            step(i + 1, 0)
                        scale(i, u)

                with act.Fori(0, NLOOP - 1) as i:
                    body(i)
                body(NLOOP - 1, more=False)

            @block.vector
            def _(dve):
                LINKS = 2

                def rows_in(i, u):
                    t = i * U + u
                    v = u % 2
                    dve.wait_ge(xt_full, t + 1)
                    nc.vector.tensor_copy(xh0[v][:, :], bank[0][:, 0:P])
                    nc.vector.tensor_copy(xh1[v][0:D1, :], bank[0][0:D1, P:2 * P]).then_inc(link_c, 1)
                    nc.vector.tensor_copy(xhl[v][0:D1, :], bank[0][0:D1, P:2 * P]).then_inc(link_c, 1)
                    dve.wait_ge(link_c, t * LINKS + 2)
                    nc.vector.tensor_tensor(xl0[v][:, :], bank[0][:, 0:P], xh0[v][:, :].bitcast(fp32), ALU.subtract)
                    nc.vector.tensor_tensor(xhl[v][D1:P, :], bank[0][0:D1, P:2 * P], xh1[v][0:D1, :].bitcast(fp32),
                                            ALU.subtract).then_inc(xt_ready, 1)
                    dve.wait_ge(xq_in[u], i * 16 + 16)
                    dve.wait_ge(added, t + 1)
                    nc.vector.tensor_copy(idx[u][:, :], xq[u][:, D + 1:D + 2])

                def rest(i, u):
                    t = i * U + u
                    dve.wait_ge(ht_full, t * 2 + 1)
                    nc.vector.tensor_copy(hidt[:, 0:4, :], bank[5][:, 0:4 * P]).then_inc(ht_dve, 1)

                def add_bias(i, u):
                    t = i * U + u
                    e = dve.value_load(exptab[0:1, bass.ds(t, 1)], min_val=0, max_val=E - 1)
                    dve.wait_ge(y_full, t + 1)
                    dve.wait_ge(y_scaled, t + 1)
                    nc.vector.tensor_tensor(ysum[u % 2][:, :], bank[7][:, 0:D],
                                            b2s[:, :, :].rearrange("p e d -> p (e d)")[:, bass.ds(e * D, D)],
                                            ALU.add).then_inc(y_added, 1)

                for v in range(2):
                    nc.vector.memset(xh1[v][D1:D1 + 2, :].bitcast(fp32), 1.0)
                dve.sem_inc(y_added, 1)
                dve.sem_inc(xt_ready, 1)
                rows_in(0, 0)
                rows_in(0, 1)

                def body(i, more=True):
                    for u in range(U):
                        rest(i, u)
                        if u < U - 2:
                            rows_in(i, u + 2)
                        elif more:
                            rows_in(i + 1, u + 2 - U)
                        add_bias(i, u)

                with dve.Fori(0, NLOOP - 1) as i:
                    body(i)
                body(NLOOP - 1, more=False)

            @block.tensor
            def _(pe):
                mm = nc.tensor.matmul
                w2_f = w2s[:, :, :, :].rearrange("p e k d -> p (e k d)")

                def transpose_rows(i, u):
                    t = i * U + u
                    pe.wait_ge(xq_in[u], i * 16 + 16)
                    pe.wait_ge(xt_ready, t + 1)
                    nc.tensor.transpose(bank[0][:, 0:P], xq[u][:, 0:P], ident[:, :])
                    nc.tensor.transpose(bank[0][0:D1, P:2 * P], xq[u][:, P:D], ident[:, :]).then_inc(xt_full, 1)

                def up(i, u, e):
                    t = i * U + u
                    v = u % 2
                    pe.wait_ge(xt_ready, t + 2)
                    for n in range(2):
                        o = bank[1 + 2 * (u % 2) + n][:, 0:F // 2]
                        cols = bass.ds(e * F + n * F // 2, F // 2)
                        mm(o, xh0[v][:, :], w1ah[:, cols], start=True, stop=False)
                        mm(o, xh0[v][:, :], w1al[:, cols], start=False, stop=False)
                        mm(o, xl0[v][:, :], w1ah[:, cols], start=False, stop=False)
                        mm(o, xhl[v][:, :], w1bh[:, cols], start=False, stop=False)
                        last = mm(o, xh1[v][:, :], w1bl[:, cols], start=False, stop=True)
                    last.then_inc(h_full, 1)

                def transpose_hidden(i, u):
                    t = i * U + u
                    pe.wait_ge(gelu_done, t + 2)
                    for k in range(KH):
                        last = nc.tensor.transpose(bank[5 + k // 4][:, (k % 4) * P:(k % 4 + 1) * P],
                                                   hid[:, k * P:(k + 1) * P], ident[:, :])
                        if k in (3, KH - 1):
                            last.then_inc(ht_full, 1)

                def down(i, u, e):
                    t = i * U + u
                    pe.wait_ge(ht_dve, t + 1)
                    pe.wait_ge(ht_act, t + 1)
                    pe.wait_ge(y_added, t + 1)
                    for k in range(KH):
                        last = mm(bank[7][:, 0:D], hidt[:, k, :], w2_f[:, bass.ds(e * (KH * D) + k * D, D)],
                                  start=(k == 0), stop=(k == KH - 1))
                    last.then_inc(y_full, 1)

                def expert(t):
                    return pe.value_load(exptab[0:1, bass.ds(t, 1)], min_val=0, max_val=E - 1)

                def body(i, more=True):
                    for u in range(U):
                        transpose_hidden(i, u)
                        if u < U - 2:
                            transpose_rows(i, u + 2)
                        elif more:
                            transpose_rows(i + 1, u + 2 - U)
                        if u < U - 1:
                            up(i, u + 1, expert(i * U + u + 1))
                        elif more:
                            up(i + 1, 0, expert((i + 1) * U))
                        down(i, u, expert(i * U + u))

                transpose_rows(0, 0)
                up(0, 0, expert(0))
                transpose_rows(0, 1)
                pe.wait_ge(ld_w2, 16)
                with pe.Fori(0, NLOOP - 1) as i:
                    body(i)
                body(NLOOP - 1, more=False)


_INS = ["x", "cls_tok", "L0_tok_W", "L0_tok_b", "L0_attn_W_Q", "L0_attn_b_Q", "L0_attn_W_K", "L0_attn_b_K",
        "L0_attn_W_V", "L0_attn_b_V", "L0_attn_W_O", "L0_attn_b_O", "L0_ffn_gate_w", "L0_ffn_gate_b",
        "L0_ffn_w1", "L0_ffn_b1", "L0_ffn_w2", "L0_ffn_b2"]


def kernel(**inputs):
    import numpy as np
    import concourse.bacc as bacc
    from concourse.bass_utils import run_bass_kernel_spmd

    nc = bacc.Bacc("TRN2", target_bir_lowering=False, num_devices=1)
    arrays, args = {}, []
    for name in _INS:
        a = np.ascontiguousarray(inputs[name])
        arrays[f"in_{name}"] = a
        args.append(nc.dram_tensor(f"in_{name}", a.shape, mybir.dt.from_np(a.dtype), kind="ExternalInput").ap())
    batch, channels, side, _ = inputs["x"].shape
    tokens = (side // 16) ** 2 + 1
    out = nc.dram_tensor("out_0", [batch * tokens + 128, inputs["L0_tok_W"].shape[0]], mybir.dt.float32, kind="ExternalOutput").ap()
    vit_tower_kernel(nc, *args, out)
    r = run_bass_kernel_spmd(nc, [arrays], core_ids=[0])
    return r.results[0]["out_0"][:batch * tokens].reshape(batch, tokens, -1)
```
